# Optimizing a Trainium2 kernel written in Bass

```python
import numpy as np
import jax
import jax.numpy as jnp

def _softmax(x, axis=-1):
    return jax.nn.softmax(x, axis=axis)

def _gelu(x):
    return jax.nn.gelu(x, approximate=True)

def _silu(x):
    return jax.nn.silu(x)

def _sigmoid(x):
    return jax.nn.sigmoid(x)

def _layernorm(x, axis=-1, eps=1e-05):
    m = jnp.mean(x, axis=axis, keepdims=True)
    v = jnp.var(x, axis=axis, keepdims=True)
    return (x - m) / jnp.sqrt(v + eps)

def _scatter_add(tgt, idx, src, axis=0):
    return tgt.at[idx].add(src)

def _segment_sum(src, seg, n):
    return jax.ops.segment_sum(src, seg, n)
kernel_name = 'mk_lm_tower_d2_tok_ids512_r4_94ba74'

def setup_inputs(seed: int=0):
    np.random.seed(seed)
    _w = jnp.asarray

    def _rec_inputs():
        import jax
        import jax.numpy as jnp
        _rk = jax.random.key(seed)
        x = jax.random.randint(jax.random.fold_in(_rk, 1), (2, 2048), 0, 125, jnp.int32)
        return x
    x = _rec_inputs()

    def _L0_tok_setup():
        import jax, jax.numpy as jnp
        import numpy as np
        QMAX = 127.0
        CTX = 2

        def fake_quant(w):
            scale = jnp.max(jnp.abs(w)) / QMAX
            wq = jnp.round(w / scale) * scale
            return w + jax.lax.stop_gradient(wq - w)
        key = jax.random.key(seed)
        k1, k2, k3 = jax.random.split(key, 3)
        y = jax.random.randint(k1, (64, 512), 0, 125, dtype=jnp.int64)
        emb_weight = jax.random.normal(k2, (125, 128), dtype=jnp.float32)
        conv_weight = jax.random.normal(k3, (128, 1, 2), dtype=jnp.float32)
        return {'y': y, 'emb_weight': emb_weight, 'conv_weight': conv_weight}
    _L0_tok_all = _L0_tok_setup()
    _L0_tok_in = {k: v for k, v in _L0_tok_all.items() if k in ('emb_weight', 'conv_weight')}
    del _L0_tok_all

    def _L0_attn_setup():
        import jax, jax.numpy as jnp
        import numpy as np
        B, N, D = (4, 1024, 128)
        H, DH = (8, 64)
        M = 64
        ITERS = 6
        K = 33

        def _pinv(x, iters=ITERS):
            ax = jnp.abs(x)
            norm = jnp.max(ax.sum(-1)) * jnp.max(ax.sum(-2))
            z = jnp.swapaxes(x, -1, -2) / norm
            I = jnp.eye(x.shape[-1], dtype=x.dtype)
            for _ in range(iters):
                xz = x @ z
                z = 0.25 * z @ (13 * I - xz @ (15 * I - xz @ (7 * I - xz)))
            return z
        key = jax.random.key(seed)
        k0, k1, k2, k3 = jax.random.split(key, 4)
        inner = H * DH
        return {'x': jax.random.normal(k0, (B, N, D), jnp.float32), 'W_qkv': jax.random.normal(k1, (D, 3 * inner), jnp.float32) * 0.02, 'W_out': jax.random.normal(k2, (inner, D), jnp.float32) * 0.02, 'b_out': jnp.zeros((D,), jnp.float32), 'conv_w': jax.random.normal(k3, (H, 1, K, 1), jnp.float32) * 0.05}
    _L0_attn_all = _L0_attn_setup()
    _L0_attn_in = {k: v for k, v in _L0_attn_all.items() if k in ('W_qkv', 'W_out', 'b_out', 'conv_w')}
    del _L0_attn_all

    def _L0_ffn_setup():
        import math
        import jax, jax.numpy as jnp
        import numpy as np
        B, T, D, FF, E = (32, 256, 128, 512, 8)
        CAPACITY_FACTOR = 1.25
        CAP = int(math.ceil(CAPACITY_FACTOR * B * T / E))

        def _bank_residual(x2, Wr, br, W1, b1, W2, b2):
            N, d = x2.shape
            e = Wr.shape[1]
            logits = x2 @ Wr + br
            probs = jax.nn.softmax(logits, axis=-1)
            expert = jnp.argmax(probs, axis=-1)
            gate = jnp.take_along_axis(probs, expert[:, None], axis=-1)[:, 0]
            oneh = jax.nn.one_hot(expert, e, dtype=x2.dtype)
            pos = (jnp.cumsum(oneh, axis=0) * oneh).sum(-1).astype(jnp.int32) - 1
            keep = pos < CAP
            slot = expert.astype(jnp.int32) * CAP + jnp.minimum(pos, CAP - 1)
            xd = jnp.where(keep[:, None], x2, 0.0)
            buf = jnp.zeros((e * CAP, d), x2.dtype).at[slot].add(xd)
            buf = buf.reshape(e, CAP, d)
            h = jax.nn.gelu(jnp.einsum('ecd,edf->ecf', buf, W1) + b1[:, None, :], approximate=False)
            out = jnp.einsum('ecf,efd->ecd', h, W2) + b2[:, None, :]
            y = out.reshape(e * CAP, d)[slot]
            return y * (gate * keep.astype(x2.dtype))[:, None]
        key = jax.random.key(seed)
        ks = jax.random.split(key, 18)
        s = 0.02
        inp = {'x': jax.random.normal(ks[0], (B, T, D), dtype=jnp.float32), 'Wr_sp': jax.random.normal(ks[1], (D, E)) * s, 'br_sp': jnp.zeros((E,), jnp.float32), 'Wr_fq': jax.random.normal(ks[2], (D, E)) * s, 'br_fq': jnp.zeros((E,), jnp.float32), 'Ws1': jax.random.normal(ks[3], (D, FF)) * s, 'bs1': jnp.zeros((FF,), jnp.float32), 'Ws2': jax.random.normal(ks[4], (FF, D)) * s, 'bs2': jnp.zeros((D,), jnp.float32), 'W1_sp': jax.random.normal(ks[5], (E, D, FF)) * s, 'b1_sp': jnp.zeros((E, FF), jnp.float32), 'W2_sp': jax.random.normal(ks[6], (E, FF, D)) * s, 'b2_sp': jnp.zeros((E, D), jnp.float32), 'W1_fq': jax.random.normal(ks[7], (E, D, FF)) * s, 'b1_fq': jnp.zeros((E, FF), jnp.float32), 'W2_fq': jax.random.normal(ks[8], (E, FF, D)) * s, 'b2_fq': jnp.zeros((E, D), jnp.float32)}
        return inp
    _L0_ffn_all = _L0_ffn_setup()
    _L0_ffn_in = {k: v for k, v in _L0_ffn_all.items() if k in ('Wr_sp', 'br_sp', 'Wr_fq', 'br_fq', 'Ws1', 'bs1', 'Ws2', 'bs2', 'W1_sp', 'b1_sp', 'W2_sp', 'b2_sp', 'W1_fq', 'b1_fq', 'W2_fq', 'b2_fq')}
    del _L0_ffn_all

    def _L1_attn_setup():
        import jax, jax.numpy as jnp
        import numpy as np
        B, T, C, H = (2, 1024, 128, 8)
        D = C // H
        key = jax.random.key(seed)
        ks = jax.random.split(key, 4)
        s = 0.02
        return {'x': jax.random.normal(ks[0], (B, T, C), dtype=jnp.float32), 'Wq': jax.random.normal(ks[1], (C, C), dtype=jnp.float32) * s, 'bq': jnp.zeros((C,), dtype=jnp.float32), 'Wk': jax.random.normal(ks[2], (C, C), dtype=jnp.float32) * s, 'bk': jnp.zeros((C,), dtype=jnp.float32), 'Wv': jax.random.normal(ks[3], (C, C), dtype=jnp.float32) * s, 'bv': jnp.zeros((C,), dtype=jnp.float32)}
    _L1_attn_all = _L1_attn_setup()
    _L1_attn_in = {k: v for k, v in _L1_attn_all.items() if k in ('Wq', 'bq', 'Wk', 'bk', 'Wv', 'bv')}
    del _L1_attn_all

    def _L1_ffn_setup():
        import jax, jax.numpy as jnp
        import numpy as np
        DIM, DEPTH, MULT = (128, 3, 4)
        E = 2 ** DEPTH
        HID = MULT * DIM
        B, S = (4, 256)

        def _leaf_probs(flat_x, rw, rb):
            n_tok = flat_x.shape[0]
            leaf = jnp.ones((n_tok, 1), dtype=flat_x.dtype)
            for d in range(DEPTH):
                off, n = (2 ** d - 1, 2 ** d)
                logits = flat_x @ rw[off:off + n].T + rb[off:off + n]
                p = jax.nn.sigmoid(logits)
                leaf = (leaf[:, :, None] * jnp.stack([1.0 - p, p], axis=2)).reshape(n_tok, 2 * n)
            return leaf
        key = jax.random.key(seed)
        ks = jax.random.split(key, 7)
        sd = 1.0 / np.sqrt(DIM)
        sh = 1.0 / np.sqrt(HID)
        return {'x': jax.random.normal(ks[0], (B, S, DIM), dtype=jnp.float32), 'rw': jax.random.normal(ks[1], (E - 1, DIM), dtype=jnp.float32) * sd, 'rb': jax.random.normal(ks[2], (E - 1,), dtype=jnp.float32) * sd, 'w1': jax.random.normal(ks[3], (E, DIM, HID), dtype=jnp.float32) * sd, 'b1': jax.random.normal(ks[4], (E, HID), dtype=jnp.float32) * sd, 'w2': jax.random.normal(ks[5], (E, HID, DIM), dtype=jnp.float32) * sh, 'b2': jax.random.normal(ks[6], (E, DIM), dtype=jnp.float32) * sh}
    _L1_ffn_all = _L1_ffn_setup()
    _L1_ffn_in = {k: v for k, v in _L1_ffn_all.items() if k in ('rw', 'rb', 'w1', 'b1', 'w2', 'b2')}
    del _L1_ffn_all
    return {'x': x, 'L0_tok_emb_weight': _L0_tok_in['emb_weight'], 'L0_tok_conv_weight': _L0_tok_in['conv_weight'], 'L0_attn_W_qkv': _L0_attn_in['W_qkv'], 'L0_attn_W_out': _L0_attn_in['W_out'], 'L0_attn_b_out': _L0_attn_in['b_out'], 'L0_attn_conv_w': _L0_attn_in['conv_w'], 'L0_ffn_Wr_sp': _L0_ffn_in['Wr_sp'], 'L0_ffn_br_sp': _L0_ffn_in['br_sp'], 'L0_ffn_Wr_fq': _L0_ffn_in['Wr_fq'], 'L0_ffn_br_fq': _L0_ffn_in['br_fq'], 'L0_ffn_Ws1': _L0_ffn_in['Ws1'], 'L0_ffn_bs1': _L0_ffn_in['bs1'], 'L0_ffn_Ws2': _L0_ffn_in['Ws2'], 'L0_ffn_bs2': _L0_ffn_in['bs2'], 'L0_ffn_W1_sp': _L0_ffn_in['W1_sp'], 'L0_ffn_b1_sp': _L0_ffn_in['b1_sp'], 'L0_ffn_W2_sp': _L0_ffn_in['W2_sp'], 'L0_ffn_b2_sp': _L0_ffn_in['b2_sp'], 'L0_ffn_W1_fq': _L0_ffn_in['W1_fq'], 'L0_ffn_b1_fq': _L0_ffn_in['b1_fq'], 'L0_ffn_W2_fq': _L0_ffn_in['W2_fq'], 'L0_ffn_b2_fq': _L0_ffn_in['b2_fq'], 'L1_attn_Wq': _L1_attn_in['Wq'], 'L1_attn_bq': _L1_attn_in['bq'], 'L1_attn_Wk': _L1_attn_in['Wk'], 'L1_attn_bk': _L1_attn_in['bk'], 'L1_attn_Wv': _L1_attn_in['Wv'], 'L1_attn_bv': _L1_attn_in['bv'], 'L1_ffn_rw': _L1_ffn_in['rw'], 'L1_ffn_rb': _L1_ffn_in['rb'], 'L1_ffn_w1': _L1_ffn_in['w1'], 'L1_ffn_b1': _L1_ffn_in['b1'], 'L1_ffn_w2': _L1_ffn_in['w2'], 'L1_ffn_b2': _L1_ffn_in['b2']}

def reference(x, L0_tok_emb_weight, L0_tok_conv_weight, L0_attn_W_qkv, L0_attn_W_out, L0_attn_b_out, L0_attn_conv_w, L0_ffn_Wr_sp, L0_ffn_br_sp, L0_ffn_Wr_fq, L0_ffn_br_fq, L0_ffn_Ws1, L0_ffn_bs1, L0_ffn_Ws2, L0_ffn_bs2, L0_ffn_W1_sp, L0_ffn_b1_sp, L0_ffn_W2_sp, L0_ffn_b2_sp, L0_ffn_W1_fq, L0_ffn_b1_fq, L0_ffn_W2_fq, L0_ffn_b2_fq, L1_attn_Wq, L1_attn_bq, L1_attn_Wk, L1_attn_bk, L1_attn_Wv, L1_attn_bv, L1_ffn_rw, L1_ffn_rb, L1_ffn_w1, L1_ffn_b1, L1_ffn_w2, L1_ffn_b2):
    import jax
    import jax.numpy as jnp

    def _L0_tok_ref(y, emb_weight, conv_weight):
        import jax, jax.numpy as jnp
        import numpy as np
        QMAX = 127.0
        CTX = 2

        def fake_quant(w):
            scale = jnp.max(jnp.abs(w)) / QMAX
            wq = jnp.round(w / scale) * scale
            return w + jax.lax.stop_gradient(wq - w)
        w_emb = fake_quant(emb_weight)
        e = w_emb[jnp.clip(y, 0)]
        e = e * (y >= 0)[..., None].astype(e.dtype)
        x = jnp.pad(e, ((0, 0), (CTX - 1, 0), (0, 0)))
        D = conv_weight.shape[0]
        w = fake_quant(conv_weight).transpose(2, 1, 0)
        out = jax.lax.conv_general_dilated(x, w, window_strides=(1,), padding='VALID', feature_group_count=D, dimension_numbers=('NWC', 'WIO', 'NWC'))
        return jax.nn.relu(out)

    def _L0_attn_ref(x, W_qkv, W_out, b_out, conv_w):
        import jax, jax.numpy as jnp
        import numpy as np
        B, N, D = (4, 1024, 128)
        H, DH = (8, 64)
        M = 64
        ITERS = 6
        K = 33

        def _pinv(x, iters=ITERS):
            ax = jnp.abs(x)
            norm = jnp.max(ax.sum(-1)) * jnp.max(ax.sum(-2))
            z = jnp.swapaxes(x, -1, -2) / norm
            I = jnp.eye(x.shape[-1], dtype=x.dtype)
            for _ in range(iters):
                xz = x @ z
                z = 0.25 * z @ (13 * I - xz @ (15 * I - xz @ (7 * I - xz)))
            return z
        b, n, _ = x.shape
        qkv = x @ W_qkv
        q, k, v = jnp.split(qkv, 3, axis=-1)
        to_bhnd = lambda t: t.reshape(b, n, H, DH).transpose(0, 2, 1, 3)
        q, k, v = (to_bhnd(q), to_bhnd(k), to_bhnd(v))
        q = q * DH ** (-0.5)
        l = n // M
        q_l = q.reshape(b, H, M, l, DH).mean(3)
        k_l = k.reshape(b, H, M, l, DH).mean(3)
        sim1 = jnp.einsum('bhid,bhjd->bhij', q, k_l)
        sim2 = jnp.einsum('bhid,bhjd->bhij', q_l, k_l)
        sim3 = jnp.einsum('bhid,bhjd->bhij', q_l, k)
        attn1 = jax.nn.softmax(sim1, axis=-1)
        attn2 = jax.nn.softmax(sim2, axis=-1)
        attn3 = jax.nn.softmax(sim3, axis=-1)
        attn2_inv = _pinv(attn2)
        out = attn1 @ attn2_inv @ (attn3 @ v)
        res = jax.lax.conv_general_dilated(v, conv_w, window_strides=(1, 1), padding=[(K // 2, K // 2), (0, 0)], dimension_numbers=('NCHW', 'OIHW', 'NCHW'), feature_group_count=H)
        out = out + res
        out = out.transpose(0, 2, 1, 3).reshape(b, n, H * DH)
        return out @ W_out + b_out

    def _L0_ffn_ref(x, Wr_sp, br_sp, Wr_fq, br_fq, Ws1, bs1, Ws2, bs2, W1_sp, b1_sp, W2_sp, b2_sp, W1_fq, b1_fq, W2_fq, b2_fq):
        import math
        import jax, jax.numpy as jnp
        import numpy as np
        B, T, D, FF, E = (32, 256, 128, 512, 8)
        CAPACITY_FACTOR = 1.25
        CAP = int(math.ceil(CAPACITY_FACTOR * B * T / E))

        def _bank_residual(x2, Wr, br, W1, b1, W2, b2):
            N, d = x2.shape
            e = Wr.shape[1]
            logits = x2 @ Wr + br
            probs = jax.nn.softmax(logits, axis=-1)
            expert = jnp.argmax(probs, axis=-1)
            gate = jnp.take_along_axis(probs, expert[:, None], axis=-1)[:, 0]
            oneh = jax.nn.one_hot(expert, e, dtype=x2.dtype)
            pos = (jnp.cumsum(oneh, axis=0) * oneh).sum(-1).astype(jnp.int32) - 1
            keep = pos < CAP
            slot = expert.astype(jnp.int32) * CAP + jnp.minimum(pos, CAP - 1)
            xd = jnp.where(keep[:, None], x2, 0.0)
            buf = jnp.zeros((e * CAP, d), x2.dtype).at[slot].add(xd)
            buf = buf.reshape(e, CAP, d)
            h = jax.nn.gelu(jnp.einsum('ecd,edf->ecf', buf, W1) + b1[:, None, :], approximate=False)
            out = jnp.einsum('ecf,efd->ecd', h, W2) + b2[:, None, :]
            y = out.reshape(e * CAP, d)[slot]
            return y * (gate * keep.astype(x2.dtype))[:, None]
        b, t, d = x.shape
        x2 = x.reshape(b * t, d)
        shared = jax.nn.gelu(x2 @ Ws1 + bs1, approximate=False) @ Ws2 + bs2
        y = shared
        y = y + _bank_residual(x2, Wr_sp, br_sp, W1_sp, b1_sp, W2_sp, b2_sp)
        y = y + _bank_residual(x2, Wr_fq, br_fq, W1_fq, b1_fq, W2_fq, b2_fq)
        return y.reshape(b, t, d)

    def _L1_attn_ref(x, Wq, bq, Wk, bk, Wv, bv):
        import jax, jax.numpy as jnp
        import numpy as np
        B, T, C, H = (2, 1024, 128, 8)
        D = C // H
        b, t, c = x.shape
        q = (x @ Wq.T + bq).reshape(b, t, H, D).transpose(0, 2, 1, 3)
        k = (x @ Wk.T + bk).reshape(b, t, H, D).transpose(0, 2, 1, 3)
        v = (x @ Wv.T + bv).reshape(b, t, H, D).transpose(0, 2, 1, 3)
        scale = 1.0 / jnp.sqrt(jnp.asarray(D, dtype=x.dtype))
        logits = jnp.einsum('bhqd,bhkd->bhqk', q, k) * scale
        causal = jnp.triu(jnp.ones((t, t), dtype=bool), 1)
        logits = jnp.where(causal, jnp.asarray(-jnp.inf, dtype=x.dtype), logits)
        attn = jax.nn.softmax(logits, axis=-1)
        out = jnp.einsum('bhqk,bhkd->bhqd', attn, v)
        return out.transpose(0, 2, 1, 3).reshape(b, t, c)

    def _L1_ffn_ref(x, rw, rb, w1, b1, w2, b2):
        import jax, jax.numpy as jnp
        import numpy as np
        DIM, DEPTH, MULT = (128, 3, 4)
        E = 2 ** DEPTH
        HID = MULT * DIM
        B, S = (4, 256)

        def _leaf_probs(flat_x, rw, rb):
            n_tok = flat_x.shape[0]
            leaf = jnp.ones((n_tok, 1), dtype=flat_x.dtype)
            for d in range(DEPTH):
                off, n = (2 ** d - 1, 2 ** d)
                logits = flat_x @ rw[off:off + n].T + rb[off:off + n]
                p = jax.nn.sigmoid(logits)
                leaf = (leaf[:, :, None] * jnp.stack([1.0 - p, p], axis=2)).reshape(n_tok, 2 * n)
            return leaf
        b, s, dim = x.shape
        flat_x = x.reshape(b * s, dim)
        leaf_probs = _leaf_probs(flat_x, rw, rb)
        h = jnp.einsum('nd,edh->neh', flat_x, w1) + b1[None]
        h = jax.nn.gelu(h, approximate=False)
        y = jnp.einsum('neh,ehd->ned', h, w2) + b2[None]
        out = jnp.einsum('ned,ne->nd', y, leaf_probs)
        return out.reshape(b, s, dim)
    h = _L0_tok_ref(x, L0_tok_emb_weight, L0_tok_conv_weight)
    h = h + _L0_attn_ref(_layernorm(h, axis=-1), L0_attn_W_qkv, L0_attn_W_out, L0_attn_b_out, L0_attn_conv_w)
    h = h + _L0_ffn_ref(_layernorm(h, axis=-1), L0_ffn_Wr_sp, L0_ffn_br_sp, L0_ffn_Wr_fq, L0_ffn_br_fq, L0_ffn_Ws1, L0_ffn_bs1, L0_ffn_Ws2, L0_ffn_bs2, L0_ffn_W1_sp, L0_ffn_b1_sp, L0_ffn_W2_sp, L0_ffn_b2_sp, L0_ffn_W1_fq, L0_ffn_b1_fq, L0_ffn_W2_fq, L0_ffn_b2_fq)
    h = h + _L1_attn_ref(_layernorm(h, axis=-1), L1_attn_Wq, L1_attn_bq, L1_attn_Wk, L1_attn_bk, L1_attn_Wv, L1_attn_bv)
    h = h + _L1_ffn_ref(_layernorm(h, axis=-1), L1_ffn_rw, L1_ffn_rb, L1_ffn_w1, L1_ffn_b1, L1_ffn_w2, L1_ffn_b2)
    return h

_drawn_inputs = setup_inputs


def setup_inputs(seed=0):
    import zlib

    import numpy as np

    out = dict(_drawn_inputs(seed))
    spreads = {'L0_attn_b_out': (0.0, 0.1),
     'L0_ffn_br_sp': (0.0, 0.512),
     'L0_ffn_br_fq': (0.0, 0.576),
     'L0_ffn_bs1': (0.0, 0.315),
     'L0_ffn_bs2': (0.0, 0.1),
     'L0_ffn_b1_sp': (0.0, 0.8),
     'L0_ffn_b2_sp': (0.0, 0.444),
     'L0_ffn_b1_fq': (0.0, 0.8),
     'L0_ffn_b2_fq': (0.0, 0.434),
     'L1_attn_bq': (0.0, 0.8),
     'L1_attn_bk': (0.0, 2.0),
     'L1_attn_bv': (0.0, 0.1)}
    factors = {'L0_ffn_Wr_sp': 2.922,
     'L0_ffn_Wr_fq': 2.853,
     'L0_ffn_W1_sp': 5.924,
     'L0_ffn_W2_sp': 5.429,
     'L0_ffn_W1_fq': 5.956,
     'L0_ffn_W2_fq': 5.409,
     'L1_attn_Wq': 8.0,
     'L1_attn_Wk': 8.0,
     'L1_ffn_rb': 4.525,
     'L1_ffn_b2': 2.945,
     'L1_ffn_b1': 2.985}
    for name, (base, spread) in spreads.items():
        noise = np.random.default_rng([zlib.crc32(name.encode()), seed]).standard_normal(out[name].shape)
        drawn = base * np.exp(spread * noise) if base else spread * noise
        out[name] = jnp.asarray(drawn.astype(out[name].dtype))
    for name, factor in factors.items():
        out[name] = (out[name] * factor).astype(out[name].dtype)
    return out
```

```python
from contextlib import ExitStack

import concourse.bass as bass
from concourse import mybir

F32 = mybir.dt.float32
BF16 = mybir.dt.bfloat16
I32 = mybir.dt.int32
ALU = mybir.AluOpType
ACT = mybir.ActivationFunctionType
X = mybir.AxisListType.X
RMAX = bass.bass_isa.ReduceOp.max

P = 128
B = 2
T = 2048
N = B * T
CH = 512
NC = N // CH
NT = N // P
TB = T // P
CB = T // CH
TC = CH // P
VOC = 125
EPS = 1e-5
MAGIC = 1.5 * 2.0 ** 23

H0, M, K = 8, 64, 33
PR = H0 // 2
LM = T // M
ITERS = 6
HALF = K // 2
CW = P + K - 1
BP = B * PR

E, KF = 8, 4
CAP = 1280
NBLK = N // P + E
SLOTS = NBLK * P
BK = 2
TG = NT * BK
C_IOTA8, C_J128, C_LT, C_TRASH, C_IOTAB = 0, 8, 18, 82, 82 + NT
C_ROUTE = C_IOTAB + NBLK


H1, D1 = 8, 16
UN = B * H1
TERMS = 6
KS_ROWS = TERMS * D1
KROWS = KS_ROWS + 3
RING = 8
LEAD = 2
NEG = -1e30


def max_pieces(i):
    return [(qt, s, min(1024, (qt + 1) * P - 1024 * s)) for qt in range(TC * i, TC * i + TC) for s in range(1 + (qt >= 8))]


def exp_tiles(i):
    return [(j, max(0, (j - TC * i) * P)) for j in range(TC * (i + 1))]


def step_items(u, i):
    pieces = [("max", x) for x in max_pieces(i)] if u + LEAD < UN else []
    tiles = [("exp", x) for x in exp_tiles(i)] if u >= 0 else []
    out, n = [], max(len(pieces), len(tiles))
    for k in range(n):
        out += pieces[len(pieces) * k // n:len(pieces) * (k + 1) // n] + tiles[len(tiles) * k // n:len(tiles) * (k + 1) // n]
    return out


def pause(items):
    seen = 0
    for n, (kind, _) in enumerate(items):
        seen += kind == "exp"
        if seen == 4:
            return n + 1
    return len(items)


def maxima_before(items):
    return sum(kind == "max" for kind, _ in items[:pause(items)])


LAG1 = 3
HB = 4
HK = E * KF

STEPS = [(u, i) for u in range(-LEAD, UN) for i in range(CB)]


def conv_pieces(c):
    lo, out = (c % CB) * CH, []
    for t in range(TB):
        a, b = max(t * P - HALF, lo), min(t * P - HALF + CW, lo + CH)
        if a < b:
            out.append((t, a - lo, b - a, a - (t * P - HALF)))
    return out


def tower(nc, a):
    with ExitStack() as ctx:
        def sb(name, shape, dt=F32):
            return ctx.enter_context(nc.sbuf_tensor(name, shape, dt))

        def sem(name):
            return ctx.enter_context(nc.semaphore(name))

        low = ctx.enter_context(nc.psum_tensor("low", [P, 4 * CH], F32))
        high = ctx.enter_context(nc.psum_tensor("high", [P, 4 * CH], F32))
        bank = [(low if i < 4 else high)[:, (i % 4) * CH:(i % 4 + 1) * CH] for i in range(8)]

        def wide_bank(k):
            return low[:, k * 2 * CH:(k + 1) * 2 * CH]

        hT = sb("hT", [P, N])
        xnT = sb("xnT", [P, N])
        arena_a = sb("arena_a", [P, 16384])
        arena_b = sb("arena_b", [P, 16384])
        arena_c = sb("arena_c", [P, 8192])
        ident = sb("ident", [P, P])
        idk = sb("idk", [P, 3, P])
        mean_w = sb("mean_w", [P, P])
        iota = sb("iota", [P, 1])
        eps = sb("eps", [P, 1])
        conv2 = sb("conv2", [P, 2])
        qcol = sb("qcol", [P, 8])
        b_out = sb("b_out", [P, 1])

        tok = arena_c[:, 0:N].bitcast(I32)
        emb = arena_c[:, N:N + P]
        emb_q = arena_c[:, N + P:N + 2 * P]
        emb_e = arena_c[:, N + 2 * P:N + 3 * P]
        onehot = arena_b[:, 0:2 * CH].rearrange("p (s c) -> p s c", s=2)
        eT = arena_a[:, 0:B * (T + 1)].rearrange("p (b t) -> p b t", b=B)
        tmp = arena_b[:, 2 * CH:4 * CH].rearrange("p (s c) -> p s c", s=2)

        ln_xc = sb("ln_xc", [P, 2, CH])
        ln_sq = sb("ln_sq", [P, 2, CH])
        ln_sd = sb("ln_sd", [P, 2, CH])

        V = arena_a[:, :].rearrange("p (t f) -> p t f", t=NT)

        def block(i):
            return arena_b[:, i * BP * P:(i + 1) * BP * P].rearrange("p (g c) -> p g c", g=BP)
        QL, KL, M3, M1, A, AT, Z0, Z1, ZT0, ZT1, XZT, U = (block(i) for i in range(12))
        Z, ZT = [Z0, Z1], [ZT0, ZT1]
        W, G = QL, KL
        P3 = arena_c[:, 0:2 * T].rearrange("p (s n) -> p s n", s=2)
        P3T = arena_c[:, 2 * T:4 * T].rearrange("p (s t c) -> p s t c", s=2, t=TB)
        P1 = arena_c[:, 0:2 * CH].rearrange("p (s h m) -> p s h m", s=2, h=H0)
        P1T = arena_c[:, 2 * CH:10 * CH].rearrange("p (s g c) -> p s g c", s=2, g=PR)
        OT = arena_c[:, 10 * CH:14 * CH].rearrange("p (g c) -> p g c", g=PR)
        wqkv = arena_b[:, 12 * BP * P:12 * BP * P + 1536]
        wqT, wkT = Z1[:, 0:PR, :], ZT1[:, 0:PR, :]
        wout = arena_b[:, 13824:13824 + 512].rearrange("p (g d) -> p g d", g=PR)
        band = arena_b[:, 14336:14336 + H0 * CW].rearrange("p (h c) -> p h c", h=H0)
        xl = arena_b[:, 15616:15616 + P]
        T2 = U.rearrange("p g c -> p (g c)")[:, 0:512].rearrange("p (g m) -> p g m", g=BP)
        mx2 = sb("mx2", [P, BP])
        s2 = sb("s2", [P, BP])
        r2 = sb("r2", [P, BP])
        nsum = sb("nsum", [P, 2 * BP])
        nmax = sb("nmax", [P, 2])
        nall = sb("nall", [P, 2])
        nrm = sb("nrm", [P, 2])
        m3 = sb("m3", [P, BP])
        s3 = sb("s3", [P, BP])
        r3 = sb("r3", [P, BP])
        s3p = sb("s3p", [P, BP * CB])
        m1 = sb("m1", [P, 2, H0])
        s1 = sb("s1", [P, 2, H0])
        r1 = sb("r1", [P, 2, H0])

        w1 = arena_a[:, 0:BK * E * CH].rearrange("p (e f) -> p e f", e=BK * E)
        w2 = arena_a[:, BK * E * CH:2 * BK * E * CH].rearrange("p (e k d) -> p e k d", e=BK * E, k=KF)
        ws1 = arena_b[:, 0:512]
        ws2 = arena_b[:, 512:1024].rearrange("p (k d) -> p k d", k=KF)
        b1 = arena_b[:, 1024:1024 + BK * E * KF].rearrange("p (e k) -> p e k", k=KF)
        bs1 = arena_b[:, 1088:1092]
        bs2 = arena_b[:, 1092:1093]
        brt = arena_b[:, 1104:1120]
        wr = arena_b[:, 1120:1136]
        ones = arena_b[:, 1152:1280]
        tri = arena_b[:, 1280:1408]
        cr = arena_b[:, 1408:1408 + C_ROUTE]
        b2 = arena_b[:, 2048:4096].rearrange("p (e d) -> p e d", e=BK * E)
        xtm = arena_b[:, 4096:8192].rearrange("p (t d) -> p t d", t=NT)
        hs = arena_b[:, 8192:12288].rearrange("p (s k c) -> p s k c", s=2, k=KF)

        def route(i):
            return arena_b[:, 12288 + i * 512:12800 + i * 512]
        lg, ex, oneh, sc_a, sc_b, tot = (route(i) for i in range(6))
        rs = arena_b[:, 15360:16384].rearrange("p (i c) -> p i c", c=TG)
        w1s = arena_b[:, 8192:9216].rearrange("p (s f) -> p s f", s=2)
        hb = arena_b[:, 9216:10240].rearrange("p (s k c) -> p s k c", s=2, k=KF)
        xb = arena_b[:, 10240:10496].rearrange("p (s d) -> p s d", s=2)
        xbT = arena_b[:, 10496:10752].rearrange("p (s d) -> p s d", s=2)
        yb = arena_b[:, 10752:11008].rearrange("p (s d) -> p s d", s=2)
        b1s = arena_b[:, 11008:11016].rearrange("p (s k) -> p s k", s=2)
        ygt = arena_c[:, :].rearrange("p (t k d) -> p t k d", t=NT, k=BK)
        comb = arena_b[:, 4096:8192].rearrange("p (t d) -> p t d", t=NT)
        expert_of = arena_b[:, 1600:1680].bitcast(I32).rearrange("p (k n) -> p k n", k=BK)
        put_at = arena_b[:, 1696:1760].bitcast(I32).rearrange("p (k n) -> p k n", k=BK)
        get_at = arena_b[:, 1760:1824].bitcast(I32).rearrange("p (k n) -> p k n", k=BK)
        gate = arena_b[:, 1824:1888].rearrange("p (t k) -> p t k", k=BK)
        xbuf = [nc.dram_tensor(f"xbuf{k}", [SLOTS + N, P], F32, kind="Internal") for k in range(BK)]
        ybuf = [nc.dram_tensor(f"ybuf{k}", [SLOTS, P], F32, kind="Internal") for k in range(BK)]
        zero = arena_b[:, 16000:16128]

        ab = arena_a[:, :].bitcast(BF16).rearrange("p (k u t) -> p k u t", k=2, u=RING)
        QS, KS = ab[:, 0], ab[:, 1]
        parts = arena_b[:, 0:3072].bitcast(BF16).rearrange("p (k s r c) -> p k s r c", k=2, s=2, r=3)
        wqkvT = arena_b[:, 3072:3456].rearrange("p (k c) -> p k c", k=3)
        bvt = arena_b[:, 3456:3584]
        mask_qk = arena_b[:, 3584:3648].bitcast(BF16)
        mask_kq = arena_b[:, 3648:3712].bitcast(BF16)
        masks = arena_c[:, 4096:4352].rearrange("p (k c) -> p k c", k=2)
        identb = arena_b[:, 3712:3776].bitcast(BF16)
        bqk = arena_b[:, 3776:3778]
        V1 = arena_b[:, 4096:4096 + NT * H1 * 32].rearrange("p (t h c) -> p t h c", t=NT, h=H1)
        O = arena_b[:, 12288:16384].rearrange("p (t h c) -> p t h c", t=NT, h=H1)
        PT = arena_c[:, 0:4 * CH].rearrange("p (s c) -> p s c", s=4)
        OTp = arena_c[:, 4 * CH:6 * CH].rearrange("p (s c) -> p s c", s=2)
        OS = arena_c[:, 6 * CH:6 * CH + TB * 17].rearrange("p (t c) -> p t c", c=17)
        pm = arena_c[:, 3584:3584 + 64].rearrange("p (s t k) -> p s t k", s=2, k=2)
        negm = arena_c[:, 3648:3680].rearrange("p (s t) -> p s t", s=2)
        osum = arena_c[:, 3680:3696]
        mres = arena_c[:, 3712:3840]
        mparts = arena_c[:, 3840:3840 + 384].bitcast(BF16).rearrange("p (s r c) -> p s r c", s=2, r=3)
        qk_parts = [nc.dram_tensor(f"qk_parts{k}", [3 * P, N], BF16, kind="Internal") for k in range(2)]

        f1 = arena_a[:, 0:E * CH].rearrange("p (e f) -> p e f", e=E)
        f2 = arena_a[:, E * CH:2 * E * CH].rearrange("p (e k d) -> p e k d", e=E, k=KF)
        pbc = arena_a[:, 2 * E * CH:4 * E * CH].rearrange("p (s e c) -> p s e c", s=2, e=E)
        leafT = arena_c[0:E, 0:N]
        hid = arena_b[:, 0:HB * CH].rearrange("p (s c) -> p s c", s=HB)
        yT = arena_b[:, 3072:3072 + CH]
        yout = arena_b[:, 3584:3584 + 2 * CH].rearrange("p (s t d) -> p s t d", s=2, t=TC)
        fb1 = arena_b[:, 4608:4640].rearrange("p (e k) -> p e k", e=E)
        rwT = arena_b[:, 4640:4647]
        rbt = arena_b[:, 4648:4655]
        fb2 = arena_b[0:E, 4736:4864]
        node = arena_b[:, 4864:4864 + NT * 7].rearrange("p (t n) -> p t n", n=7)
        nodn = arena_b[:, 5120:5120 + NT * 7].rearrange("p (t n) -> p t n", n=7)
        leaf1 = arena_b[:, 5376:5376 + NT * 2].rearrange("p (t i) -> p t i", i=2)
        leaf2 = arena_b[:, 5440:5440 + NT * 4].rearrange("p (t i) -> p t i", i=4)
        leaf3 = arena_b[:, 5632:5632 + NT * 8].rearrange("p (t i) -> p t i", i=8)
        leaf_rows = nc.dram_tensor("leaf_rows", [E, N + 2 * CH], F32, kind="Internal")

        loaded, tok_loaded, loaded0, zeroed = sem("loaded"), sem("tok_loaded"), sem("loaded0"), sem("zeroed")
        col_max, all_max, dve_step = sem("col_max"), sem("all_max"), sem("dve_step")
        onehot_ready, e_ready, e_copied = sem("onehot_ready"), sem("e_ready"), sem("e_copied")
        emb_ready, h_ready = sem("emb_ready"), sem("h_ready")
        mean_ready, xc_ready, sq_ready = sem("mean_ready"), sem("xc_ready"), sem("sq_ready")
        var_ready, sd_ready, xn_ready = sem("var_ready"), sem("sd_ready"), sem("xn_ready")
        xl_ready, lm_ready, lm_copied = sem("xl_ready"), sem("lm_ready"), sem("lm_copied")
        fold_ready, m3_copied, m1_copied, sim2_ready = sem("fold_ready"), sem("m3_copied"), sem("m1_copied"), sem("sim2_ready")
        t2_ready, e2_ready, a_ready, at_ready, at_copied = sem("t2_ready"), sem("e2_ready"), sem("a_ready"), sem("at_ready"), sem("at_copied")
        nmax_ready, nall_ready, z_ready, zt_ready = sem("nmax_ready"), sem("nall_ready"), sem("z_ready"), sem("zt_ready")
        pinv_mm, xzt_ready, u_ready = sem("pinv_mm"), sem("xzt_ready"), sem("u_ready")
        v_ready, v_copied = sem("v_ready"), sem("v_copied")
        sim3_ready, max3_ready, exp3_ready = sem("sim3_ready"), sem("max3_ready"), sem("exp3_ready")
        p3t_ready, p3t_copied, w3_ready, w_ready = sem("p3t_ready"), sem("p3t_copied"), sem("w3_ready"), sem("w_ready")
        p3t_copied_a = sem("p3t_copied_a")
        g_mm, g_copied = sem("g_mm"), sem("g_copied")
        sim1_ready, sub1_ready, exp1_ready, p1_ready = sem("sim1_ready"), sem("sub1_ready"), sem("exp1_ready"), sem("p1_ready")
        p1t_ready, p1t_copied, o_ready, o_copied, y_ready = sem("p1t_ready"), sem("p1t_copied"), sem("o_ready"), sem("o_copied"), sem("y_ready")
        cleared, loaded1, loaded2, zero_ready = sem("cleared"), sem("loaded1"), sem("loaded2"), sem("zero_ready")
        logits_ready, lg_ready, exg_ready, oneh_ready = sem("logits_ready"), sem("lg_ready"), sem("exg_ready"), sem("oneh_ready")
        xtm_mm, xtm_copied, prefix_ready, routed = sem("xtm_mm"), sem("xtm_copied"), sem("prefix_ready"), sem("routed")
        sh_mm, sh_gelu, shy_ready, shy_added = sem("sh_mm"), sem("sh_gelu"), sem("shy_ready"), sem("shy_added")
        put, xb_free, xb_loaded, xbT_mm, xbT_copied = sem("put"), sem("xb_free"), [sem("xb_loaded0"), sem("xb_loaded1")], sem("xbT_mm"), sem("xbT_copied")
        w1s_free, w1s_ready, hb_mm, hb_free, hb_ready = sem("w1s_free"), sem("w1s_ready"), sem("hb_mm"), sem("hb_free"), sem("hb_ready")
        yb_mm, yb_free, yb_ready, yb_stored = sem("yb_mm"), sem("yb_free"), sem("yb_ready"), [sem("yb_stored0"), sem("yb_stored1")]
        got, comb_ready, combT_ready = [sem(f"got{i}") for i in range(NC)], sem("comb_ready"), sem("combT_ready")
        loaded3, p1_done, r1_done, p2_done, p3_done = sem("loaded3"), sem("p1_done"), sem("r1_done"), sem("p2_done"), sem("p3_done")
        qk_mm, parts_stored, v1_mm, v1_copied = sem("qk_mm"), sem("parts_stored"), sem("v1_mm"), sem("v1_copied")
        v1_cleared = sem("v1_cleared")
        ones_set, stack_loaded = sem("ones_set"), [sem(f"stack_loaded{i}") for i in range(RING)]
        s1_ready, s1_read, negm_ready, mT_ready, mparts_ready = sem("s1_ready"), sem("s1_read"), sem("negm_ready"), sem("mT_ready"), sem("mparts_ready")
        mrows = [sem("mrows0"), sem("mrows1")]
        st_ready, exp_done, pv_done, ot_copied, otT_ready, otT_read = sem("st_ready"), sem("exp_done"), sem("pv_done"), sem("ot_copied"), sem("otT_ready"), sem("otT_read")
        o_done, oT_ready = sem("o_done"), sem("oT_ready")
        loaded4, loaded5, node_mm, node_ready, node_sig = sem("loaded4"), sem("loaded5"), sem("node_mm"), sem("node_ready"), sem("node_sig")
        leaf_ready, leafT_mm, leafT_copied, leaf_stored = sem("leaf_ready"), sem("leafT_mm"), sem("leafT_copied"), sem("leaf_stored")
        pbc_loaded = [sem("pbc_loaded0"), sem("pbc_loaded1")]
        hid_mm, gelu_done, weighed, used, yT_ready, yT_mm, yout_ready = (sem(n) for n in (
            "hid_mm", "gelu_done", "weighed", "used", "yT_ready", "yT_mm", "yout_ready"))
        yout_stored = [sem("yout_stored0"), sem("yout_stored1")]

        def pinv_count(it, stage, k):
            return 12 * it + {0: 0, 1: 4, 2: 6, 3: 8}[stage] + k + 1

        step = [0]

        def pieces_before(u, i):
            return u * sum(len(max_pieces(c)) for c in range(CB)) + sum(len(max_pieces(c)) for c in range(i))

        def tiles_before(u, i):
            return u * sum(len(exp_tiles(c)) for c in range(CB)) + sum(len(exp_tiles(c)) for c in range(i))

        def where(n):
            u, n = divmod(n, tiles_before(1, 0))
            for i in range(CB):
                if n < len(exp_tiles(i)):
                    return u, i, n
                n -= len(exp_tiles(i))

        def hidden_bank(m):
            return bank[(0, 1, 2, 6)[m % 4]]

        def leaf_rows2(c):
            return leaf_rows.ap()[:, bass.ds(c * CH, CH)].partition_broadcast(P)

        blk = ctx.enter_context(nc.Block())

        @blk.sync
        def _(sp):
            sp.dma_start(tok, a["x"].rearrange("b t -> (b t)").partition_broadcast(P)).then_inc(tok_loaded, 16)
            sp.wait_ge(zeroed, 1)
            for dst, src in ((emb[0:VOC, :], a["emb"]), (conv2[:, :], a["conv2"]), (ident[:, :], a["c_ident"]),
                             (idk[:, :, :], a["c_idk"]), (mean_w[:, :], a["c_mean"]), (iota[:, :], a["c_iota"]),
                             (b_out[:, :], a["b_out"])):
                sp.dma_start(dst, src).then_inc(loaded, 16)
            for dst, src in ((wqkv, a["wqkv"]), (wqT, a["wqT"]), (wkT, a["wkT"]), (wout, a["wout"]),
                             (band, a["band"])):
                sp.dma_start(dst, src).then_inc(loaded0, 16)
            sp.wait_ge(zero_ready, 1)
            for k in range(BK):
                sp.dma_start(xbuf[k].ap()[0:SLOTS, :].rearrange("(n p) d -> p n d", p=P),
                             zero.unsqueeze(1).to_broadcast([P, NBLK, P])).then_inc(cleared, 16)
            sp.wait_ge(y_ready, NC)
            for dst, src in ((ws1, a["ws1"]), (ws2, a["ws2"]), (b1, a["b1"]), (bs1, a["bs1"]), (bs2, a["bs2"]),
                             (brt, a["brt"].partition_broadcast(P)), (wr, a["wr"]), (ones, a["c_ones"]), (tri, a["c_tri"]),
                             (cr, a["c_route"])):
                sp.dma_start(dst, src).then_inc(loaded1, 16)
            for dst, src in ((b2, a["b2"].partition_broadcast(P)), (w1[:, 0:E], a["w1"][:, 0:E]), (w2[:, 0:E], a["w2"][:, 0:E]),
                             (w1[:, E:], a["w1"][:, E:]), (w2[:, E:], a["w2"][:, E:])):
                sp.dma_start(dst, src).then_inc(loaded2, 16)
            sp.wait_ge(put, 16 * TG)
            for k in range(BK):
                with sp.Fori(0, NBLK // 2) as i:
                    for s in range(2):
                        sp.wait_ge(xb_free, i * 2 + (k * NBLK + s + 1))
                        sp.dma_start(xb[:, s, :], xbuf[k].ap()[bass.ds((i * 2 + s) * P, P), :]).then_inc(xb_loaded[s], 16)
            sp.wait_ge(combT_ready, NC)
            for dst, src in ((wqkvT, a["wqkvT"]), (bvt, a["bv"].partition_broadcast(P)), (masks, a["c_masks"]), (bqk, a["bqk"])):
                sp.dma_start(dst, src).then_inc(loaded3, 16)
            for c in range(NC):
                for k in range(2):
                    n = 2 * c + k
                    sp.wait_ge(p3_done, n + 1)
                    sp.dma_start(qk_parts[k].ap()[:, c * CH:(c + 1) * CH].rearrange("(r p) c -> p r c", r=3),
                                 parts[:, k, c % 2]).then_inc(parts_stored, 16)
                sp.wait_ge(parts_stored, 32 * (c + 1))

            def load_unit(u):
                b, h, s = u // H1, u % H1, u % RING
                if u >= RING:
                    sp.wait_ge(st_ready, tiles_before(u - RING + 1, 0))
                    sp.wait_ge(s1_ready, pieces_before(u - RING + 1, 0))
                t = slice(b * T, (b + 1) * T)
                q = qk_parts[0].ap().rearrange("(r h f) t -> r h f t", r=3, f=D1)
                k = qk_parts[1].ap().rearrange("(r h f) t -> r h f t", r=3, f=D1)
                for dst, r0, src in ((QS, 0, q[0, h, :, t].unsqueeze(0).to_broadcast([3, D1, T])),
                                     (QS, 3, q[1, h, :, t].unsqueeze(0).to_broadcast([2, D1, T])),
                                     (QS, 5, q[2, h, :, t]),
                                     (KS, 0, k[:, h, :, t]), (KS, 3, k[0:2, h, :, t]), (KS, 5, k[0, h, :, t])):
                    rows = (3, 0, 0, 2, 0, 1)[r0]
                    sp.dma_start(dst[r0 * D1:(r0 + rows) * D1, s, :], src).then_inc(stack_loaded[s], 16)

            def row_of_maxima(u):
                sp.wait_ge(mparts_ready, u + 1)
                for r in range(3):
                    sp.dma_start(QS[KS_ROWS + r:KS_ROWS + r + 1, u % RING, :],
                                 mparts[0:TB, u % 2, r, :]).then_inc(mrows[u % 2], 16)
            for u in range(RING):
                load_unit(u)
            for u in range(UN):
                row_of_maxima(u)
                if RING <= u + 4 < UN:
                    load_unit(u + 4)
            sp.wait_ge(oT_ready, NC)
            for dst, src in ((fb1, a["fb1"]), (rwT, a["rwT"]), (rbt, a["rb"].partition_broadcast(P)), (fb2, a["fb2"])):
                sp.dma_start(dst, src).then_inc(loaded4, 16)
            for dst, src in ((f1, a["f1"]), (f2, a["f2"])):
                sp.dma_start(dst, src).then_inc(loaded5, 16)
            sp.wait_ge(leafT_copied, NC)
            sp.dma_start(leaf_rows.ap()[:, 0:N], leafT).then_inc(leaf_stored, 16)
            sp.dma_start(leaf_rows.ap()[:, N:N + 2 * CH], leafT[:, 0:2 * CH]).then_inc(leaf_stored, 16)
            sp.wait_ge(leaf_stored, 32)

            def load_weights(c, s):
                sp.dma_start(pbc[:, s], leaf_rows.ap()[:, bass.ds(c * CH, CH)].partition_broadcast(P)).then_inc(pbc_loaded[s], 16)
            load_weights(0, 0)
            load_weights(1, 1)
            with sp.Fori(0, NC // 2) as i:
                for s in range(2):
                    sp.wait_ge(yout_ready, i * 2 + (s + 2))
                    sp.dma_start(a["out"].rearrange("(c t p) d -> c p t d", t=TC, p=P)[bass.ds(i * 2 + s, 1)].rearrange("c p t d -> (c p) t d"),
                                 yout[:, s]).then_inc(yout_stored[s], 16)
                    if s == 0:
                        sp.wait_ge(weighed, (i * 2 + 1) * HK)
                        sp.dma_start(pbc[:, 0], leaf_rows2(i * 2 + 2)).then_inc(pbc_loaded[0], 16)
                    else:
                        sp.wait_ge(weighed, (i * 2 + 2) * HK)
                        sp.dma_start(pbc[:, 1], leaf_rows2(i * 2 + 3)).then_inc(pbc_loaded[1], 16)
            for s in range(2):
                sp.wait_ge(yout_stored[s], 16 * (NC // 2 + 1))
                sp.wait_ge(pbc_loaded[s], 16 * (NC // 2 + 1))

        def norm_pe(pe, n):
            if n > 0:
                pe.wait_ge(h_ready, (n + 1) * NC)
            for c in range(NC + 1):
                i = n * NC + c
                if c < NC:
                    pe.wait_ge(h_ready, i + 1)
                    if i >= 2:
                        pe.wait_ge(xc_ready, i - 1)
                    nc.tensor.matmul(bank[6 + c % 2][:, :], mean_w[:, :], hT[:, c * CH:(c + 1) * CH],
                                     start=True, stop=True).then_inc(mean_ready, 1)
                if c > 0:
                    pe.wait_ge(sq_ready, i)
                    if i > 2:
                        pe.wait_ge(sd_ready, i - 2)
                    nc.tensor.matmul(bank[4 + (c - 1) % 2][:, :], mean_w[:, :], ln_sq[:, (c - 1) % 2, :],
                                     start=True, stop=True).then_inc(var_ready, 1)

        def norm_act(act, n):
            for c in range(NC):
                i = n * NC + c
                act.wait_ge(xc_ready, i + 1)
                if i >= 2:
                    act.wait_ge(var_ready, i - 1)
                nc.scalar.activation(ln_sq[:, c % 2, :], ln_xc[:, c % 2, :], ACT.Square).then_inc(sq_ready, 1)
                act.wait_ge(var_ready, i + 1)
                if i >= 2:
                    act.wait_ge(xn_ready, i - 1)
                nc.scalar.activation(ln_sd[:, c % 2, :], bank[4 + c % 2][:, :], ACT.Sqrt,
                                     bias=eps[:, :]).then_inc(sd_ready, 1)

        def norm_dve(dve, n):
            for c in range(NC + 1):
                i = n * NC + c
                if c < NC:
                    dve.wait_ge(mean_ready, i + 1)
                    if i >= 2:
                        dve.wait_ge(xn_ready, i - 1)
                        dve.wait_ge(sq_ready, i - 1)
                    nc.vector.tensor_tensor(ln_xc[:, c % 2, :], hT[:, c * CH:(c + 1) * CH], bank[6 + c % 2][:, :],
                                            ALU.subtract).then_inc(xc_ready, 1)
                if c > 0:
                    dve.wait_ge(sd_ready, i)
                    s = (c - 1) % 2
                    nc.vector.reciprocal(ln_sd[:, s, :], ln_sd[:, s, :]).then_inc(dve_step, 1)
                    step[0] += 1
                    dve.wait_ge(dve_step, step[0])
                    nc.vector.tensor_tensor(xnT[:, (c - 1) * CH:c * CH], ln_xc[:, s, :], ln_sd[:, s, :],
                                            ALU.mult).then_inc(xn_ready, 1)

        step = [0]

        @blk.vector
        def _(dve):
            def then(ins):
                ins.then_inc(dve_step, 1)
                step[0] += 1
                dve.wait_ge(dve_step, step[0])

            nc.vector.memset(emb, 0.0).then_inc(zeroed, 1)
            nc.vector.memset(eps[:, :], EPS)
            nc.vector.memset(zero, 0.0).then_inc(zero_ready, 1)
            nc.vector.memset(eT[:, :, 0:1], 0.0)
            dve.wait_ge(loaded, 16 * 7)
            nc.vector.tensor_reduce(qcol[:, 0:1], emb, X, ALU.max, apply_absolute_value=True)
            nc.vector.tensor_reduce(qcol[:, 1:2], conv2[:, :], X, ALU.max, apply_absolute_value=True).then_inc(col_max, 1)
            dve.wait_ge(all_max, 1)
            then(nc.vector.tensor_scalar(qcol[:, 4:6], qcol[:, 2:4], 1.0 / 127.0, None, ALU.mult))
            then(nc.vector.reciprocal(qcol[:, 6:8], qcol[:, 4:6]))
            for w, q, e, k in ((emb, emb_q, emb_e, 0), (conv2[:, :], ln_sq[:, 0, 0:2], ln_sq[:, 0, 2:4], 1)):
                then(nc.vector.tensor_scalar(q, w, qcol[:, 6 + k:7 + k], MAGIC, ALU.mult, ALU.add))
                then(nc.vector.tensor_scalar(q, q, MAGIC, qcol[:, 4 + k:5 + k], ALU.subtract, ALU.mult))
                then(nc.vector.tensor_tensor(e, q, w, ALU.subtract))
                then(nc.vector.tensor_tensor(e, e, w, ALU.add))
            then(nc.vector.tensor_copy(conv2[:, :], ln_sq[:, 0, 2:4]))
            dve.wait_ge(tok_loaded, 16)
            for c in range(NC + 1):
                if c < NC:
                    if c >= 2:
                        dve.wait_ge(e_ready, c - 1)
                    nc.vector.tensor_scalar(onehot[:, c % 2, :], tok[:, c * CH:(c + 1) * CH], float(VOC - 1), iota[:, :],
                                            ALU.min, ALU.is_equal).then_inc(onehot_ready, 1)
                if c > 0:
                    k = c - 1
                    b, t0 = k // CB, (k % CB) * CH
                    dve.wait_ge(e_copied, c)
                    then(nc.vector.tensor_scalar(tmp[:, k % 2, :], eT[:, b, 1 + t0:1 + t0 + CH], conv2[:, 1:2], None, ALU.mult))
                    then(nc.vector.scalar_tensor_tensor(tmp[:, k % 2, :], eT[:, b, t0:t0 + CH], conv2[:, 0:1], tmp[:, k % 2, :],
                                                        ALU.mult, ALU.add))
                    nc.vector.tensor_scalar(hT[:, k * CH:(k + 1) * CH], tmp[:, k % 2, :], 0.0, None, ALU.max).then_inc(h_ready, 1)
            norm_dve(dve, 0)

            for t in (QL, KL, A):
                nc.vector.memset(t, 0.0)
            dve.wait_ge(xn_ready, NC)
            nc.vector.tensor_reduce(xl, xnT[:, :].rearrange("p (m l) -> p m l", l=LM), X, ALU.add).then_inc(xl_ready, 1)
            dve.wait_ge(lm_ready, 1)
            for t, k, s in ((QL, 0, 0.125 / LM), (KL, 1, 1.0 / LM)):
                for j in range(2):
                    r = slice(64 * j, 64 * j + 64)
                    for b in range(B):
                        nc.vector.tensor_scalar(t[r, b * PR:(b + 1) * PR, r],
                                                bank[k][r, :].rearrange("p (g b m) -> p b g m", g=PR, b=B)[:, b],
                                                s, None, ALU.mult).then_inc(lm_copied, 1)
            dve.wait_ge(sim2_ready, 1)
            sim2 = [[bank[6 + k][64 * j:64 * j + 64, :].rearrange("p (g c) -> p g c", g=PR)[:, :, 64 * j:64 * j + 64]
                     for j in range(2)] for k in range(2)]
            for k in range(2):
                for j in range(2):
                    r = slice(64 * j, 64 * j + 64)
                    last = nc.vector.tensor_reduce(mx2[r, k * PR:(k + 1) * PR], sim2[k][j], X, ALU.max)
            then(last)
            for k in range(2):
                for j in range(2):
                    r = slice(64 * j, 64 * j + 64)
                    last = nc.vector.tensor_tensor(T2[r, k * PR:(k + 1) * PR, :], sim2[k][j],
                                                   mx2[r, k * PR:(k + 1) * PR].unsqueeze(2).to_broadcast([64, PR, 64]), ALU.subtract)
            last.then_inc(t2_ready, 1)
            dve.wait_ge(e2_ready, 1)
            then(nc.vector.tensor_reduce(s2[:, :], T2, X, ALU.add))
            then(nc.vector.reciprocal(r2[:, :], s2[:, :]))
            for j in range(2):
                r = slice(64 * j, 64 * j + 64)
                last = nc.vector.tensor_tensor(A[r, :, r], T2[r, :, :], r2[r, :].unsqueeze(2).to_broadcast([64, BP, 64]), ALU.mult)
            last.then_inc(a_ready, 1)
            dve.wait_ge(a_ready, 1)
            nc.vector.tensor_reduce(nsum[:, 0:BP], A, X, ALU.add, apply_absolute_value=True)
            dve.wait_ge(at_copied, 2)
            then(nc.vector.tensor_reduce(nsum[:, BP:2 * BP], AT, X, ALU.add, apply_absolute_value=True))
            nc.vector.tensor_reduce(nmax[:, :], nsum[:, :].rearrange("p (k g) -> p k g", k=2), X, ALU.max).then_inc(nmax_ready, 1)
            dve.wait_ge(nall_ready, 1)
            then(nc.vector.tensor_tensor(nrm[:, 0:1], nall[:, 0:1], nall[:, 1:2], ALU.mult))
            then(nc.vector.reciprocal(nrm[:, 1:2], nrm[:, 0:1]))
            for k in range(2):
                g = slice(k * PR, (k + 1) * PR)
                nc.vector.tensor_scalar(Z[0][:, g, :], AT[:, g, :], nrm[:, 1:2], None, ALU.mult).then_inc(z_ready, 1)
                nc.vector.tensor_scalar(ZT[0][:, g, :], A[:, g, :], nrm[:, 1:2], None, ALU.mult).then_inc(zt_ready, 1)
            for it in range(ITERS):
                for stage in range(3):
                    for k in range(2):
                        g = slice(k * PR, (k + 1) * PR)
                        dve.wait_ge(pinv_mm, pinv_count(it, stage, k))
                        src = bank[[0, 4, 0][stage] + k][:, :].rearrange("p (g c) -> p g c", g=PR)
                        nc.vector.scalar_tensor_tensor(U[:, g, :], src, -1.0,
                                                       idk[:, stage, :].unsqueeze(1).to_broadcast([P, PR, P]),
                                                       ALU.mult, ALU.add).then_inc(u_ready, 1)
                for k in range(2):
                    g = slice(k * PR, (k + 1) * PR)
                    dve.wait_ge(pinv_mm, pinv_count(it, 3, k))
                    src = bank[4 + k][:, :].rearrange("p (g c) -> p g c", g=PR)
                    nc.vector.tensor_scalar(Z[(it + 1) % 2][:, g, :], src, 0.25, None, ALU.mult).then_inc(z_ready, 1)
            then(nc.vector.memset(W, 0.0))
            for i in range(BP + 1):
                if i < BP:
                    for c in range(CB):
                        dve.wait_ge(sim3_ready, i * CB + c + 1)
                        last = nc.vector.tensor_reduce(ln_sq[:, 0, c:c + 1], bank[c][:, :], X, ALU.max)
                    then(last)
                    nc.vector.tensor_reduce(m3[:, i:i + 1], ln_sq[:, 0, 0:CB], X, ALU.max, negate=True).then_inc(max3_ready, 1)
                    for q in (1, 3):
                        dve.wait_ge(p3t_ready, 4 * i + q + 1)
                        nc.vector.tensor_copy(P3T[:, i % 2, 4 * q:4 * q + 4, :],
                                              bank[4 + q % 2][:, :].rearrange("p (t c) -> p t c", t=4)).then_inc(p3t_copied, 1)
                if i > 0:
                    k = i - 1
                    dve.wait_ge(exp3_ready, CB * i)
                    then(nc.vector.tensor_reduce(s3[:, k:k + 1], s3p[:, k * CB:(k + 1) * CB], X, ALU.add))
                    then(nc.vector.reciprocal(r3[:, k:k + 1], s3[:, k:k + 1]))
                    dve.wait_ge(w3_ready, i)
                    for j in range(2):
                        r = slice(64 * j, 64 * j + 64)
                        last = nc.vector.tensor_scalar(W[r, k, r], bank[6 + k % 2][r, r], r3[r, k:k + 1], None, ALU.mult)
                    last.then_inc(w_ready, 1)
            for k in range(2):
                dve.wait_ge(g_mm, k + 1)
                nc.vector.tensor_copy(G[:, k * PR:(k + 1) * PR, :],
                                      bank[6 + k][:, :].rearrange("p (g c) -> p g c", g=PR)).then_inc(g_copied, 1)
            def soft1(t):
                s = t % 2
                sim = bank[s][:, :].rearrange("p (h m) -> p h m", h=H0)
                dve.wait_ge(sim1_ready, t + 1)
                then(nc.vector.tensor_reduce(m1[:, s, :], sim, X, ALU.max))
                if t >= 2:
                    dve.wait_ge(p1t_ready, t - 1)
                nc.vector.tensor_tensor(P1[:, s], sim, m1[:, s, :].unsqueeze(2).to_broadcast([P, H0, M]),
                                        ALU.subtract).then_inc(sub1_ready, 1)

            def norm1(t):
                s = t % 2
                dve.wait_ge(exp1_ready, t + 1)
                then(nc.vector.tensor_reduce(s1[:, s, :], P1[:, s], X, ALU.add))
                then(nc.vector.reciprocal(r1[:, s, :], s1[:, s, :]))
                nc.vector.tensor_tensor(P1[:, s], P1[:, s], r1[:, s, :].unsqueeze(2).to_broadcast([P, H0, M]),
                                        ALU.mult).then_inc(p1_ready, 1)

            def add0(c):
                dve.wait_ge(y_ready, c + 1)
                nc.vector.scalar_tensor_tensor(hT[:, c * CH:(c + 1) * CH], bank[7][:, :], b_out[:, 0:1],
                                               hT[:, c * CH:(c + 1) * CH], ALU.add, ALU.add).then_inc(h_ready, 1)
            soft1(0)
            for t in range(1, NT + 1):
                if t < NT:
                    soft1(t)
                norm1(t - 1)
                if t >= 2 * TC and t % TC == 0:
                    add0(t // TC - 2)
            add0(NC - 1)
            norm_dve(dve, 1)
            lg3 = lg.rearrange("p (g e) -> p g e", e=E)
            ex3 = ex.rearrange("p (g e) -> p g e", e=E)
            oneh3 = oneh.rearrange("p (g e) -> p g e", e=E)

            def wide(ap, n=TG):
                return ap.unsqueeze(2).to_broadcast([P, n, E])

            def const(lo, n):
                return cr[:, lo:lo + n]
            mx, cand, esum, ginv, pos, base, slot, keep, dst = (rs[:, i, :] for i in range(9))
            nb, sbk, ends = rs[:, 9, 0:16], rs[:, 10, 0:16], rs[:, 11, 0:16]
            dve.wait_ge(loaded1, 16 * 10)
            dve.wait_ge(cleared, 16 * BK)
            dve.wait_ge(logits_ready, 1)
            then(nc.vector.tensor_tensor(lg.rearrange("p (t c) -> p t c", t=NT), bank[0][:, :].rearrange("p (t c) -> p t c", t=NT),
                                         brt.unsqueeze(1).to_broadcast([P, NT, BK * E]), ALU.add))
            then(nc.vector.tensor_reduce(mx, lg3, X, ALU.max))
            nc.vector.tensor_tensor(lg3, lg3, wide(mx), ALU.subtract).then_inc(lg_ready, 1)
            dve.wait_ge(lg_ready, 1)
            then(nc.vector.tensor_scalar(oneh, lg, 0.0, None, ALU.is_equal))
            then(nc.vector.scalar_tensor_tensor(oneh3, oneh3, -float(E), const(C_IOTA8, E).unsqueeze(1).to_broadcast([P, TG, E]),
                                                ALU.mult, ALU.add))
            then(nc.vector.tensor_reduce(cand, oneh3, X, ALU.min))
            then(nc.vector.tensor_scalar(cand, cand, float(E), None, ALU.add))
            nc.vector.tensor_tensor(oneh3, const(C_IOTA8, E).unsqueeze(1).to_broadcast([P, TG, E]), wide(cand),
                                    ALU.is_equal).then_inc(oneh_ready, 1)
            dve.wait_ge(exg_ready, 1)
            then(nc.vector.tensor_reduce(esum, ex3, X, ALU.add))
            then(nc.vector.reciprocal(ginv, esum))
            dve.wait_ge(prefix_ready, 2)
            then(nc.vector.tensor_copy(sc_a, bank[7][:, :]))
            then(nc.vector.tensor_copy(tot, sc_a))
            src, dstb, w = sc_a, sc_b, BK * E
            for n in (1, 2, 4, 8, 16):
                nc.vector.tensor_copy(dstb[:, 0:n * w], src[:, 0:n * w])
                then(nc.vector.tensor_tensor(dstb[:, n * w:], src[:, n * w:], src[:, 0:(NT - n) * w], ALU.add))
                src, dstb = dstb, src
            incl = src
            total = incl[:, (NT - 1) * w:NT * w]
            cmp = ex[:, 0:160].rearrange("p (e j) -> p e j", j=CAP // P)
            then(nc.vector.tensor_tensor(cmp, total.unsqueeze(2).to_broadcast([P, w, CAP // P]),
                                         const(C_J128, CAP // P).unsqueeze(1).to_broadcast([P, w, CAP // P]), ALU.is_gt))
            then(nc.vector.tensor_reduce(nb, cmp, X, ALU.add))
            for k in range(BK):
                last = nc.vector.tensor_tensor(ex[:, 192 + k * 64:256 + k * 64].rearrange("p (e f) -> p e f", f=E),
                                               nb[:, k * E:(k + 1) * E].unsqueeze(1).to_broadcast([P, E, E]),
                                               const(C_LT, 64).rearrange("p (e f) -> p e f", f=E), ALU.mult)
            then(last)
            then(nc.vector.tensor_reduce(sbk, ex[:, 192:320].rearrange("p (e f) -> p e f", f=E), X, ALU.add))
            then(nc.vector.tensor_tensor(ends, sbk, nb, ALU.add))
            then(nc.vector.tensor_tensor(incl, incl, tot, ALU.subtract))
            then(nc.vector.tensor_tensor(incl, incl, bank[6][:, :], ALU.add))
            then(nc.vector.tensor_tensor(incl, incl, oneh, ALU.mult))
            then(nc.vector.tensor_reduce(pos, incl.rearrange("p (g e) -> p g e", e=E), X, ALU.add))
            then(nc.vector.tensor_tensor(tot.rearrange("p (t c) -> p t c", t=NT), oneh.rearrange("p (t c) -> p t c", t=NT),
                                         sbk.unsqueeze(1).to_broadcast([P, NT, w]), ALU.mult))
            then(nc.vector.tensor_reduce(base, tot.rearrange("p (g e) -> p g e", e=E), X, ALU.add))
            then(nc.vector.scalar_tensor_tensor(slot, base, float(P), pos, ALU.mult, ALU.add))
            then(nc.vector.tensor_scalar(keep, pos, float(CAP), None, ALU.is_lt))
            then(nc.vector.tensor_tensor(gate.rearrange("p t k -> p (t k)"), ginv, keep, ALU.mult))
            trash = const(C_TRASH, NT).unsqueeze(2).to_broadcast([P, NT, BK])

            def tk(ap):
                return ap.rearrange("p (t k) -> p t k", k=BK)
            then(nc.vector.tensor_tensor(tk(dst), tk(slot), trash, ALU.subtract))
            then(nc.vector.tensor_tensor(dst, dst, keep, ALU.mult))
            then(nc.vector.tensor_tensor(tk(dst), tk(dst), trash, ALU.add))
            for k in range(BK):
                nc.vector.tensor_copy(put_at[:, k, :], tk(dst)[:, :, k])
                nc.vector.tensor_scalar(get_at[:, k, :], tk(dst)[:, :, k], float(SLOTS - 1), None, ALU.min)
            for k in range(BK):
                e4 = ex[:, 0:NBLK * E].rearrange("p (n e) -> p n e", e=E)
                then(nc.vector.tensor_tensor(e4, const(C_IOTAB, NBLK).unsqueeze(2).to_broadcast([P, NBLK, E]),
                                             ends[:, k * E:(k + 1) * E].unsqueeze(1).to_broadcast([P, NBLK, E]), ALU.is_ge))
                then(nc.vector.tensor_reduce(incl[:, 0:NBLK], e4, X, ALU.add))
                then(nc.vector.tensor_scalar(expert_of[:, k, :], incl[:, 0:NBLK], float(E - 1), float(k * E), ALU.min, ALU.add))
            nc.vector.tensor_copy(rs[:, 12, 0:1], rs[:, 11, 0:1]).then_inc(routed, 1)
            for c in range(NC):
                dve.wait_ge(shy_ready, c + 1)
                nc.vector.scalar_tensor_tensor(hT[:, c * CH:(c + 1) * CH], bank[5][:, :], bs2, hT[:, c * CH:(c + 1) * CH],
                                               ALU.add, ALU.add).then_inc(shy_added, 1)
            dve.wait_ge(loaded2, 16 * 5)
            for k in range(BK):
                with dve.Fori(0, NBLK // 2) as i:
                    for s in range(2):
                        n = i * 2 + (k * NBLK + s + 1)
                        e = dve.value_load(expert_of[0:1, k, bass.ds(i * 2 + s, 1)], min_val=0, max_val=BK * E - 1)
                        dve.wait_ge(w1s_free, n)
                        nc.vector.tensor_copy(w1s[:, s, :], w1[:, bass.ds(e, 1), :].rearrange("p e f -> p (e f)"))
                        nc.vector.tensor_copy(b1s[:, s, :], b1[:, bass.ds(e, 1), :].rearrange("p e f -> p (e f)")).then_inc(w1s_ready, 1)
                        dve.wait_ge(xbT_mm, n)
                        nc.vector.tensor_copy(xbT[:, s, :], bank[s][:, 0:P]).then_inc(xbT_copied, 1)
                        dve.wait_ge(yb_mm, n)
                        dve.wait_ge(yb_free, n)
                        dve.wait_ge(yb_stored[s], (i + (k * NBLK // 2 + 1)) * 16)
                        nc.vector.tensor_tensor(yb[:, s, :], bank[4 + s][:, 0:P], b2[:, bass.ds(e, 1), :].rearrange("p e f -> p (e f)"),
                                                ALU.add).then_inc(yb_ready, 1)
            def addc(c):
                dve.wait_ge(combT_ready, c + 1)
                nc.vector.tensor_tensor(hT[:, c * CH:(c + 1) * CH], bank[6 + c % 2][:, :], hT[:, c * CH:(c + 1) * CH],
                                        ALU.add).then_inc(h_ready, 1)
            for t in range(NT):
                dve.wait_ge(got[t // TC], 16 * BK * TC)
                then(nc.vector.tensor_scalar(comb[:, t, :], ygt[:, t, 0, :], gate[:, t, 0:1], None, ALU.mult))
                nc.vector.scalar_tensor_tensor(comb[:, t, :], ygt[:, t, 1, :], gate[:, t, 1:2], comb[:, t, :],
                                               ALU.mult, ALU.add).then_inc(comb_ready, 1)
                if t % TC == TC - 1 and t > TC:
                    addc(t // TC - 1)
            addc(NC - 1)
            norm_dve(dve, 2)
            dve.wait_ge(loaded3, 16 * 4)
            then(nc.vector.tensor_scalar(bqk[:, 0:1], bqk[:, 0:1], 0.25, None, ALU.mult))
            for dst, src in ((mask_qk, masks[:, 0, :]), (mask_kq, masks[:, 1, :]), (identb, ident[:, :])):
                nc.vector.tensor_copy(dst, src)
            then(nc.vector.memset(V1, 0.0))
            then(nc.vector.memset(V1[:, :, :, D1:D1 + 1], 1.0))
            nc.vector.memset(pm, -3.0e38).then_inc(v1_cleared, 1)
            for c in range(NC):
                for k in range(2):
                    n = 2 * c + k
                    dve.wait_ge(p1_done, n + 1)
                    if n >= 2:
                        dve.wait_ge(p3_done, n - 1)
                    nc.vector.tensor_tensor(ln_sq[:, k, :], ln_xc[:, k, :], parts[:, k, c % 2, 0, :], ALU.subtract).then_inc(r1_done, 1)
                    dve.wait_ge(p2_done, n + 1)
                    nc.vector.tensor_tensor(parts[:, k, c % 2, 2, :], ln_sq[:, k, :], parts[:, k, c % 2, 1, :], ALU.subtract).then_inc(p3_done, 1)
                dve.wait_ge(v1_mm, c + 1)
                dve.wait_ge(v1_cleared, 1)
                nc.vector.tensor_tensor(V1[:, TC * c:TC * c + TC, :, 0:D1],
                                        bank[4 + c % 2][:, :].rearrange("p (t h c) -> p t h c", t=TC, h=H1),
                                        bvt.rearrange("p (h c) -> p h c", h=H1).unsqueeze(1).to_broadcast([P, TC, H1, D1]),
                                        ALU.add).then_inc(v1_copied, 1)

            def left_over(u, i):
                if u >= 0:
                    m = u * CB + i
                    dve.wait_ge(otT_ready, m + 1)
                    if i == 0 and u > 0:
                        dve.wait_ge(o_done, u)
                    if i == 0:
                        ins = nc.vector.tensor_copy(OS[:, 0:TC, :], bank[7].rearrange("p (t g c) -> p t g c", t=TC, g=4)[:, :, 0, 0:17])
                    else:
                        ins = nc.vector.tensor_reduce(OS[:, TC * i:TC * i + TC, :],
                                                  bank[7][:, :].rearrange("p (t g c) -> p t c g", t=TC, g=4)[:, :, 0:17, :], X, ALU.add)
                    ins.then_inc(otT_read, 1)
                    if i == CB - 1:
                        dve.wait_ge(otT_read, m + 1)
                        then(nc.vector.reciprocal(osum, OS[:, :, 16]))
                        b, h = u // H1, u % H1
                        nc.vector.tensor_tensor(O[:, b * TB:(b + 1) * TB, h, :], OS[:, :, 0:D1],
                                                osum.unsqueeze(2).to_broadcast([P, TB, D1]), ALU.mult).then_inc(o_done, 1)
                if i == CB - 1 and u + LEAD < UN:
                    v = u + LEAD
                    dve.wait_ge(mT_ready, v + 1)
                    if v >= 2:
                        dve.wait_ge(mrows[v % 2], 48 * (v // 2))
                    mt = bank[7][0:TB, 0:P]
                    mp = mparts[0:TB, v % 2]
                    then(nc.vector.tensor_copy(mp[:, 0, :], mt))
                    then(nc.vector.tensor_tensor(mres[0:TB, :], mt, mp[:, 0, :], ALU.subtract))
                    then(nc.vector.tensor_copy(mp[:, 1, :], mres[0:TB, :]))
                    nc.vector.tensor_tensor(mp[:, 2, :], mres[0:TB, :], mp[:, 1, :], ALU.subtract).then_inc(mparts_ready, 1)

            before = None
            for u, i in STEPS:
                items = step_items(u, i)
                seen = 0
                if before and maxima_before(items) == 0:
                    left_over(*before)
                for kind, x in items:
                    if kind == "max":
                        qt, s, w = x
                        v = u + LEAD
                        n = pieces_before(v, i) + seen
                        dve.wait_ge(s1_ready, n + 1)
                        if v >= 2:
                            dve.wait_ge(negm_ready, v - 1)
                        nc.vector.tensor_reduce(pm[:, v % 2, qt, s:s + 1], wide_bank(n % 2)[:, 0:w], X, ALU.max).then_inc(s1_read, 1)
                        seen += 1
                        if before and seen == maxima_before(items):
                            left_over(*before)
                if i == CB - 1 and u + LEAD < UN:
                    v = u + LEAD
                    dve.wait_ge(s1_read, pieces_before(v + 1, 0))
                    if v >= 2:
                        dve.wait_ge(mT_ready, v - 1)
                    nc.vector.tensor_reduce(negm[:, v % 2, :], pm[:, v % 2], X, ALU.max, negate=True).then_inc(negm_ready, 1)
                before = (u, i)
            left_over(*before)
            for c in range(NC):
                dve.wait_ge(oT_ready, c + 1)
                nc.vector.tensor_tensor(hT[:, c * CH:(c + 1) * CH], bank[c % 2][:, :], hT[:, c * CH:(c + 1) * CH],
                                        ALU.add).then_inc(h_ready, 1)
            norm_dve(dve, 3)
            dve.wait_ge(loaded4, 16 * 4)
            dve.wait_ge(node_mm, 1)
            nc.vector.tensor_tensor(node, bank[0][:, 0:NT * 8].rearrange("p (t n) -> p t n", n=8)[:, :, 0:7],
                                    rbt.unsqueeze(1).to_broadcast([P, NT, 7]), ALU.add).then_inc(node_ready, 1)
            dve.wait_ge(node_sig, 1)
            then(nc.vector.tensor_scalar(nodn, node, -1.0, 1.0, ALU.mult, ALU.add))
            nc.vector.tensor_copy(leaf1[:, :, 0:1], nodn[:, :, 0:1])
            then(nc.vector.tensor_copy(leaf1[:, :, 1:2], node[:, :, 0:1]))
            for lo, up, first, n in ((leaf1, leaf2, 1, 2), (leaf2, leaf3, 3, 4)):
                up = up.rearrange("p t (i s) -> p t i s", s=2)
                nc.vector.tensor_tensor(up[:, :, :, 0], lo, nodn[:, :, first:first + n], ALU.mult)
                last = nc.vector.tensor_tensor(up[:, :, :, 1], lo, node[:, :, first:first + n], ALU.mult)
                if n == 2:
                    then(last)
            last.then_inc(leaf_ready, 1)
            for c in range(NC):
                dve.wait_ge(leafT_mm, c + 1)
                nc.vector.tensor_copy(leafT[:, c * CH:(c + 1) * CH], bank[1 + c % 2][0:E, :]).then_inc(leafT_copied, 1)
            with dve.Fori(0, NC // 2) as i:
                for s in range(2):
                    dve.wait_ge(pbc_loaded[s], (i + 1) * 16)
                    for k in range(HK):
                        n = i * (2 * HK) + (s * HK + k)
                        dve.wait_ge(gelu_done, n + (1 + 4))
                        h = hid[:, (s * HK + k) % HB, :]
                        nc.vector.tensor_tensor(h, h, pbc[:, s, k // KF, :], ALU.mult).then_inc(weighed, 1)
                    dve.wait_ge(used, i * (2 * HK) + ((s + 1) * HK + HB))
                    dve.wait_ge(yT_mm, i * 2 + (s + 1))
                    nc.vector.tensor_tensor(yT, bank[3 + s], hT[:, bass.ds((i * 2 + s) * CH, CH)], ALU.add).then_inc(yT_ready, 1)

        def ot_copy(act, u, i):
            m = u * CB + i
            act.wait_ge(pv_done, tiles_before(u, i + 1))
            if m >= 2:
                act.wait_ge(otT_ready, m - 1)
            rows = 32 if i == 0 else P
            nc.scalar.copy(OTp[0:rows, m % 2, :], bank[6][0:rows, :]).then_inc(ot_copied, 1)

        @blk.scalar
        def _(act):
            for c in range(NC):
                b, t0 = c // CB, (c % CB) * CH
                act.wait_ge(e_ready, c + 1)
                nc.scalar.copy(eT[:, b, 1 + t0:1 + t0 + CH], bank[c % 2][:, :]).then_inc(e_copied, 1)
            norm_act(act, 0)
            act.wait_ge(fold_ready, 2)
            for k in range(2):
                nc.scalar.copy(M3[:, k * PR:(k + 1) * PR, :],
                               bank[2 + k][:, :].rearrange("p (g c) -> p g c", g=PR)).then_inc(m3_copied, 1)
            act.wait_ge(fold_ready, 4)
            for k in range(2):
                nc.scalar.mul(M1[:, k * PR:(k + 1) * PR, :],
                              bank[4 + k][:, :].rearrange("p (g c) -> p g c", g=PR), 0.125).then_inc(m1_copied, 1)
            act.wait_ge(t2_ready, 1)
            nc.scalar.activation(T2, T2, ACT.Exp).then_inc(e2_ready, 1)
            act.wait_ge(at_ready, 2)
            for k in range(2):
                nc.scalar.copy(AT[:, k * PR:(k + 1) * PR, :],
                               bank[k][:, :].rearrange("p (g c) -> p g c", g=PR)).then_inc(at_copied, 1)
            for it in range(ITERS):
                for k in range(2):
                    g = slice(k * PR, (k + 1) * PR)
                    act.wait_ge(pinv_mm, 12 * it + 2 + k + 1)
                    nc.scalar.copy(XZT[:, g, :], bank[2 + k][:, :].rearrange("p (g c) -> p g c", g=PR)).then_inc(xzt_ready, 1)
                for k in range(2):
                    g = slice(k * PR, (k + 1) * PR)
                    act.wait_ge(pinv_mm, 12 * it + 10 + k + 1)
                    nc.scalar.mul(ZT[(it + 1) % 2][:, g, :], bank[2 + k][:, :].rearrange("p (g c) -> p g c", g=PR),
                                  0.25).then_inc(zt_ready, 1)
            for t in range(NT):
                act.wait_ge(v_ready, t + 1)
                nc.scalar.copy(V[:, t, :], bank[6 + t % 2][:, :]).then_inc(v_copied, 1)
            for i in range(BP):
                act.wait_ge(max3_ready, i + 1)
                if i >= 2:
                    act.wait_ge(p3t_ready, 4 * (i - 1))
                for c in range(CB):
                    nc.scalar.activation(P3[:, i % 2, c * CH:(c + 1) * CH], bank[c][:, :], ACT.Exp, bias=m3[:, i:i + 1],
                                         accum_out=s3p[:, i * CB + c:i * CB + c + 1]).then_inc(exp3_ready, 1)
                if i >= 2:
                    act.wait_ge(w3_ready, i - 1)
                for q in (0, 2):
                    act.wait_ge(p3t_ready, 4 * i + q + 1)
                    nc.scalar.copy(P3T[:, i % 2, 4 * q:4 * q + 4, :],
                                   bank[4 + q % 2][:, :].rearrange("p (t c) -> p t c", t=4)).then_inc(p3t_copied_a, 1)

            def exp1(t):
                act.wait_ge(sub1_ready, t + 1)
                nc.scalar.activation(P1[:, t % 2], P1[:, t % 2], ACT.Exp).then_inc(exp1_ready, 1)

            def turn1(t):
                act.wait_ge(p1t_ready, t + 1)
                c, q = t // TC, t % TC
                nc.scalar.copy(P1T[:, c % 2, :, q * P:(q + 1) * P],
                               bank[2 + t % 2][:, :].rearrange("p (g c) -> p g c", g=PR)).then_inc(p1t_copied, 1)

            def out1(c):
                for g in range(PR):
                    act.wait_ge(o_ready, c * PR + g + 1)
                    if c >= 1 and g == 0:
                        act.wait_ge(y_ready, c)
                    nc.scalar.copy(OT[:, g, :], bank[4 + g % 2][:, :]).then_inc(o_copied, 1)
            exp1(0)
            for t in range(1, NT + 1):
                if t < NT:
                    exp1(t)
                turn1(t - 1)
                if t % TC == 0:
                    out1(t // TC - 1)
            norm_act(act, 1)
            for q in range(NC):
                act.wait_ge(xtm_mm, q + 1)
                nc.scalar.copy(xtm[:, 4 * q:4 * q + 4, :], bank[1 + q % 2][:, :].rearrange("p (t d) -> p t d", t=4)).then_inc(xtm_copied, 1)
            act.wait_ge(lg_ready, 1)
            nc.scalar.activation(ex, lg, ACT.Exp).then_inc(exg_ready, 1)
            for c in range(NC):
                for k in range(KF):
                    n = c * KF + k
                    act.wait_ge(sh_mm, n + 1)
                    if c >= 2 and k == 0:
                        act.wait_ge(shy_ready, c - 1)
                    nc.scalar.activation(hs[:, c % 2, k, :], bank[3 + n % 2][:, :], ACT.Gelu, bias=bs1[:, k:k + 1]).then_inc(sh_gelu, 1)
            for k in range(BK):
                with act.Fori(0, NBLK // 2) as i:
                    for s in range(2):
                        n = i * 2 + (k * NBLK + s + 1)
                        act.wait_ge(hb_mm, n)
                        act.wait_ge(w1s_ready, n)
                        act.wait_ge(hb_free, n)
                        for q in range(KF):
                            last = nc.scalar.activation(hb[:, s, q, :], bank[2 + s][:, q * P:(q + 1) * P], ACT.Gelu, bias=b1s[:, s, q:q + 1])
                        last.then_inc(hb_ready, 1)
                        act.wait_ge(yb_ready, n)
                        act.dma_start(ybuf[k].ap()[bass.ds((i * 2 + s) * P, P), :], yb[:, s, :]).then_inc(yb_stored[s], 16)
            norm_act(act, 2)
            act.wait_ge(loaded3, 16 * 4)
            act.wait_ge(v1_cleared, 1)
            for c in range(NC):
                for k in range(2):
                    n = 2 * c + k
                    act.wait_ge(qk_mm, n + 1)
                    if n >= 2:
                        act.wait_ge(r1_done, n - 1)
                    if c >= 2:
                        act.wait_ge(parts_stored, 32 * (c - 1))
                    scale = (0.25, 1.0)[k]
                    nc.scalar.activation(ln_xc[:, k, :], bank[2 * k + c % 2], ACT.Identity, bias=bqk[:, k:k + 1], scale=scale)
                    nc.scalar.activation(parts[:, k, c % 2, 0, :], bank[2 * k + c % 2], ACT.Identity, bias=bqk[:, k:k + 1],
                                         scale=scale).then_inc(p1_done, 1)
                    act.wait_ge(r1_done, n + 1)
                    nc.scalar.copy(parts[:, k, c % 2, 1, :], ln_sq[:, k, :]).then_inc(p2_done, 1)
            before = None
            for u, i in STEPS:
                seen = 0
                for kind, x in step_items(u, i):
                    if kind == "exp":
                        j, q0 = x
                        n = tiles_before(u, i) + seen
                        act.wait_ge(st_ready, n + 1)
                        if n >= 4:
                            act.wait_ge(pv_done, n - 3)
                        nc.scalar.activation(PT[:, n % 4, q0:CH], bank[4 + n % 2][:, q0:CH], ACT.Exp).then_inc(exp_done, 1)
                        seen += 1
                        if seen == 2 and before:
                            ot_copy(act, *before)
                if u >= 0:
                    before = (u, i)
            ot_copy(act, *before)
            norm_act(act, 3)
            act.wait_ge(node_ready, 1)
            nc.scalar.activation(node, node, ACT.Sigmoid).then_inc(node_sig, 1)
            act.wait_ge(loaded4, 16 * 4)
            act.sem_inc(gelu_done, 4)
            act.sem_inc(yout_ready, 1)
            for s in range(2):
                act.sem_inc(yout_stored[s], 16)
            with act.Fori(0, NC // 2) as i:
                for s in range(2):
                    for k in range(HK):
                        m = s * HK + k
                        n = i * (2 * HK) + m
                        act.wait_ge(hid_mm, n + 1)
                        act.wait_ge(used, n + 1)
                        nc.scalar.activation(hid[:, m % HB, :], hidden_bank(m), ACT.Gelu,
                                             bias=fb1[:, k // KF, k % KF:k % KF + 1]).then_inc(gelu_done, 1)
                    act.wait_ge(yT_mm, i * 2 + (s + 2))
                    act.wait_ge(yout_stored[s], (i + 1) * 16)
                    nc.scalar.copy(yout[:, s], bank[5].rearrange("p (t d) -> p t d", t=TC)).then_inc(yout_ready, 1)

        @blk.gpsimd
        def _(pool):
            pool.wait_ge(col_max, 1)
            nc.gpsimd.partition_all_reduce(qcol[:, 2:4], qcol[:, 0:2], P, RMAX).then_inc(all_max, 1)
            pool.wait_ge(nmax_ready, 1)
            nc.gpsimd.partition_all_reduce(nall[:, :], nmax[:, :], P, RMAX).then_inc(nall_ready, 1)
            pool.wait_ge(cleared, 16 * BK)
            pool.wait_ge(routed, 1)
            pool.wait_ge(xtm_copied, NC)
            for k in range(BK):
                for t in range(NT):
                    pool.indirect_dma_start(out=xbuf[k].ap(), out_offset=bass.IndirectOffsetOnAxis(ap=put_at[:, k, t:t + 1], axis=0),
                                            in_=xtm[:, t, :], in_offset=None).then_inc(put, 16)
            for s in range(2):
                pool.wait_ge(yb_stored[s], 16 * (BK * NBLK // 2 + 1))
            for t in range(NT):
                for k in range(BK):
                    pool.indirect_dma_start(out=ygt[:, t, k, :], out_offset=None, in_=ybuf[k].ap(),
                                            in_offset=bass.IndirectOffsetOnAxis(ap=get_at[:, k, t:t + 1], axis=0)).then_inc(got[t // TC], 16)
            pool.wait_ge(combT_ready, NC)
            nc.gpsimd.memset(KS[KS_ROWS:KROWS, :, :], 1.0).then_inc(ones_set, 1)

        @blk.tensor
        def _(pe):
            for c in range(NC):
                pe.wait_ge(onehot_ready, c + 1)
                if c >= 2:
                    pe.wait_ge(e_copied, c - 1)
                nc.tensor.matmul(bank[c % 2][:, :], emb_e, onehot[:, c % 2, :],
                                 start=True, stop=True).then_inc(e_ready, 1)
            norm_pe(pe, 0)
            pe.wait_ge(xl_ready, 1)
            pe.wait_ge(loaded0, 16 * 5)
            for k in range(2):
                for g in range(PR):
                    last = nc.tensor.matmul(bank[k][:, g * P:(g + 1) * P], wqkv[:, k * 512 + g * P:k * 512 + (g + 1) * P], xl,
                                            start=True, stop=True)
            last.then_inc(lm_ready, 1)
            pe.wait_ge(lm_copied, 8)
            for w, t, o in ((wkT, QL, 2), (wqT, KL, 4)):
                for b in range(B):
                    if o == 4:
                        pe.wait_ge(sd_ready, NC - b)
                    for g in range(PR):
                        last = nc.tensor.matmul(bank[o + b][:, g * P:(g + 1) * P], w[:, g, :], t[:, b * PR + g, :],
                                                start=True, stop=True)
                    last.then_inc(fold_ready, 1)
            for b in range(B):
                for g in range(PR):
                    last = nc.tensor.matmul(bank[6 + b][:, g * P:(g + 1) * P], QL[:, b * PR + g, :], KL[:, b * PR + g, :],
                                            start=True, stop=True)
            last.then_inc(sim2_ready, 1)
            pe.wait_ge(a_ready, 1)
            for b in range(B):
                for g in range(PR):
                    last = nc.tensor.transpose(bank[b][:, g * P:(g + 1) * P], A[:, b * PR + g, :], ident[:, :])
                last.then_inc(at_ready, 1)

            def products(o, lhsT, rhs, waits):
                for k in range(2):
                    for s, v in waits:
                        pe.wait_ge(s, v + k)
                    for g in range(k * PR, (k + 1) * PR):
                        last = nc.tensor.matmul(bank[o + k][:, (g % PR) * P:(g % PR + 1) * P], lhsT[:, g, :], rhs[:, g, :],
                                                start=True, stop=True)
                    last.then_inc(pinv_mm, 1)
            pe.wait_ge(at_copied, 2)
            pe.wait_ge(m3_copied, 2)
            pe.wait_ge(m1_copied, 2)
            for it in range(ITERS):
                z, zt = Z[it % 2], ZT[it % 2]
                u = 6 * it
                products(0, AT, z, [(z_ready, 2 * it + 1)] + ([(u_ready, u - 1)] if it else []))
                products(2, z, AT, [(z_ready, 2 * it + 1)] + ([(zt_ready, 2 * it + 1)] if it else []))
                products(4, XZT, U, [(xzt_ready, 2 * it + 1), (u_ready, u + 1)])
                products(0, XZT, U, [(u_ready, u + 3)])
                products(4, zt, U, [(u_ready, u + 5), (zt_ready, 2 * it + 1)])
                products(2, U, zt, [(u_ready, u + 5)])
            for t in range(NT):
                if t >= 2:
                    pe.wait_ge(v_copied, t - 1)
                nc.tensor.matmul(bank[6 + t % 2][:, :], xnT[:, t * P:(t + 1) * P], wqkv[:, 1024:1536],
                                 start=True, stop=True).then_inc(v_ready, 1)
            pe.wait_ge(v_copied, NT)
            pe.wait_ge(z_ready, 2 * ITERS + 2)
            for i in range(BP + 1):
                if i < BP:
                    b = i // PR
                    for c in range(CB):
                        if i >= 1:
                            pe.wait_ge(exp3_ready, (i - 1) * CB + c + 1)
                        nc.tensor.matmul(bank[c][:, :], M3[:, i, :], xnT[:, b * T + c * CH:b * T + (c + 1) * CH],
                                         start=True, stop=True).then_inc(sim3_ready, 1)
                if i > 0:
                    k = i - 1
                    b, g = k // PR, k % PR
                    if k >= 2:
                        pe.wait_ge(w_ready, k - 1)
                    for t in range(TB):
                        pe.wait_ge(p3t_copied_a if (t // 4) % 2 == 0 else p3t_copied, 2 * k + t // 8 + 1)
                        last = nc.tensor.matmul(bank[6 + k % 2][:, 0:P], P3T[:, k % 2, t, :], V[:, b * TB + t, g * P:(g + 1) * P],
                                                start=(t == 0), stop=(t == TB - 1))
                    last.then_inc(w3_ready, 1)
                if i < BP:
                    pe.wait_ge(exp3_ready, CB * (i + 1))
                    for q in range(4):
                        m = 4 * i + q
                        if m >= 2:
                            pe.wait_ge(p3t_copied_a if q % 2 == 0 else p3t_copied, m // 2)
                        for t in range(4 * q, 4 * q + 4):
                            last = nc.tensor.transpose(bank[4 + q % 2][:, (t % 4) * P:(t % 4 + 1) * P],
                                                       P3[:, i % 2, t * P:(t + 1) * P], ident[:, :])
                        last.then_inc(p3t_ready, 1)
            pe.wait_ge(w_ready, BP)
            pe.wait_ge(zt_ready, 2 * ITERS + 2)
            for k in range(2):
                for g in range(PR):
                    last = nc.tensor.matmul(bank[6 + k][:, g * P:(g + 1) * P], ZT[ITERS % 2][:, k * PR + g, :], W[:, k * PR + g, :],
                                            start=True, stop=True)
                last.then_inc(g_mm, 1)

            def sim1(t):
                b = t // TB
                if t >= 2:
                    pe.wait_ge(sub1_ready, t - 1)
                nc.tensor.matmul(bank[t % 2][:, :], xnT[:, t * P:(t + 1) * P],
                                 M1[:, b * PR:(b + 1) * PR, :].rearrange("p g c -> p (g c)"),
                                 start=True, stop=True).then_inc(sim1_ready, 1)

            def turn1(t):
                pe.wait_ge(p1_ready, t + 1)
                if t >= 2:
                    pe.wait_ge(p1t_copied, t - 1)
                for g in range(PR):
                    last = nc.tensor.transpose(bank[2 + t % 2][:, g * P:(g + 1) * P],
                                               P1[:, t % 2, 2 * g:2 * g + 2, :].rearrange("p h m -> p (h m)"), ident[:, :])
                last.then_inc(p1t_ready, 1)

            def out1(c):
                pe.wait_ge(p1t_copied, TC * (c + 1))
                b = c // CB
                for g in range(PR):
                    n = c * PR + g
                    if n >= 2:
                        pe.wait_ge(o_copied, n - 1)
                    o = bank[4 + g % 2]
                    nc.tensor.matmul(o[:, :], G[:, b * PR + g, :], P1T[:, c % 2, g, :], start=True, stop=False,
                                     skip_group_check=True)
                    pieces = conv_pieces(c)
                    for n, (t, c0, w, k0) in enumerate(pieces):
                        for j in range(2):
                            last = nc.tensor.matmul(o[64 * j:64 * j + 64, c0:c0 + w],
                                                    V[:, b * TB + t, g * P + 64 * j:g * P + 64 * j + 64],
                                                    band[:, 2 * g + j, k0:k0 + w], start=False,
                                                    stop=(n == len(pieces) - 1), skip_group_check=True)
                    last.then_inc(o_ready, 1)

            def project1(c):
                pe.wait_ge(o_copied, PR * (c + 1))
                if c >= 1:
                    pe.wait_ge(h_ready, NC + c)
                for g in range(PR):
                    last = nc.tensor.matmul(bank[7][:, :], wout[:, g, :], OT[:, g, :], start=(g == 0), stop=(g == PR - 1))
                last.then_inc(y_ready, 1)
            pe.wait_ge(g_copied, 2)
            pe.wait_ge(exp3_ready, BP * CB)
            sim1(0)
            for t in range(1, NT + 1):
                if t < NT:
                    sim1(t)
                turn1(t - 1)
                if t % TC == 0:
                    out1(t // TC - 1)
                    project1(t // TC - 1)
            norm_pe(pe, 1)
            pe.wait_ge(loaded1, 16 * 10)
            for t in range(NT):
                pe.wait_ge(xn_ready, NC + t // TC + 1)
                last = nc.tensor.matmul(bank[0][:, t * BK * E:(t + 1) * BK * E], xnT[:, t * P:(t + 1) * P], wr, start=True, stop=True)
            last.then_inc(logits_ready, 1)
            for q in range(NC):
                if q >= 2:
                    pe.wait_ge(xtm_copied, q - 1)
                for t in range(4 * q, 4 * q + 4):
                    last = nc.tensor.transpose(bank[1 + q % 2][:, (t % 4) * P:(t % 4 + 1) * P], xnT[:, t * P:(t + 1) * P], ident[:, :])
                last.then_inc(xtm_mm, 1)
            pe.wait_ge(sd_ready, 2 * NC)
            for c in range(NC + 1):
                if c < NC:
                    for k in range(KF):
                        n = c * KF + k
                        if n >= 2:
                            pe.wait_ge(sh_gelu, n - 1)
                        nc.tensor.matmul(bank[3 + n % 2][:, :], ws1[:, k * P:(k + 1) * P], xnT[:, c * CH:(c + 1) * CH],
                                         start=True, stop=True).then_inc(sh_mm, 1)
                if c == 2:
                    pe.wait_ge(oneh_ready, 1)
                    nc.tensor.matmul(bank[6][:, :], tri, oneh, start=True, stop=True).then_inc(prefix_ready, 1)
                    nc.tensor.matmul(bank[7][:, :], ones, oneh, start=True, stop=True).then_inc(prefix_ready, 1)
                if c > 0:
                    pe.wait_ge(sh_gelu, c * KF)
                    if c >= 2:
                        pe.wait_ge(shy_added, c - 1)
                    for k in range(KF):
                        last = nc.tensor.matmul(bank[5][:, :], ws2[:, k, :], hs[:, (c - 1) % 2, k, :], start=(k == 0), stop=(k == KF - 1))
                    last.then_inc(shy_ready, 1)
            pe.wait_ge(shy_added, NC)
            for s in (xb_free, w1s_free, hb_free, yb_free):
                pe.sem_inc(s, 2)
            for s in range(2):
                pe.sem_inc(yb_stored[s], 16)
            pe.wait_ge(loaded2, 16 * 5)
            for k in range(BK):
                with pe.Fori(0, NBLK // 2) as i:
                    for s in range(2):
                        n = i * 2 + (k * NBLK + s + 1)
                        e = pe.value_load(expert_of[0:1, k, bass.ds(i * 2 + s, 1)], min_val=0, max_val=BK * E - 1)
                        pe.wait_ge(xb_loaded[s], (i + (k * NBLK // 2 + 1)) * 16)
                        nc.tensor.transpose(bank[s][:, 0:P], xb[:, s, :], ident[:, :]).then_inc(xbT_mm, 1)
                        pe.wait_ge(xbT_copied, n)
                        pe.sem_inc(xb_free, 1)
                        pe.wait_ge(w1s_ready, n)
                        for q in range(KF):
                            last = nc.tensor.matmul(bank[2 + s][:, q * P:(q + 1) * P], w1s[:, s, q * P:(q + 1) * P], xbT[:, s, :],
                                                    start=True, stop=True)
                        last.then_inc(hb_mm, 1)
                        pe.wait_ge(hb_ready, n)
                        pe.sem_inc(w1s_free, 1)
                        for q in range(KF):
                            last = nc.tensor.matmul(bank[4 + s][:, 0:P], hb[:, s, q, :],
                                                    w2[:, bass.ds(e, 1), q, :].rearrange("p e d -> p (e d)"),
                                                    start=(q == 0), stop=(q == KF - 1))
                        last.then_inc(yb_mm, 1)
                        pe.wait_ge(yb_ready, n)
                        pe.sem_inc(hb_free, 1)
                        pe.sem_inc(yb_free, 1)
            for c in range(NC):
                pe.wait_ge(comb_ready, TC * (c + 1))
                if c >= 2:
                    pe.wait_ge(h_ready, 2 * NC + c - 1)
                for t in range(TC):
                    last = nc.tensor.transpose(bank[6 + c % 2][:, t * P:(t + 1) * P], comb[:, TC * c + t, :], ident[:, :])
                last.then_inc(combT_ready, 1)
            norm_pe(pe, 2)
            pe.wait_ge(loaded3, 16 * 4)
            pe.wait_ge(xn_ready, 3 * NC)
            for c in range(NC):
                for k in range(2):
                    if c >= 2:
                        pe.wait_ge(p1_done, 2 * (c - 2) + k + 1)
                    nc.tensor.matmul(bank[2 * k + c % 2], wqkvT[:, k, :], xnT[:, c * CH:(c + 1) * CH],
                                     start=True, stop=True).then_inc(qk_mm, 1)
                if c >= 2:
                    pe.wait_ge(v1_copied, c - 1)
                for t in range(TC):
                    last = nc.tensor.matmul(bank[4 + c % 2][:, t * P:(t + 1) * P], xnT[:, (TC * c + t) * P:(TC * c + t + 1) * P],
                                            wqkvT[:, 2, :], start=True, stop=True)
                last.then_inc(v1_mm, 1)
            pe.wait_ge(ones_set, 1)
            pe.wait_ge(v1_cleared, 1)
            pe.wait_ge(v1_copied, NC)

            def maxima(u, i, k, x):
                qt, s, w = x
                n = pieces_before(u, i) + k
                if k == 0 and i == 0:
                    pe.wait_ge(stack_loaded[u % RING], 96 * (u // RING + 1))
                if n >= 2:
                    pe.wait_ge(s1_read, n - 1)
                else:
                    pe.wait_ge(p1_done, 2 * NC)
                out = wide_bank(n % 2)
                q = QS[0:KS_ROWS, u % RING, qt * P:(qt + 1) * P]
                diag = 1024 * s + w == (qt + 1) * P
                for c0 in range(0, w, CH):
                    c1 = min(w, c0 + CH)
                    on_diag = diag and c1 == w
                    last = nc.tensor.matmul(out[:, c0:c1], q, KS[0:KS_ROWS, u % RING, 1024 * s + c0:1024 * s + c1],
                                            start=True, stop=True)
                    if on_diag:
                        last = nc.tensor.matmul(out[:, w - P:w], identb, mask_qk, start=False, stop=True, skip_group_check=True)
                last.then_inc(s1_ready, 1)

            def scores(u, i, k, x):
                j, q0 = x
                n = tiles_before(u, i) + k
                if k == 0 and i == 0:
                    pe.wait_ge(mrows[u % 2], 48 * (u // 2 + 1))
                if n >= 2:
                    pe.wait_ge(exp_done, n - 1)
                out = bank[4 + n % 2]
                diag = j >= TC * i
                last = nc.tensor.matmul(out[:, q0:CH], KS[0:KROWS, u % RING, j * P:(j + 1) * P],
                                        QS[0:KROWS, u % RING, i * CH + q0:(i + 1) * CH], start=True, stop=True)
                if diag:
                    last = nc.tensor.matmul(out[:, q0:q0 + P], identb, mask_kq, start=False, stop=True, skip_group_check=True)
                last.then_inc(st_ready, 1)

            def weigh(n):
                u, i, k = where(n)
                j, q0 = exp_tiles(i)[k]
                pe.wait_ge(exp_done, n + 1)
                if k == 0 and (u, i) != (0, 0):
                    pe.wait_ge(ot_copied, u * CB + i)
                g = j % 4 if i else 0
                nc.tensor.matmul(bank[6][32 * g:32 * g + 32, q0:CH], V1[:, (u // H1) * TB + j, u % H1, :], PT[:, n % 4, q0:CH],
                                 start=(j < 4 if i else j == 0), stop=True, skip_group_check=True).then_inc(pv_done, 1)

            def left_over(u, i):
                if u >= 0:
                    m = u * CB + i
                    pe.wait_ge(ot_copied, m + 1)
                    pe.wait_ge(mparts_ready, min(u + LEAD, UN))
                    if m >= 1:
                        pe.wait_ge(otT_read, m)
                    rows = 32 if i == 0 else P
                    for t in range(TC):
                        last = nc.tensor.transpose(bank[7][:, t * P:t * P + rows], OTp[0:rows, m % 2, t * P:(t + 1) * P],
                                                   ident[0:rows, 0:rows])
                    last.then_inc(otT_ready, 1)
                if i == CB - 1 and u + LEAD < UN:
                    v = u + LEAD
                    pe.wait_ge(negm_ready, v + 1)
                    if u >= 0:
                        pe.wait_ge(otT_read, u * CB + i + 1)
                    if v >= 1:
                        pe.wait_ge(mparts_ready, v)
                    nc.tensor.transpose(bank[7][0:TB, 0:P], negm[:, v % 2, :], ident[:, :]).then_inc(mT_ready, 1)

            before = None
            for u, i in STEPS:
                items = step_items(u, i)
                seen = {"max": 0, "exp": 0}
                for n, (kind, x) in enumerate(items):
                    if kind == "max":
                        maxima(u + LEAD, i, seen[kind], x)
                    else:
                        scores(u, i, seen[kind], x)
                        m = tiles_before(u, i) + seen[kind]
                        if m >= 2:
                            weigh(m - 2)
                    seen[kind] += 1
                    if before and n + 1 == pause(items):
                        left_over(*before)
                before = (u, i)
            weigh(tiles_before(UN, 0) - 2)
            weigh(tiles_before(UN, 0) - 1)
            left_over(*before)
            pe.wait_ge(o_done, UN)
            for c in range(NC):
                if c >= 2:
                    pe.wait_ge(h_ready, 3 * NC + c - 1)
                for t in range(TC):
                    last = nc.tensor.transpose(bank[c % 2][:, t * P:(t + 1) * P],
                                               O[:, TC * c + t].rearrange("p h c -> p (h c)"), ident[:, :])
                last.then_inc(oT_ready, 1)
            norm_pe(pe, 3)
            pe.wait_ge(loaded4, 16 * 4)
            for t in range(NT):
                pe.wait_ge(xn_ready, 3 * NC + t // TC + 1)
                last = nc.tensor.matmul(bank[0][:, t * 8:t * 8 + 7], xnT[:, t * P:(t + 1) * P], rwT, start=True, stop=True)
            last.then_inc(node_mm, 1)
            pe.wait_ge(leaf_ready, 1)
            for c in range(NC):
                if c >= 2:
                    pe.wait_ge(leafT_copied, c - 1)
                for t in range(TC):
                    last = nc.tensor.transpose(bank[1 + c % 2][0:E, t * P:(t + 1) * P], leaf3[:, TC * c + t, :], ident[:, :])
                last.then_inc(leafT_mm, 1)
            pe.wait_ge(leafT_copied, NC)
            pe.wait_ge(sd_ready, 4 * NC)
            pe.wait_ge(loaded5, 16 * 2)
            pe.sem_inc(used, HB)
            pe.sem_inc(yT_mm, 1)
            with pe.Fori(0, NC // 2) as i:
                for s in range(2):
                    xc = xnT[:, bass.ds((i * 2 + s) * CH, CH)]
                    for k in range(HK + LAG1):
                        m = s * HK + k
                        n = i * (2 * HK) + m
                        if k < HK:
                            pe.wait_ge(gelu_done, n + 1)
                            nc.tensor.matmul(hidden_bank(m), f1[:, k // KF, (k % KF) * P:(k % KF + 1) * P], xc,
                                             start=True, stop=True).then_inc(hid_mm, 1)
                        if k == 0:
                            nc.tensor.matmul(bank[3 + s], fb2, leafT[:, bass.ds((i * 2 + s) * CH, CH)], start=True, stop=False)
                        if k >= LAG1:
                            q = k - LAG1
                            pe.wait_ge(weighed, n + (1 - LAG1))
                            last = nc.tensor.matmul(bank[3 + s], f2[:, q // KF, q % KF, :], hid[:, (m - LAG1) % HB, :],
                                                    start=False, stop=(q == HK - 1))
                            last.then_inc(used, 1)
                    pe.wait_ge(yT_ready, i * 2 + s + 1)
                    pe.wait_ge(yout_ready, i * 2 + (s + 1))
                    for t in range(TC):
                        last = nc.tensor.transpose(bank[5][:, t * P:(t + 1) * P], yT[:, t * P:(t + 1) * P], ident[:, :])
                    last.then_inc(yT_mm, 1)


def host(ins):
    import numpy as np
    f = {}
    f["x"] = np.ascontiguousarray(ins["x"])
    f["emb"] = np.ascontiguousarray(ins["L0_tok_emb_weight"])
    f["conv2"] = np.ascontiguousarray(np.asarray(ins["L0_tok_conv_weight"])[:, 0, :])
    eye = np.eye(P, dtype=np.float32)
    f["c_ident"] = eye
    f["c_idk"] = np.ascontiguousarray(np.stack([7 * eye, 15 * eye, 13 * eye], axis=1))
    f["c_mean"] = np.full((P, P), 1 / P, np.float32)
    f["c_iota"] = np.arange(P, dtype=np.float32)[:, None].copy()
    f["b_out"] = np.asarray(ins["L0_attn_b_out"])[:, None].copy()
    w = np.asarray(ins["L0_attn_W_qkv"])
    f["wqkv"] = w
    f["wqT"] = np.ascontiguousarray(w[:, 0:512].T.reshape(PR, P, P).transpose(1, 0, 2))
    f["wkT"] = np.ascontiguousarray(w[:, 512:1024].T.reshape(PR, P, P).transpose(1, 0, 2))
    f["wout"] = np.ascontiguousarray(np.asarray(ins["L0_attn_W_out"]).reshape(PR, P, P).transpose(1, 0, 2))
    cw = np.asarray(ins["L0_attn_conv_w"])[:, 0, :, 0]
    band = np.zeros((P, H0, CW), np.float32)
    for p in range(P):
        band[p, :, p:p + K] = cw[:, ::-1]
    f["band"] = band

    def g(n):
        return np.asarray(ins[n])
    f["ws1"] = g("L0_ffn_Ws1")
    f["ws2"] = np.ascontiguousarray(g("L0_ffn_Ws2").reshape(KF, P, P).transpose(1, 0, 2))
    f["bs1"] = np.ascontiguousarray(g("L0_ffn_bs1").reshape(KF, P).T)
    f["bs2"] = g("L0_ffn_bs2")[:, None].copy()
    f["wr"] = np.concatenate([g("L0_ffn_Wr_sp"), g("L0_ffn_Wr_fq")], axis=1)
    f["brt"] = np.concatenate([g("L0_ffn_br_sp"), g("L0_ffn_br_fq")])
    f["w1"] = np.ascontiguousarray(np.concatenate([g("L0_ffn_W1_sp"), g("L0_ffn_W1_fq")]).transpose(1, 0, 2))
    w2 = np.concatenate([g("L0_ffn_W2_sp"), g("L0_ffn_W2_fq")])
    f["w2"] = np.ascontiguousarray(w2.reshape(BK * E, KF, P, P).transpose(2, 0, 1, 3))
    bb = np.concatenate([g("L0_ffn_b1_sp"), g("L0_ffn_b1_fq")])
    f["b1"] = np.ascontiguousarray(bb.reshape(BK * E, KF, P).transpose(2, 0, 1))
    f["b2"] = np.concatenate([g("L0_ffn_b2_sp"), g("L0_ffn_b2_fq")])
    f["f1"] = np.ascontiguousarray(g("L1_ffn_w1").transpose(1, 0, 2))
    f["f2"] = np.ascontiguousarray(g("L1_ffn_w2").reshape(E, KF, P, P).transpose(2, 0, 1, 3))
    f["fb1"] = np.ascontiguousarray(g("L1_ffn_b1").reshape(E, KF, P).transpose(2, 0, 1))
    f["fb2"] = g("L1_ffn_b2")
    f["rwT"] = np.ascontiguousarray(g("L1_ffn_rw").T)
    f["rb"] = g("L1_ffn_rb")
    wt = np.stack([g("L1_attn_W" + x).T for x in "qkv"], axis=1)
    f["wqkvT"] = np.ascontiguousarray(wt)
    f["bv"] = g("L1_attn_bv")
    f["bqk"] = np.stack([g("L1_attn_bq"), g("L1_attn_bk")], axis=1)
    f["c_masks"] = np.ascontiguousarray(np.stack([np.triu(np.full((P, P), NEG, np.float32), 1),
                                                  np.tril(np.full((P, P), NEG, np.float32), -1)], axis=1))
    f["c_ones"] = np.ones((P, P), np.float32)
    f["c_tri"] = np.triu(np.ones((P, P), np.float32), 1)
    cr = np.zeros((P, C_ROUTE), np.float32)
    cr[:, C_IOTA8:C_IOTA8 + E] = np.arange(E)
    cr[:, C_J128:C_J128 + CAP // P] = P * np.arange(CAP // P)
    cr[:, C_LT:C_LT + E * E] = np.tril(np.ones((E, E)), -1).ravel()
    cr[:, C_TRASH:C_TRASH + NT] = SLOTS + np.arange(P)[:, None] + P * np.arange(NT)[None]
    cr[:, C_IOTAB:C_IOTAB + NBLK] = np.arange(NBLK)
    f["c_route"] = cr
    return f


def kernel(**inputs):
    import concourse.bacc as bacc
    from concourse.bass_utils import run_bass_kernel_spmd

    nc = bacc.Bacc("TRN2", target_bir_lowering=False, num_devices=1)
    arrays, aps = {}, {}
    for name, value in host(inputs).items():
        arrays["in_" + name] = value
        aps[name] = nc.dram_tensor("in_" + name, value.shape, mybir.dt.from_np(value.dtype), kind="ExternalInput").ap()
    aps["out"] = nc.dram_tensor("out_h", (N, P), F32, kind="ExternalOutput").ap()
    tower(nc, aps)
    result = run_bass_kernel_spmd(nc, [arrays], core_ids=[0])
    return result.results[0]["out_h"].reshape(B, T, P)
```

```python
from contextlib import ExitStack

import concourse.bass as bass
from concourse import mybir

F32 = mybir.dt.float32
BF16 = mybir.dt.bfloat16
I32 = mybir.dt.int32
ALU = mybir.AluOpType
ACT = mybir.ActivationFunctionType
X = mybir.AxisListType.X
RMAX = bass.bass_isa.ReduceOp.max

P = 128
B = 2
T = 2048
N = B * T
CH = 512
NC = N // CH
NT = N // P
TB = T // P
CB = T // CH
TC = CH // P
VOC = 125
EPS = 1e-5
MAGIC = 1.5 * 2.0 ** 23

PL0, DL0, PL, DL = 2, 4, 2, 3

H0, M, K = 8, 64, 33
PR = H0 // 2
LM = T // M
ITERS = 6
HALF = K // 2
CW = P + K - 1
BP = B * PR

E, KF = 8, 4
CAP = 1280
NBLK = N // P + E
SLOTS = NBLK * P
BK = 2
TG = NT * BK
ALLB = BK * NBLK
XS = 4
GG = 4
C_IOTA8, C_J128, C_LT, C_TRASH, C_IOTAB = 0, 8, 18, 82, 82 + NT
C_ROUTE = C_IOTAB + NBLK


H1, D1 = 8, 16
UN = B * H1
TERMS = 6
KS_ROWS = TERMS * D1
KROWS = KS_ROWS + 3
RING = 8
SB = 3
WR = 6
LEAD = 2
NEG = -1e30


def max_pieces(i):
    return [(qt, s, min(CH, (qt + 1) * P - CH * s)) for qt in range(TC * i, TC * i + TC) for s in range(i + 1)]


def exp_tiles(i):
    return [(j, max(0, (j - TC * i) * P)) for j in range(TC * (i + 1))]


def step_items(u, i):
    pieces = [("max", x) for x in max_pieces(i)] if u + LEAD < UN else []
    tiles = [("exp", x) for x in exp_tiles(i)] if u >= 0 else []
    out, n = [], max(len(pieces), len(tiles))
    for k in range(n):
        out += pieces[len(pieces) * k // n:len(pieces) * (k + 1) // n] + tiles[len(tiles) * k // n:len(tiles) * (k + 1) // n]
    return out


def pause(items):
    seen = 0
    for n, (kind, _) in enumerate(items):
        seen += kind == "exp"
        if seen == 4:
            return n + 1
    return len(items)


def maxima_before(items):
    return sum(kind == "max" for kind, _ in items[:pause(items)])


LAG1 = 3
HB = 4
HK = E * KF

OUT_LAG = TC + 2
STEPS1 = NT + OUT_LAG + 1
STEPS = [(u, i) for u in range(-LEAD, UN) for i in range(CB)]


def conv_pieces(c):
    lo, out = (c % CB) * CH, []
    for t in range(TB):
        a, b = max(t * P - HALF, lo), min(t * P - HALF + CW, lo + CH)
        if a < b:
            out.append((t, a - lo, b - a, a - (t * P - HALF)))
    return out


def tower(nc, a):
    with ExitStack() as ctx:
        def sb(name, shape, dt=F32):
            return ctx.enter_context(nc.sbuf_tensor(name, shape, dt))

        def sem(name):
            return ctx.enter_context(nc.semaphore(name))

        low = ctx.enter_context(nc.psum_tensor("low", [P, 4 * CH], F32))
        high = ctx.enter_context(nc.psum_tensor("high", [P, 4 * CH], F32))
        bank = [(low if i < 4 else high)[:, (i % 4) * CH:(i % 4 + 1) * CH] for i in range(8)]

        hT = sb("hT", [P, N])
        xnT = sb("xnT", [P, N])
        arena_a = sb("arena_a", [P, 16384])
        arena_b = sb("arena_b", [P, 16384])
        arena_c = sb("arena_c", [P, 8192])
        ident = sb("ident", [P, P])
        idk = sb("idk", [P, 3, P])
        centre = sb("centre", [P, P])
        mean_col = sb("mean_col", [P, 1])
        ones_w = sb("ones_w", [P, P])
        iota = sb("iota", [P, 1])
        eps = sb("eps", [P, 1])
        conv2 = sb("conv2", [P, 2])
        qcol = sb("qcol", [P, 8])
        b_out = sb("b_out", [P, 1])

        tok = arena_c[:, 0:N].bitcast(I32)
        emb = arena_c[:, N:N + P]
        emb_q = arena_c[:, N + P:N + 2 * P]
        emb_e = arena_c[:, N + 2 * P:N + 3 * P]
        onehot = arena_b[:, 0:2 * CH].rearrange("p (s c) -> p s c", s=2)
        eT = arena_a[:, 0:B * (T + 1)].rearrange("p (b t) -> p b t", b=B)
        tmp = arena_b[:, 2 * CH:4 * CH].rearrange("p (s c) -> p s c", s=2)

        ln_xc = sb("ln_xc", [P, 2, CH])
        ln_sq = sb("ln_sq", [P, 2, CH])
        ln_sd = sb("ln_sd", [P, 2, TC])

        V = arena_a[:, :].rearrange("p (t f) -> p t f", t=NT)

        def block(i):
            return arena_b[:, i * BP * P:(i + 1) * BP * P].rearrange("p (g c) -> p g c", g=BP)
        QL, KL, M3, M1, A, AT, Z0, Z1, ZT0, ZT1, XZT, U = (block(i) for i in range(12))
        Z, ZT = [Z0, Z1], [ZT0, ZT1]
        W, G = QL, KL
        P3 = arena_c[:, 0:2 * T].rearrange("p (s n) -> p s n", s=2)
        P3T = arena_c[:, 2 * T:4 * T].rearrange("p (s t c) -> p s t c", s=2, t=TB)
        P1 = arena_c[:, 0:2 * CH].rearrange("p (s h m) -> p s h m", s=2, h=H0)
        P1T = arena_c[:, 2 * CH:10 * CH].rearrange("p (s g c) -> p s g c", s=2, g=PR)
        OT = arena_c[:, 10 * CH:14 * CH].rearrange("p (g c) -> p g c", g=PR)
        wqkv = arena_b[:, 12 * BP * P:12 * BP * P + 1536]
        wqT, wkT = Z1[:, 0:PR, :], ZT1[:, 0:PR, :]
        wout = arena_b[:, 13824:13824 + 512].rearrange("p (g d) -> p g d", g=PR)
        band = arena_b[:, 14336:14336 + H0 * CW].rearrange("p (h c) -> p h c", h=H0)
        xl = arena_b[:, 15616:15616 + P]
        T2 = U.rearrange("p g c -> p (g c)")[:, 0:512].rearrange("p (g m) -> p g m", g=BP)
        mx2 = sb("mx2", [P, BP])
        s2 = sb("s2", [P, BP])
        r2 = sb("r2", [P, BP])
        nsum = sb("nsum", [P, 2 * BP])
        nmax = sb("nmax", [P, 2])
        nall = sb("nall", [P, 2])
        nrm = sb("nrm", [P, 2])
        m3 = sb("m3", [P, BP])
        s3 = sb("s3", [P, BP])
        r3 = sb("r3", [P, BP])
        s3p = sb("s3p", [P, BP * CB])
        m1 = sb("m1", [P, 2, H0])
        s1 = sb("s1", [P, 2, H0])
        r1 = sb("r1", [P, 2, H0])

        w1 = arena_a[:, 0:BK * E * CH].rearrange("p (e f) -> p e f", e=BK * E)
        w2 = arena_a[:, BK * E * CH:2 * BK * E * CH].rearrange("p (e k d) -> p e k d", e=BK * E, k=KF)
        ws1 = arena_b[:, 3072:3584]
        ws2 = arena_b[:, 3584:4096].rearrange("p (k d) -> p k d", k=KF)
        b1 = arena_b[:, 2048:2048 + BK * E * KF].rearrange("p (e k) -> p e k", k=KF)
        bs1 = arena_b[:, 2112:2116]
        bs2 = arena_b[:, 2116:2117]
        brt = arena_b[:, 2128:2144]
        wr = arena_b[:, 2144:2160]
        ones = arena_b[:, 2176:2304]
        tri = arena_b[:, 2304:2432]
        cr = arena_b[:, 2432:2432 + C_ROUTE]
        b2 = arena_b[:, 0:2048].rearrange("p (e d) -> p e d", e=BK * E)
        xtm = arena_b[:, 4096:8192].rearrange("p (t d) -> p t d", t=NT)
        hs = arena_b[:, 8192:12288].rearrange("p (s k c) -> p s k c", s=2, k=KF)

        def route(i):
            return arena_b[:, 12288 + i * 512:12800 + i * 512]
        lg, ex, oneh, sc_a, sc_b, tot = (route(i) for i in range(6))
        rs = arena_b[:, 15360:16384].rearrange("p (i c) -> p i c", c=TG)
        w1s = arena_b[:, 8192:9216].rearrange("p (s f) -> p s f", s=2)
        hb = arena_b[:, 9216:10240].rearrange("p (s k c) -> p s k c", s=2, k=KF)
        xb = arena_b[:, 10240:10752].rearrange("p (s d) -> p s d", s=XS)
        xbT = arena_b[:, 10752:11008].rearrange("p (s d) -> p s d", s=2)
        yb = arena_b[:, 11008:11520].rearrange("p (s d) -> p s d", s=XS)
        b1s = arena_b[:, 11520:11536].rearrange("p (s k) -> p s k", s=XS)
        ygt = arena_c[:, :].rearrange("p (t k d) -> p t k d", t=NT, k=BK)
        comb = arena_b[:, 4096:8192].rearrange("p (t d) -> p t d", t=NT)
        expert_of = arena_b[:, 2624:2704].bitcast(I32).rearrange("p (k n) -> p k n", k=BK)
        put_at = arena_b[:, 2720:2784].bitcast(I32).rearrange("p (k n) -> p k n", k=BK)
        get_at = arena_b[:, 2784:2848].bitcast(I32).rearrange("p (k n) -> p k n", k=BK)
        gate = arena_b[:, 2848:2912].rearrange("p (t k) -> p t k", k=BK)
        experts = arena_b[:, 2624:2704].bitcast(I32)
        xbuf = [nc.dram_tensor(f"xbuf{k}", [SLOTS + N, P], F32, kind="Internal") for k in range(BK)]
        ybuf = [nc.dram_tensor(f"ybuf{k}", [SLOTS, P], F32, kind="Internal") for k in range(BK)]
        zero = arena_b[:, 16000:16128]

        ab = arena_a[:, :].bitcast(BF16).rearrange("p (k u t) -> p k u t", k=2, u=RING)
        QS, KS = ab[:, 0], ab[:, 1]
        parts = [arena_b[:, o:o + 3072].bitcast(BF16).rearrange("p (k s r c) -> p k s r c", k=2, s=2, r=3) for o in (0, 12288)]

        def parts_of(k, c):
            return parts[c % 4 // 2][:, k, c % 2]
        wqkvT = arena_b[:, 3072:3456].rearrange("p (k c) -> p k c", k=3)
        bvt = arena_b[:, 3456:3584]
        mask_qk = arena_b[:, 3584:3648].bitcast(BF16)
        mask_kq = arena_b[:, 3648:3712].bitcast(BF16)
        masks = arena_c[:, 5632:5888].rearrange("p (k c) -> p k c", k=2)
        identb = arena_b[:, 3712:3776].bitcast(BF16)
        bqk = arena_b[:, 3776:3778]
        V1 = arena_b[:, 4096:4096 + NT * H1 * 32].rearrange("p (t h c) -> p t h c", t=NT, h=H1)
        O = arena_b[:, 12288:16384].rearrange("p (t h c) -> p t h c", t=NT, h=H1)
        PT = arena_c[:, 0:WR * CH].rearrange("p (s c) -> p s c", s=WR)
        OTp = arena_c[:, 6 * CH:8 * CH].rearrange("p (s c) -> p s c", s=2)
        OS = arena_c[:, 8 * CH:8 * CH + TB * 17].rearrange("p (t c) -> p t c", c=17)
        pm = arena_c[:, 4416:4544].rearrange("p (s t k) -> p s t k", s=2, k=CB)
        negm = arena_c[:, 4672:4704].rearrange("p (s t) -> p s t", s=2)
        osum = arena_c[:, 4704:4720]
        mres = arena_c[:, 4736:4864]
        mparts = arena_c[:, 4864:4864 + 384].bitcast(BF16).rearrange("p (s r c) -> p s r c", s=2, r=3)
        qk_parts = [nc.dram_tensor(f"qk_parts{k}", [3 * P, N], BF16, kind="Internal") for k in range(2)]

        f1 = arena_a[:, 0:E * CH].rearrange("p (e f) -> p e f", e=E)
        f2 = arena_a[:, 2 * E * CH:3 * E * CH].rearrange("p (e k d) -> p e k d", e=E, k=KF)
        pbc = arena_a[:, :].rearrange("p (s w e c) -> p w s e c", s=2, w=2, e=E)[:, 1]
        leafT = arena_c[0:E, 0:N]
        hid = arena_b[:, 0:HB * CH].rearrange("p (s c) -> p s c", s=HB)
        yT = arena_b[:, 3072:3072 + CH]
        yout = arena_b[:, 3584:3584 + 2 * CH].rearrange("p (s t d) -> p s t d", s=2, t=TC)
        fb1 = arena_b[:, 4608:4640].rearrange("p (e k) -> p e k", e=E)
        rwT = arena_b[:, 4640:4647]
        rbt = arena_b[:, 4648:4655]
        fb2 = arena_b[0:E, 4736:4864]
        node = arena_b[:, 4864:4864 + NT * 7].rearrange("p (t n) -> p t n", n=7)
        nodn = arena_b[:, 5120:5120 + NT * 7].rearrange("p (t n) -> p t n", n=7)
        leaf1 = arena_b[:, 5376:5376 + NT * 2].rearrange("p (t i) -> p t i", i=2)
        leaf2 = arena_b[:, 5440:5440 + NT * 4].rearrange("p (t i) -> p t i", i=4)
        leaf3 = arena_b[:, 5632:5632 + NT * 8].rearrange("p (t i) -> p t i", i=8)
        leaf_rows = nc.dram_tensor("leaf_rows", [E, N + 2 * CH], F32, kind="Internal")

        loaded, tok_loaded, loaded0, zeroed = sem("loaded"), [sem(f"tok_loaded{b}") for b in range(B)], sem("loaded0"), sem("zeroed")
        col_max, all_max, dve_step = sem("col_max"), sem("all_max"), sem("dve_step")
        onehot_ready, e_ready, e_copied = sem("onehot_ready"), sem("e_ready"), sem("e_copied")
        h_ready = sem("h_ready")
        centre_mm, xc_ready, sq_ready = sem("centre_mm"), sem("xc_ready"), sem("sq_ready")
        diag_ready, bc_ready = sem("diag_ready"), sem("bc_ready")
        var_ready, sd_ready, xn_ready = sem("var_ready"), sem("sd_ready"), sem("xn_ready")
        xl_ready, lm_ready, lm_copied = sem("xl_ready"), sem("lm_ready"), sem("lm_copied")
        fold_ready, m3_copied, m1_copied, sim2_ready = sem("fold_ready"), sem("m3_copied"), sem("m1_copied"), sem("sim2_ready")
        t2_ready, e2_ready, a_ready, at_ready, at_copied = sem("t2_ready"), sem("e2_ready"), sem("a_ready"), sem("at_ready"), sem("at_copied")
        nmax_ready, nall_ready, z_ready, zt_ready = sem("nmax_ready"), sem("nall_ready"), sem("z_ready"), sem("zt_ready")
        pinv_mm, xzt_ready, u_ready = sem("pinv_mm"), sem("xzt_ready"), sem("u_ready")
        v_ready, v_copied = sem("v_ready"), sem("v_copied")
        sim3_ready, max3_ready, exp3_ready = sem("sim3_ready"), sem("max3_ready"), sem("exp3_ready")
        p3t_ready, p3t_copied, w3_ready, w_ready = sem("p3t_ready"), sem("p3t_copied"), sem("w3_ready"), sem("w_ready")
        p3t_copied_a = sem("p3t_copied_a")
        g_mm, g_copied = sem("g_mm"), sem("g_copied")
        sim1_ready, sub1_ready, exp1_ready, p1_ready = sem("sim1_ready"), sem("sub1_ready"), sem("exp1_ready"), sem("p1_ready")
        p1t_ready, p1t_copied, o_ready, o_copied, y_ready = sem("p1t_ready"), sem("p1t_copied"), sem("o_ready"), sem("o_copied"), sem("y_ready")
        cleared, loaded1, loaded2, zero_ready = sem("cleared"), sem("loaded1"), sem("loaded2"), sem("zero_ready")
        logits_ready, lg_ready, exg_ready, oneh_ready = sem("logits_ready"), sem("lg_ready"), sem("exg_ready"), sem("oneh_ready")
        xtm_mm, xtm_copied, prefix_ready, routed = sem("xtm_mm"), sem("xtm_copied"), sem("prefix_ready"), sem("routed")
        sh_mm, sh_gelu, shy_ready, shy_added = sem("sh_mm"), sem("sh_gelu"), sem("shy_ready"), sem("shy_added")
        put, xb_loaded = [sem(f"put{k}") for k in range(BK)], [sem(f"xb_loaded{s}") for s in range(XS)]
        xbT_mm, xbT_copied, w1s_ready, hb_mm, hb_ready = sem("xbT_mm"), sem("xbT_copied"), sem("w1s_ready"), sem("hb_mm"), sem("hb_ready")
        yb_mm, yb_ready, yb_stored, blocks_clear = sem("yb_mm"), sem("yb_ready"), [sem(f"yb_stored{s}") for s in range(XS)], sem("blocks_clear")
        got0, got1 = sem("got0"), [sem(f"got1_{i}") for i in range(GG)]
        comb_ready, combT_ready = sem("comb_ready"), sem("combT_ready")
        loaded3, p1_done, r1_done, p2_done, p3_done = sem("loaded3"), sem("p1_done"), sem("r1_done"), sem("p2_done"), sem("p3_done")
        qk_mm, parts_stored, v1_mm, v1_copied = sem("qk_mm"), sem("parts_stored"), sem("v1_mm"), sem("v1_copied")
        v1_cleared, qk_scaled = sem("v1_cleared"), sem("qk_scaled")
        ones_set, stack_loaded = sem("ones_set"), [sem(f"stack_loaded{i}") for i in range(RING)]
        s1_ready, s1_read, negm_ready, mT_ready, mparts_ready = sem("s1_ready"), sem("s1_read"), sem("negm_ready"), sem("mT_ready"), sem("mparts_ready")
        mrows = [sem("mrows0"), sem("mrows1")]
        st_ready, exp_done, pv_done, ot_copied, otT_ready, otT_read = sem("st_ready"), sem("exp_done"), sem("pv_done"), sem("ot_copied"), sem("otT_ready"), sem("otT_read")
        o_done, oT_ready = sem("o_done"), sem("oT_ready")
        loaded5, node_mm, node_ready, node_sig = sem("loaded5"), sem("node_mm"), sem("node_ready"), sem("node_sig")
        leaf_ready, leafT_mm, leafT_copied, leaf_stored = sem("leaf_ready"), sem("leafT_mm"), sem("leafT_copied"), sem("leaf_stored")
        pbc_loaded = [sem("pbc_loaded0"), sem("pbc_loaded1")]
        hid_mm, gelu_done, weighed, used, yT_ready, yT_mm, yout_ready = (sem(n) for n in (
            "hid_mm", "gelu_done", "weighed", "used", "yT_ready", "yT_mm", "yout_ready"))
        yout_stored = [sem("yout_stored0"), sem("yout_stored1")]

        def pinv_count(it, stage, k):
            return 12 * it + {0: 0, 1: 4, 2: 6, 3: 8}[stage] + k + 1

        step = [0]

        def pieces_before(u, i):
            return u * sum(len(max_pieces(c)) for c in range(CB)) + sum(len(max_pieces(c)) for c in range(i))

        def tiles_before(u, i):
            return u * sum(len(exp_tiles(c)) for c in range(CB)) + sum(len(exp_tiles(c)) for c in range(i))

        def where(n):
            u, n = divmod(n, tiles_before(1, 0))
            for i in range(CB):
                if n < len(exp_tiles(i)):
                    return u, i, n
                n -= len(exp_tiles(i))

        def whole(n, s):
            return (n - s) // XS + 1 if isinstance(n, int) else n // XS + 1

        def hidden_bank(m):
            return bank[(0, 1, 2, 6)[m % 4]]

        def leaf_rows2(c):
            return leaf_rows.ap()[:, bass.ds(c * CH, CH)].partition_broadcast(P)

        blk = ctx.enter_context(nc.Block())

        @blk.sync
        def _(sp):
            sp.wait_ge(zeroed, 1)
            for dst, src in ((emb[0:VOC, :], a["emb"]), (conv2[:, :], a["conv2"]), (ident[:, :], a["c_ident"]),
                             (idk[:, :, :], a["c_idk"]), (centre[:, :], a["c_centre"]), (iota[:, :], a["c_iota"]),
                             (b_out[:, :], a["b_out"])):
                sp.dma_start(dst, src).then_inc(loaded, 16)
            for b in range(B):
                sp.dma_start(tok[:, b * T:(b + 1) * T], a["x"][b].partition_broadcast(P)).then_inc(tok_loaded[b], 16)
            for dst, src in ((wqkv, a["wqkv"]), (wqT, a["wqT"]), (wkT, a["wkT"]), (wout, a["wout"]),
                             (band, a["band"])):
                sp.dma_start(dst, src).then_inc(loaded0, 16)
            sp.wait_ge(zero_ready, 1)
            for k in range(BK):
                sp.dma_start(xbuf[k].ap()[0:SLOTS, :].rearrange("(n p) d -> p n d", p=P),
                             zero.unsqueeze(1).to_broadcast([P, NBLK, P])).then_inc(cleared, 16)
            sp.wait_ge(exp3_ready, BP * CB)
            for dst, src in ((b1, a["b1"]), (bs1, a["bs1"]), (bs2, a["bs2"]), (brt, a["brt"].partition_broadcast(P)),
                             (wr, a["wr"]), (ones, a["c_ones"]), (tri, a["c_tri"]), (cr, a["c_route"])):
                sp.dma_start(dst, src).then_inc(loaded1, 16)
            sp.wait_ge(y_ready, NC)
            for dst, src in ((ws1, a["ws1"]), (ws2, a["ws2"])):
                sp.dma_start(dst, src).then_inc(loaded0, 16)
            for dst, src in ((b2, a["b2"].partition_broadcast(P)), (w1[:, 0:E], a["w1"][:, 0:E]), (w2[:, 0:E], a["w2"][:, 0:E]),
                             (w1[:, E:], a["w1"][:, E:]), (w2[:, E:], a["w2"][:, E:])):
                sp.dma_start(dst, src).then_inc(loaded2, 16)
            sp.wait_ge(blocks_clear, 1)

            def load_rows(k, n, s):
                sp.dma_start(xb[:, s, :], xbuf[k].ap()[bass.ds(n * P, P), :]).then_inc(xb_loaded[s], 16)

            def store_rows(k, n, s):
                sp.wait_ge(yb_ready, n + (k * NBLK + 3))
                sp.dma_start(ybuf[k].ap()[bass.ds(n * P, P), :], yb[:, s, :]).then_inc(yb_stored[s], 16)
            sp.wait_ge(put[0], 16 * NT)
            for s in range(XS):
                load_rows(0, s, s)
            for k in range(BK):
                with sp.Fori(0, NBLK // XS - 1) as i:
                    for s in range(XS):
                        sp.wait_ge(xbT_mm, i * XS + (k * NBLK + s + 1))
                        load_rows(k, i * XS + (s + XS), s)
                        store_rows(k, i * XS + s, s)
                for n in range(NBLK - XS, NBLK):
                    if k + 1 < BK:
                        sp.wait_ge(put[k + 1], 16 * NT)
                        sp.wait_ge(xbT_mm, k * NBLK + n + 1)
                        load_rows(k + 1, n - (NBLK - XS), n % XS)
                    store_rows(k, n, n % XS)
            sp.wait_ge(combT_ready, NC)
            for dst, src in ((wqkvT, a["wqkvT"]), (bvt, a["bv"].partition_broadcast(P)), (masks, a["c_masks"]), (bqk, a["bqk"])):
                sp.dma_start(dst, src).then_inc(loaded3, 16)
            def load_unit(u):
                b, h, s = u // H1, u % H1, u % RING
                if u >= RING:
                    sp.wait_ge(st_ready, tiles_before(u - RING + 1, 0))
                    sp.wait_ge(s1_ready, pieces_before(u - RING + 1, 0))
                t = slice(b * T, (b + 1) * T)
                q = qk_parts[0].ap().rearrange("(r h f) t -> r h f t", r=3, f=D1)
                k = qk_parts[1].ap().rearrange("(r h f) t -> r h f t", r=3, f=D1)
                for dst, r0, src in ((QS, 0, q[0, h, :, t].unsqueeze(0).to_broadcast([3, D1, T])),
                                     (QS, 3, q[1, h, :, t].unsqueeze(0).to_broadcast([2, D1, T])),
                                     (QS, 5, q[2, h, :, t]),
                                     (KS, 0, k[:, h, :, t]), (KS, 3, k[0:2, h, :, t]), (KS, 5, k[0, h, :, t])):
                    rows = (3, 0, 0, 2, 0, 1)[r0]
                    sp.dma_start(dst[r0 * D1:(r0 + rows) * D1, s, :], src).then_inc(stack_loaded[s], 16)

            for c in range(NC):
                for k in range(2):
                    sp.wait_ge(p3_done, 2 * c + k + 1)
                    sp.dma_start(qk_parts[k].ap()[:, c * CH:(c + 1) * CH].rearrange("(r p) c -> p r c", r=3),
                                 parts_of(k, c)).then_inc(parts_stored, 16)
                if c == CB - 1:
                    sp.wait_ge(parts_stored, 32 * CB)
                if c >= CB - 1:
                    load_unit(c - (CB - 1))
            sp.wait_ge(parts_stored, 32 * NC)
            for u in range(CB + 1, RING):
                load_unit(u)

            def row_of_maxima(u):
                sp.wait_ge(mparts_ready, u + 1)
                for r in range(3):
                    sp.dma_start(QS[KS_ROWS + r:KS_ROWS + r + 1, u % RING, :],
                                 mparts[0:TB, u % 2, r, :]).then_inc(mrows[u % 2], 16)
            for u in range(UN):
                row_of_maxima(u)
                if RING <= u + 4 < UN:
                    load_unit(u + 4)
                if u == UN - 1:
                    sp.wait_ge(st_ready, tiles_before(UN - RING // 2, 0))
                    for dst, src in ((f1, a["f1"]), (f2, a["f2"])):
                        sp.dma_start(dst, src).then_inc(loaded5, 16)
            sp.wait_ge(oT_ready, NC)
            for dst, src in ((fb1, a["fb1"]), (rwT, a["rwT"]), (rbt, a["rb"].partition_broadcast(P)), (fb2, a["fb2"])):
                sp.dma_start(dst, src).then_inc(loaded3, 16)
            sp.wait_ge(leafT_copied, 1)
            sp.dma_start(leaf_rows.ap()[:, 0:CH], leafT[:, 0:CH]).then_inc(leaf_stored, 16)
            sp.wait_ge(leaf_stored, 16)

            def load_weights(c, s):
                sp.dma_start(pbc[:, s], leaf_rows.ap()[:, bass.ds(c * CH, CH)].partition_broadcast(P)).then_inc(pbc_loaded[s], 16)
            load_weights(0, 0)
            sp.wait_ge(leafT_copied, NC)
            sp.dma_start(leaf_rows.ap()[:, CH:N], leafT[:, CH:N]).then_inc(leaf_stored, 16)
            sp.dma_start(leaf_rows.ap()[:, N:N + 2 * CH], leafT[:, 0:2 * CH]).then_inc(leaf_stored, 16)
            sp.wait_ge(leaf_stored, 48)
            load_weights(1, 1)
            with sp.Fori(0, NC // 2) as i:
                for s in range(2):
                    sp.wait_ge(yout_ready, i * 2 + (s + 2))
                    sp.dma_start(a["out"].rearrange("(c t p) d -> c p t d", t=TC, p=P)[bass.ds(i * 2 + s, 1)].rearrange("c p t d -> (c p) t d"),
                                 yout[:, s]).then_inc(yout_stored[s], 16)
                    if s == 0:
                        sp.wait_ge(weighed, (i * 2 + 1) * HK)
                        sp.dma_start(pbc[:, 0], leaf_rows2(i * 2 + 2)).then_inc(pbc_loaded[0], 16)
                    else:
                        sp.wait_ge(weighed, (i * 2 + 2) * HK)
                        sp.dma_start(pbc[:, 1], leaf_rows2(i * 2 + 3)).then_inc(pbc_loaded[1], 16)
            for s in range(2):
                sp.wait_ge(yout_stored[s], 16 * (NC // 2 + 1))
                sp.wait_ge(pbc_loaded[s], 16 * (NC // 2 + 1))

        def centre_bank(n, c):
            return bank[(6, 0, 0, 6)[n] + c % 2]

        def norm_pe(pe, n, first=0, last=NC + 2):
            for c in range(first, last):
                i = n * NC + c
                if c < NC:
                    pe.wait_ge(h_ready, i + 1)
                    if i >= 2:
                        pe.wait_ge(xc_ready, i - 1)
                    nc.tensor.matmul(centre_bank(n, c), centre[:, :], hT[:, c * CH:(c + 1) * CH],
                                     start=True, stop=True).then_inc(centre_mm, 1)
                if 1 <= c <= NC:
                    pe.wait_ge(sq_ready, i)
                    if i > 2:
                        pe.wait_ge(sd_ready, i - 2)
                    for t in range(TC):
                        done = nc.tensor.matmul(bank[2 + (c - 1) % 2][:, t:t + 1], ln_sq[:, (c - 1) % 2, t * P:(t + 1) * P],
                                                mean_col[:, :], start=True, stop=True)
                    done.then_inc(var_ready, 1)
                if c >= 2:
                    pe.wait_ge(diag_ready, i - 1)
                    if i > 3:
                        pe.wait_ge(xn_ready, i - 3)
                    nc.tensor.matmul(bank[4 + c % 2][:, :], ones_w[:, :], ln_xc[:, c % 2, :],
                                     start=True, stop=True).then_inc(bc_ready, 1)

        def norm_act(act, n, first=0, last=NC + 1):
            for c in range(first, last):
                i = n * NC + c
                if c < NC:
                    act.wait_ge(centre_mm, i + 1)
                    if i >= 2:
                        act.wait_ge(var_ready, i - 1)
                    nc.scalar.activation(ln_sq[:, c % 2, :], centre_bank(n, c), ACT.Square).then_inc(sq_ready, 1)
                    nc.scalar.copy(xnT[:, c * CH:(c + 1) * CH], centre_bank(n, c)).then_inc(xc_ready, 1)
                if c > 0:
                    act.wait_ge(var_ready, i)
                    if i > 2:
                        act.wait_ge(diag_ready, i - 2)
                    nc.scalar.activation(ln_sd[:, (c - 1) % 2, :], bank[2 + (c - 1) % 2][:, 0:TC], ACT.Sqrt,
                                         bias=eps[:, :]).then_inc(sd_ready, 1)

        def norm_dve(dve, n, first=0, last=NC + 1):
            for c in range(first, last):
                i = n * NC + c
                if c < NC:
                    s = c % 2
                    dve.wait_ge(sd_ready, i + 1)
                    nc.vector.reciprocal(ln_sd[:, s, :], ln_sd[:, s, :]).then_inc(dve_step, 1)
                    step[0] += 1
                    dve.wait_ge(dve_step, step[0])
                    if i >= 2:
                        dve.wait_ge(bc_ready, i - 1)
                    nc.vector.tensor_tensor(ln_xc[:, s, :].rearrange("p (t c) -> p t c", t=TC),
                                            ident[:, :].unsqueeze(1).to_broadcast([P, TC, P]),
                                            ln_sd[:, s, :].unsqueeze(2).to_broadcast([P, TC, P]), ALU.mult).then_inc(diag_ready, 1)
                if c > 0:
                    x = xnT[:, (c - 1) * CH:c * CH]
                    dve.wait_ge(bc_ready, i)
                    dve.wait_ge(xc_ready, i)
                    nc.vector.tensor_tensor(x, x, bank[4 + (c - 1) % 2][:, :], ALU.mult).then_inc(xn_ready, 1)
                    if n == 0:
                        dve.wait_ge(xn_ready, c)
                        w = CH // LM
                        nc.vector.tensor_reduce(xl[:, (c - 1) * w:c * w], x.rearrange("p (m l) -> p m l", l=LM), X,
                                                ALU.add).then_inc(xl_ready, 1)

        step = [0]

        @blk.vector
        def _(dve):
            def then(ins):
                ins.then_inc(dve_step, 1)
                step[0] += 1
                dve.wait_ge(dve_step, step[0])

            nc.vector.memset(emb, 0.0).then_inc(zeroed, 1)
            nc.vector.memset(eps[:, :], EPS)
            nc.vector.memset(mean_col[:, :], 1.0 / P)
            nc.vector.memset(ones_w[:, :], 1.0)
            nc.vector.memset(zero, 0.0).then_inc(zero_ready, 1)
            nc.vector.memset(eT[:, :, 0:1], 0.0)
            dve.wait_ge(loaded, 16 * 7)
            nc.vector.tensor_reduce(qcol[:, 0:1], emb, X, ALU.max, apply_absolute_value=True)
            nc.vector.tensor_reduce(qcol[:, 1:2], conv2[:, :], X, ALU.max, apply_absolute_value=True).then_inc(col_max, 1)
            dve.wait_ge(all_max, 1)
            then(nc.vector.tensor_scalar(qcol[:, 4:6], qcol[:, 2:4], 1.0 / 127.0, None, ALU.mult))
            then(nc.vector.reciprocal(qcol[:, 6:8], qcol[:, 4:6]))
            for w, q, e, k in ((emb, emb_q, emb_e, 0), (conv2[:, :], ln_sq[:, 0, 0:2], ln_sq[:, 0, 2:4], 1)):
                then(nc.vector.tensor_scalar(q, w, qcol[:, 6 + k:7 + k], MAGIC, ALU.mult, ALU.add))
                then(nc.vector.tensor_scalar(q, q, MAGIC, qcol[:, 4 + k:5 + k], ALU.subtract, ALU.mult))
                then(nc.vector.tensor_tensor(e, q, w, ALU.subtract))
                then(nc.vector.tensor_tensor(e, e, w, ALU.add))
            then(nc.vector.tensor_copy(conv2[:, :], ln_sq[:, 0, 2:4]))
            for c in range(NC + 1):
                if c < NC:
                    dve.wait_ge(tok_loaded[c // CB], 16)
                    if c >= 2:
                        dve.wait_ge(e_ready, c - 1)
                    nc.vector.tensor_scalar(onehot[:, c % 2, :], tok[:, c * CH:(c + 1) * CH], float(VOC - 1), iota[:, :],
                                            ALU.min, ALU.is_equal).then_inc(onehot_ready, 1)
                if c > 0:
                    k = c - 1
                    b, t0 = k // CB, (k % CB) * CH
                    dve.wait_ge(e_copied, c)
                    then(nc.vector.scalar_tensor_tensor(tmp[:, k % 2, :], eT[:, b, t0:t0 + CH], conv2[:, 0:1], tmp[:, k % 2, :],
                                                        ALU.mult, ALU.add))
                    nc.vector.tensor_scalar(hT[:, k * CH:(k + 1) * CH], tmp[:, k % 2, :], 0.0, None, ALU.max).then_inc(h_ready, 1)
                if c >= DL0:
                    norm_dve(dve, 0, c - DL0, c - DL0 + 1)
            norm_dve(dve, 0, NC - DL0 + 1)

            for t in (QL, KL, A):
                last = nc.vector.memset(t, 0.0)
            then(last)
            dve.wait_ge(lm_ready, 1)
            for t, k, s in ((QL, 0, 0.125 / LM), (KL, 1, 1.0 / LM)):
                for j in range(2):
                    r = slice(64 * j, 64 * j + 64)
                    for b in range(B):
                        nc.vector.tensor_scalar(t[r, b * PR:(b + 1) * PR, r],
                                                bank[k][r, :].rearrange("p (g b m) -> p b g m", g=PR, b=B)[:, b],
                                                s, None, ALU.mult).then_inc(lm_copied, 1)
            dve.wait_ge(sim2_ready, 1)
            sim2 = [[bank[6 + k][64 * j:64 * j + 64, :].rearrange("p (g c) -> p g c", g=PR)[:, :, 64 * j:64 * j + 64]
                     for j in range(2)] for k in range(2)]
            for k in range(2):
                for j in range(2):
                    r = slice(64 * j, 64 * j + 64)
                    last = nc.vector.tensor_reduce(mx2[r, k * PR:(k + 1) * PR], sim2[k][j], X, ALU.max)
            then(last)
            for k in range(2):
                for j in range(2):
                    r = slice(64 * j, 64 * j + 64)
                    last = nc.vector.tensor_tensor(T2[r, k * PR:(k + 1) * PR, :], sim2[k][j],
                                                   mx2[r, k * PR:(k + 1) * PR].unsqueeze(2).to_broadcast([64, PR, 64]), ALU.subtract)
            last.then_inc(t2_ready, 1)
            dve.wait_ge(e2_ready, 1)
            then(nc.vector.tensor_reduce(s2[:, :], T2, X, ALU.add))
            then(nc.vector.reciprocal(r2[:, :], s2[:, :]))
            for j in range(2):
                r = slice(64 * j, 64 * j + 64)
                last = nc.vector.tensor_tensor(A[r, :, r], T2[r, :, :], r2[r, :].unsqueeze(2).to_broadcast([64, BP, 64]), ALU.mult)
            last.then_inc(a_ready, 1)
            dve.wait_ge(a_ready, 1)
            nc.vector.tensor_reduce(nsum[:, 0:BP], A, X, ALU.add, apply_absolute_value=True)
            dve.wait_ge(at_copied, 2)
            then(nc.vector.tensor_reduce(nsum[:, BP:2 * BP], AT, X, ALU.add, apply_absolute_value=True))
            nc.vector.tensor_reduce(nmax[:, :], nsum[:, :].rearrange("p (k g) -> p k g", k=2), X, ALU.max).then_inc(nmax_ready, 1)
            dve.wait_ge(nall_ready, 1)
            then(nc.vector.tensor_tensor(nrm[:, 0:1], nall[:, 0:1], nall[:, 1:2], ALU.mult))
            then(nc.vector.reciprocal(nrm[:, 1:2], nrm[:, 0:1]))
            for k in range(2):
                g = slice(k * PR, (k + 1) * PR)
                nc.vector.tensor_scalar(Z[0][:, g, :], AT[:, g, :], nrm[:, 1:2], None, ALU.mult).then_inc(z_ready, 1)
                nc.vector.tensor_scalar(ZT[0][:, g, :], A[:, g, :], nrm[:, 1:2], None, ALU.mult).then_inc(zt_ready, 1)
            for it in range(ITERS):
                for stage in range(3):
                    for k in range(2):
                        g = slice(k * PR, (k + 1) * PR)
                        dve.wait_ge(pinv_mm, pinv_count(it, stage, k))
                        src = bank[[0, 4, 0][stage] + k][:, :].rearrange("p (g c) -> p g c", g=PR)
                        nc.vector.scalar_tensor_tensor(U[:, g, :], src, -1.0,
                                                       idk[:, stage, :].unsqueeze(1).to_broadcast([P, PR, P]),
                                                       ALU.mult, ALU.add).then_inc(u_ready, 1)
                for k in range(2):
                    g = slice(k * PR, (k + 1) * PR)
                    dve.wait_ge(pinv_mm, pinv_count(it, 3, k))
                    src = bank[4 + k][:, :].rearrange("p (g c) -> p g c", g=PR)
                    nc.vector.tensor_scalar(Z[(it + 1) % 2][:, g, :], src, 0.25, None, ALU.mult).then_inc(z_ready, 1)
            then(nc.vector.memset(W, 0.0))
            for i in range(BP + 2):
                if i < BP:
                    for c in range(CB):
                        dve.wait_ge(sim3_ready, i * CB + c + 1)
                        last = nc.vector.tensor_reduce(ln_sq[:, 0, c:c + 1], bank[c][:, :], X, ALU.max)
                    then(last)
                    nc.vector.tensor_reduce(m3[:, i:i + 1], ln_sq[:, 0, 0:CB], X, ALU.max, negate=True).then_inc(max3_ready, 1)
                if 1 <= i <= BP:
                    k = i - 1
                    if k >= 2:
                        dve.wait_ge(w3_ready, k - 1)
                    for q in (1, 3):
                        dve.wait_ge(p3t_ready, 4 * k + q + 1)
                        nc.vector.tensor_copy(P3T[:, k % 2, 4 * q:4 * q + 4, :],
                                              bank[4 + q % 2][:, :].rearrange("p (t c) -> p t c", t=4)).then_inc(p3t_copied, 1)
                if i >= 2:
                    k = i - 2
                    dve.wait_ge(exp3_ready, CB * (k + 1))
                    then(nc.vector.tensor_reduce(s3[:, k:k + 1], s3p[:, k * CB:(k + 1) * CB], X, ALU.add))
                    then(nc.vector.reciprocal(r3[:, k:k + 1], s3[:, k:k + 1]))
                    dve.wait_ge(w3_ready, k + 1)
                    for j in range(2):
                        r = slice(64 * j, 64 * j + 64)
                        last = nc.vector.tensor_scalar(W[r, k, r], bank[6 + k % 2][r, r], r3[r, k:k + 1], None, ALU.mult)
                    last.then_inc(w_ready, 1)
            for k in range(2):
                dve.wait_ge(g_mm, k + 1)
                nc.vector.tensor_copy(G[:, k * PR:(k + 1) * PR, :],
                                      bank[6 + k][:, :].rearrange("p (g c) -> p g c", g=PR)).then_inc(g_copied, 1)
            def soft1(t):
                s = t % 2
                sim = bank[s][:, :].rearrange("p (h m) -> p h m", h=H0)
                dve.wait_ge(sim1_ready, t + 1)
                then(nc.vector.tensor_reduce(m1[:, s, :], sim, X, ALU.max))
                if t >= 2:
                    dve.wait_ge(p1t_ready, t - 1)
                nc.vector.tensor_tensor(P1[:, s], sim, m1[:, s, :].unsqueeze(2).to_broadcast([P, H0, M]),
                                        ALU.subtract).then_inc(sub1_ready, 1)

            def norm1(t):
                s = t % 2
                dve.wait_ge(exp1_ready, t + 1)
                then(nc.vector.tensor_reduce(s1[:, s, :], P1[:, s], X, ALU.add))
                then(nc.vector.reciprocal(r1[:, s, :], s1[:, s, :]))
                nc.vector.tensor_tensor(P1[:, s], P1[:, s], r1[:, s, :].unsqueeze(2).to_broadcast([P, H0, M]),
                                        ALU.mult).then_inc(p1_ready, 1)

            def add0(c):
                dve.wait_ge(y_ready, c + 1)
                nc.vector.scalar_tensor_tensor(hT[:, c * CH:(c + 1) * CH], bank[7][:, :], b_out[:, 0:1],
                                               hT[:, c * CH:(c + 1) * CH], ALU.add, ALU.add).then_inc(h_ready, 1)
            for t in range(STEPS1 + 1):
                if t < NT:
                    soft1(t)
                if 1 <= t <= NT:
                    norm1(t - 1)
                c, g = divmod(t - OUT_LAG - 1, PR)
                if c >= 1 and g == 0:
                    add0(c - 1)
            norm_dve(dve, 1)
            lg3 = lg.rearrange("p (g e) -> p g e", e=E)
            ex3 = ex.rearrange("p (g e) -> p g e", e=E)
            oneh3 = oneh.rearrange("p (g e) -> p g e", e=E)

            shared = [0]

            def share():
                c = shared[0]
                dve.wait_ge(shy_ready, c + 1)
                nc.vector.scalar_tensor_tensor(hT[:, c * CH:(c + 1) * CH], bank[5][:, :], bs2, hT[:, c * CH:(c + 1) * CH],
                                               ALU.add, ALU.add).then_inc(shy_added, 1)
                shared[0] += 1

            def wide(ap, n=TG):
                return ap.unsqueeze(2).to_broadcast([P, n, E])

            def const(lo, n):
                return cr[:, lo:lo + n]
            mx, cand, esum, ginv, pos, base, slot, keep, dst = (rs[:, i, :] for i in range(9))
            nb, sbk, ends = rs[:, 9, 0:16], rs[:, 10, 0:16], rs[:, 11, 0:16]
            dve.wait_ge(loaded1, 16 * 8)
            dve.wait_ge(cleared, 16 * BK)
            dve.wait_ge(logits_ready, 1)
            then(nc.vector.tensor_tensor(lg.rearrange("p (t c) -> p t c", t=NT), bank[7][:, :].rearrange("p (t c) -> p t c", t=NT),
                                         brt.unsqueeze(1).to_broadcast([P, NT, BK * E]), ALU.add))
            then(nc.vector.tensor_reduce(mx, lg3, X, ALU.max))
            nc.vector.tensor_tensor(lg3, lg3, wide(mx), ALU.subtract).then_inc(lg_ready, 1)
            dve.wait_ge(lg_ready, 1)
            then(nc.vector.tensor_scalar(oneh, lg, 0.0, None, ALU.is_equal))
            then(nc.vector.scalar_tensor_tensor(oneh3, oneh3, -float(E), const(C_IOTA8, E).unsqueeze(1).to_broadcast([P, TG, E]),
                                                ALU.mult, ALU.add))
            then(nc.vector.tensor_reduce(cand, oneh3, X, ALU.min))
            then(nc.vector.tensor_scalar(cand, cand, float(E), None, ALU.add))
            nc.vector.tensor_tensor(oneh3, const(C_IOTA8, E).unsqueeze(1).to_broadcast([P, TG, E]), wide(cand),
                                    ALU.is_equal).then_inc(oneh_ready, 1)
            dve.wait_ge(exg_ready, 1)
            then(nc.vector.tensor_reduce(esum, ex3, X, ALU.add))
            then(nc.vector.reciprocal(ginv, esum))
            dve.wait_ge(prefix_ready, 2)
            then(nc.vector.tensor_copy(sc_a, bank[7][:, :]))
            then(nc.vector.tensor_copy(tot, sc_a))
            src, dstb, w = sc_a, sc_b, BK * E
            for n in (1, 2, 4, 8, 16):
                nc.vector.tensor_copy(dstb[:, 0:n * w], src[:, 0:n * w])
                then(nc.vector.tensor_tensor(dstb[:, n * w:], src[:, n * w:], src[:, 0:(NT - n) * w], ALU.add))
                src, dstb = dstb, src
            incl = src
            share()
            total = incl[:, (NT - 1) * w:NT * w]
            cmp = ex[:, 0:160].rearrange("p (e j) -> p e j", j=CAP // P)
            then(nc.vector.tensor_tensor(cmp, total.unsqueeze(2).to_broadcast([P, w, CAP // P]),
                                         const(C_J128, CAP // P).unsqueeze(1).to_broadcast([P, w, CAP // P]), ALU.is_gt))
            then(nc.vector.tensor_reduce(nb, cmp, X, ALU.add))
            for k in range(BK):
                last = nc.vector.tensor_tensor(ex[:, 192 + k * 64:256 + k * 64].rearrange("p (e f) -> p e f", f=E),
                                               nb[:, k * E:(k + 1) * E].unsqueeze(1).to_broadcast([P, E, E]),
                                               const(C_LT, 64).rearrange("p (e f) -> p e f", f=E), ALU.mult)
            then(last)
            then(nc.vector.tensor_reduce(sbk, ex[:, 192:320].rearrange("p (e f) -> p e f", f=E), X, ALU.add))
            then(nc.vector.tensor_tensor(ends, sbk, nb, ALU.add))
            share()
            then(nc.vector.tensor_tensor(incl, incl, tot, ALU.subtract))
            then(nc.vector.tensor_tensor(incl, incl, bank[6][:, :], ALU.add))
            then(nc.vector.tensor_tensor(incl, incl, oneh, ALU.mult))
            then(nc.vector.tensor_reduce(pos, incl.rearrange("p (g e) -> p g e", e=E), X, ALU.add))
            then(nc.vector.tensor_tensor(tot.rearrange("p (t c) -> p t c", t=NT), oneh.rearrange("p (t c) -> p t c", t=NT),
                                         sbk.unsqueeze(1).to_broadcast([P, NT, w]), ALU.mult))
            then(nc.vector.tensor_reduce(base, tot.rearrange("p (g e) -> p g e", e=E), X, ALU.add))
            then(nc.vector.scalar_tensor_tensor(slot, base, float(P), pos, ALU.mult, ALU.add))
            then(nc.vector.tensor_scalar(keep, pos, float(CAP), None, ALU.is_lt))
            share()
            then(nc.vector.tensor_tensor(gate.rearrange("p t k -> p (t k)"), ginv, keep, ALU.mult))
            trash = const(C_TRASH, NT).unsqueeze(2).to_broadcast([P, NT, BK])

            def tk(ap):
                return ap.rearrange("p (t k) -> p t k", k=BK)
            then(nc.vector.tensor_tensor(tk(dst), tk(slot), trash, ALU.subtract))
            then(nc.vector.tensor_tensor(dst, dst, keep, ALU.mult))
            then(nc.vector.tensor_tensor(tk(dst), tk(dst), trash, ALU.add))
            for k in range(BK):
                last = nc.vector.tensor_copy(put_at[:, k, :], tk(dst)[:, :, k])
            last.then_inc(routed, 1)
            for k in range(BK):
                nc.vector.tensor_scalar(get_at[:, k, :], tk(dst)[:, :, k], float(SLOTS - 1), None, ALU.min)
            for k in range(BK):
                e4 = ex[:, 0:NBLK * E].rearrange("p (n e) -> p n e", e=E)
                then(nc.vector.tensor_tensor(e4, const(C_IOTAB, NBLK).unsqueeze(2).to_broadcast([P, NBLK, E]),
                                             ends[:, k * E:(k + 1) * E].unsqueeze(1).to_broadcast([P, NBLK, E]), ALU.is_ge))
                then(nc.vector.tensor_reduce(incl[:, 0:NBLK], e4, X, ALU.add))
                then(nc.vector.tensor_scalar(expert_of[:, k, :], incl[:, 0:NBLK], float(E - 1), float(k * E), ALU.min, ALU.add))
            for c in range(shared[0], NC):
                share()
            dve.wait_ge(loaded2, 16 * 5)

            def prepare(n, s):
                e = dve.value_load(experts[0:1, bass.ds(n, 1)], min_val=0, max_val=BK * E - 1)
                nc.vector.tensor_copy(w1s[:, s % 2, :], w1[:, bass.ds(e, 1), :].rearrange("p e f -> p (e f)"))
                nc.vector.tensor_copy(b1s[:, s, :], b1[:, bass.ds(e, 1), :].rearrange("p e f -> p (e f)")).then_inc(w1s_ready, 1)
                dve.wait_ge(xbT_mm, n + 1)
                nc.vector.tensor_copy(xbT[:, s % 2, :], bank[s % 2][:, 0:P]).then_inc(xbT_copied, 1)

            def finish(n, s):
                e = dve.value_load(experts[0:1, bass.ds(n, 1)], min_val=0, max_val=BK * E - 1)
                dve.wait_ge(yb_mm, n + 3)
                dve.wait_ge(yb_stored[s], whole(n, s) * 16)
                nc.vector.tensor_tensor(yb[:, s, :], bank[4 + s % 2][:, 0:P], b2[:, bass.ds(e, 1), :].rearrange("p e f -> p (e f)"),
                                        ALU.add).then_inc(yb_ready, 1)
            prepare(0, 0)
            prepare(1, 1)

            def step_dve(n, s, more=True):
                if more:
                    dve.wait_ge(hb_mm, n + 1)
                    prepare(n + 2, (s + 2) % XS)
                finish(n, s)
            with dve.Fori(0, ALLB // XS - 1) as i:
                for s in range(XS):
                    step_dve(i * XS + s, s)
            for n in range(ALLB - XS, ALLB):
                step_dve(n, n % XS, n + 2 < ALLB)
            def addc(c):
                dve.wait_ge(combT_ready, c + 1)
                nc.vector.tensor_tensor(hT[:, c * CH:(c + 1) * CH], bank[6 + c % 2][:, :], hT[:, c * CH:(c + 1) * CH],
                                        ALU.add).then_inc(h_ready, 1)
                if c >= DL:
                    norm_dve(dve, 2, c - DL, c - DL + 1)
            dve.wait_ge(got0, 16 * NT)
            for c in range(NC):
                ts = slice(TC * c, TC * (c + 1))
                last = nc.vector.tensor_tensor(comb[:, ts, :], ygt[:, ts, 0, :], gate[:, ts, 0:1].to_broadcast([P, TC, P]), ALU.mult)
            then(last)
            for t in range(NT):
                dve.wait_ge(got1[t // (NT // GG)], 16 * NT // GG)
                nc.vector.scalar_tensor_tensor(comb[:, t, :], ygt[:, t, 1, :], gate[:, t, 1:2], comb[:, t, :],
                                               ALU.mult, ALU.add).then_inc(comb_ready, 1)
                if t % TC == TC - 1 and t > TC:
                    addc(t // TC - 1)
            addc(NC - 1)
            norm_dve(dve, 2, NC - DL)
            dve.wait_ge(loaded3, 16 * 4)
            nc.vector.tensor_scalar(wqkvT[:, 0, :], wqkvT[:, 0, :], 0.25, None, ALU.mult)
            then(nc.vector.tensor_scalar(bqk[:, 0:1], bqk[:, 0:1], 0.25, None, ALU.mult))
            for dst, src in ((mask_qk, masks[:, 0, :]), (mask_kq, masks[:, 1, :]), (identb, ident[:, :])):
                nc.vector.tensor_copy(dst, src)
            nc.vector.memset(pm, -3.0e38).then_inc(qk_scaled, 1)
            for c in range(NC):
                for k in range(2):
                    n = 2 * c + k
                    dve.wait_ge(p1_done, n + 1)
                    if n >= 2:
                        dve.wait_ge(p3_done, n - 1)
                    nc.vector.scalar_tensor_tensor(ln_sq[:, k, :], bank[2 * k + c % 2], bqk[:, k:k + 1], parts_of(k, c)[:, 0, :],
                                                   ALU.add, ALU.subtract).then_inc(r1_done, 1)
                dve.wait_ge(v1_mm, c + 1)
                dve.wait_ge(v1_cleared, 2)
                nc.vector.tensor_tensor(V1[:, TC * c:TC * c + TC, :, 0:D1],
                                        bank[4 + c % 2][:, :].rearrange("p (t h c) -> p t h c", t=TC, h=H1),
                                        bvt.rearrange("p (h c) -> p h c", h=H1).unsqueeze(1).to_broadcast([P, TC, H1, D1]),
                                        ALU.add).then_inc(v1_copied, 1)

            def left_over(u, i):
                if u >= 0:
                    m = u * CB + i
                    dve.wait_ge(otT_ready, m + 1)
                    if i == 0 and u > 0:
                        dve.wait_ge(o_done, u)
                    if i == 0:
                        ins = nc.vector.tensor_copy(OS[:, 0:TC, :], bank[6].rearrange("p (t g c) -> p t g c", t=TC, g=4)[:, :, 0, 0:17])
                    else:
                        ins = nc.vector.tensor_reduce(OS[:, TC * i:TC * i + TC, :],
                                                  bank[6 + m % 2].rearrange("p (t g c) -> p t c g", t=TC, g=4)[:, :, 0:17, :], X, ALU.add)
                    ins.then_inc(otT_read, 1)
                    if i == CB - 1:
                        dve.wait_ge(otT_read, m + 1)
                        then(nc.vector.reciprocal(osum, OS[:, :, 16]))
                        b, h = u // H1, u % H1
                        nc.vector.tensor_tensor(O[:, b * TB:(b + 1) * TB, h, :], OS[:, :, 0:D1],
                                                osum.unsqueeze(2).to_broadcast([P, TB, D1]), ALU.mult).then_inc(o_done, 1)
                if i == CB - 1 and u + LEAD < UN:
                    v = u + LEAD
                    dve.wait_ge(mT_ready, v + 1)
                    if v >= 2:
                        dve.wait_ge(mrows[v % 2], 48 * (v // 2))
                    mt = bank[7][0:TB, 0:P]
                    mp = mparts[0:TB, v % 2]
                    then(nc.vector.tensor_copy(mp[:, 0, :], mt))
                    then(nc.vector.tensor_tensor(mres[0:TB, :], mt, mp[:, 0, :], ALU.subtract))
                    then(nc.vector.tensor_copy(mp[:, 1, :], mres[0:TB, :]))
                    nc.vector.tensor_tensor(mp[:, 2, :], mres[0:TB, :], mp[:, 1, :], ALU.subtract).then_inc(mparts_ready, 1)

            before = None
            for u, i in STEPS:
                items = step_items(u, i)
                seen = 0
                if before and maxima_before(items) == 0:
                    left_over(*before)
                for kind, x in items:
                    if kind == "max":
                        qt, s, w = x
                        v = u + LEAD
                        n = pieces_before(v, i) + seen
                        dve.wait_ge(s1_ready, n + 1)
                        if v >= 2:
                            dve.wait_ge(negm_ready, v - 1)
                        nc.vector.tensor_reduce(pm[:, v % 2, qt, s:s + 1], bank[n % SB][:, 0:w], X, ALU.max).then_inc(s1_read, 1)
                        seen += 1
                        if before and seen == maxima_before(items):
                            left_over(*before)
                if i == CB - 1 and u + LEAD < UN:
                    v = u + LEAD
                    dve.wait_ge(s1_read, pieces_before(v + 1, 0))
                    if v >= 2:
                        dve.wait_ge(mT_ready, v - 1)
                    nc.vector.tensor_reduce(negm[:, v % 2, :], pm[:, v % 2], X, ALU.max, negate=True).then_inc(negm_ready, 1)
                before = (u, i)
            left_over(*before)
            for c in range(NC):
                dve.wait_ge(oT_ready, c + 1)
                nc.vector.tensor_tensor(hT[:, c * CH:(c + 1) * CH], bank[c % 2][:, :], hT[:, c * CH:(c + 1) * CH],
                                        ALU.add).then_inc(h_ready, 1)
                if c >= DL:
                    norm_dve(dve, 3, c - DL, c - DL + 1)
            norm_dve(dve, 3, NC - DL)
            dve.wait_ge(loaded3, 16 * (4 + 4))
            dve.wait_ge(node_mm, 1)
            nc.vector.tensor_tensor(node, bank[0][:, 0:NT * 8].rearrange("p (t n) -> p t n", n=8)[:, :, 0:7],
                                    rbt.unsqueeze(1).to_broadcast([P, NT, 7]), ALU.add).then_inc(node_ready, 1)
            dve.wait_ge(node_sig, 1)
            then(nc.vector.tensor_scalar(nodn, node, -1.0, 1.0, ALU.mult, ALU.add))
            nc.vector.tensor_copy(leaf1[:, :, 0:1], nodn[:, :, 0:1])
            then(nc.vector.tensor_copy(leaf1[:, :, 1:2], node[:, :, 0:1]))
            for lo, up, first, n in ((leaf1, leaf2, 1, 2), (leaf2, leaf3, 3, 4)):
                up = up.rearrange("p t (i s) -> p t i s", s=2)
                nc.vector.tensor_tensor(up[:, :, :, 0], lo, nodn[:, :, first:first + n], ALU.mult)
                last = nc.vector.tensor_tensor(up[:, :, :, 1], lo, node[:, :, first:first + n], ALU.mult)
                if n == 2:
                    then(last)
            last.then_inc(leaf_ready, 1)
            for c in range(NC):
                dve.wait_ge(leafT_mm, c + 1)
                nc.vector.tensor_copy(leafT[:, c * CH:(c + 1) * CH], bank[1 + c % 2][0:E, :]).then_inc(leafT_copied, 1)
            with dve.Fori(0, NC // 2) as i:
                for s in range(2):
                    dve.wait_ge(pbc_loaded[s], (i + 1) * 16)
                    for k in range(HK):
                        n = i * (2 * HK) + (s * HK + k)
                        dve.wait_ge(gelu_done, n + (1 + 4))
                        h = hid[:, (s * HK + k) % HB, :]
                        nc.vector.tensor_tensor(h, h, pbc[:, s, k // KF, :], ALU.mult).then_inc(weighed, 1)
                    dve.wait_ge(used, i * (2 * HK) + ((s + 1) * HK + HB))
                    dve.wait_ge(yT_mm, i * 2 + (s + 1))
                    nc.vector.tensor_tensor(yT, bank[3 + s], hT[:, bass.ds((i * 2 + s) * CH, CH)], ALU.add).then_inc(yT_ready, 1)

        def ot_copy(act, u, i):
            m = u * CB + i
            act.wait_ge(pv_done, tiles_before(u, i + 1))
            if m >= 2:
                act.wait_ge(otT_ready, m - 1)
            rows = 32 if i == 0 else P
            nc.scalar.copy(OTp[0:rows, m % 2, :], bank[6 + m % 2][0:rows, :]).then_inc(ot_copied, 1)

        @blk.scalar
        def _(act):
            for c in range(NC):
                b, t0 = c // CB, (c % CB) * CH
                act.wait_ge(e_ready, c + 1)
                if c >= 2:
                    act.wait_ge(h_ready, c - 1)
                nc.scalar.activation(tmp[:, c % 2, :], bank[c % 2][:, :], ACT.Copy, scale=conv2[:, 1:2])
                nc.scalar.copy(eT[:, b, 1 + t0:1 + t0 + CH], bank[c % 2][:, :]).then_inc(e_copied, 1)
                if c >= PL0:
                    norm_act(act, 0, c - PL0, c - PL0 + 1)
            norm_act(act, 0, NC - PL0)
            act.wait_ge(fold_ready, 2)
            for k in range(2):
                nc.scalar.copy(M3[:, k * PR:(k + 1) * PR, :],
                               bank[2 + k][:, :].rearrange("p (g c) -> p g c", g=PR)).then_inc(m3_copied, 1)
            act.wait_ge(fold_ready, 4)
            for k in range(2):
                nc.scalar.mul(M1[:, k * PR:(k + 1) * PR, :],
                              bank[4 + k][:, :].rearrange("p (g c) -> p g c", g=PR), 0.125).then_inc(m1_copied, 1)
            act.wait_ge(t2_ready, 1)
            nc.scalar.activation(T2, T2, ACT.Exp).then_inc(e2_ready, 1)
            act.wait_ge(at_ready, 2)
            for k in range(2):
                nc.scalar.copy(AT[:, k * PR:(k + 1) * PR, :],
                               bank[k][:, :].rearrange("p (g c) -> p g c", g=PR)).then_inc(at_copied, 1)
            for it in range(ITERS):
                for k in range(2):
                    g = slice(k * PR, (k + 1) * PR)
                    act.wait_ge(pinv_mm, 12 * it + 2 + k + 1)
                    nc.scalar.copy(XZT[:, g, :], bank[2 + k][:, :].rearrange("p (g c) -> p g c", g=PR)).then_inc(xzt_ready, 1)
                for k in range(2):
                    g = slice(k * PR, (k + 1) * PR)
                    act.wait_ge(pinv_mm, 12 * it + 10 + k + 1)
                    nc.scalar.mul(ZT[(it + 1) % 2][:, g, :], bank[2 + k][:, :].rearrange("p (g c) -> p g c", g=PR),
                                  0.25).then_inc(zt_ready, 1)
            for t in range(NT):
                act.wait_ge(v_ready, t + 1)
                nc.scalar.copy(V[:, t, :], bank[6 + t % 2][:, :]).then_inc(v_copied, 1)
            for i in range(BP + 1):
                if i < BP:
                    act.wait_ge(max3_ready, i + 1)
                    if i >= 2:
                        act.wait_ge(p3t_ready, 4 * (i - 1))
                    for c in range(CB):
                        nc.scalar.activation(P3[:, i % 2, c * CH:(c + 1) * CH], bank[c][:, :], ACT.Exp, bias=m3[:, i:i + 1],
                                             accum_out=s3p[:, i * CB + c:i * CB + c + 1]).then_inc(exp3_ready, 1)
                if i > 0:
                    k = i - 1
                    if k >= 2:
                        act.wait_ge(w3_ready, k - 1)
                    for q in (0, 2):
                        act.wait_ge(p3t_ready, 4 * k + q + 1)
                        nc.scalar.copy(P3T[:, k % 2, 4 * q:4 * q + 4, :],
                                       bank[4 + q % 2][:, :].rearrange("p (t c) -> p t c", t=4)).then_inc(p3t_copied_a, 1)

            def exp1(t):
                act.wait_ge(sub1_ready, t + 1)
                nc.scalar.activation(P1[:, t % 2], P1[:, t % 2], ACT.Exp).then_inc(exp1_ready, 1)

            def turn1(t):
                act.wait_ge(p1t_ready, t + 1)
                c, q = t // TC, t % TC
                nc.scalar.copy(P1T[:, c % 2, :, q * P:(q + 1) * P],
                               bank[2 + t % 2][:, :].rearrange("p (g c) -> p g c", g=PR)).then_inc(p1t_copied, 1)

            def out1(c, g):
                act.wait_ge(o_ready, c * PR + g + 1)
                if c >= 1 and g == 0:
                    act.wait_ge(y_ready, c)
                nc.scalar.copy(OT[:, g, :], bank[4 + g % 2][:, :]).then_inc(o_copied, 1)
            for t in range(STEPS1):
                if t < NT:
                    exp1(t)
                if 2 <= t < NT + 2:
                    turn1(t - 2)
                c, g = divmod(t - OUT_LAG, PR)
                if 0 <= c < NC:
                    out1(c, g)
            norm_act(act, 1)
            act.wait_ge(lg_ready, 1)
            nc.scalar.activation(ex, lg, ACT.Exp).then_inc(exg_ready, 1)
            for c in range(NC):
                for k in range(KF):
                    n = c * KF + k
                    act.wait_ge(sh_mm, n + 1)
                    if c >= 2 and k == 0:
                        act.wait_ge(shy_ready, c - 1)
                    nc.scalar.activation(hs[:, c % 2, k, :], bank[3 + n % 2][:, :], ACT.Gelu, bias=bs1[:, k:k + 1]).then_inc(sh_gelu, 1)
                    if c < NC // 2 and k % 2 == 1:
                        q = 2 * c + k // 2
                        act.wait_ge(xtm_mm, q + 1)
                        nc.scalar.copy(xtm[:, 4 * q:4 * q + 4, :], bank[1 + q % 2][:, :].rearrange("p (t d) -> p t d", t=4)).then_inc(xtm_copied, 1)
            def step_act(n, s):
                act.wait_ge(hb_mm, n + 1)
                act.wait_ge(yb_mm, n + 1)
                for q in range(KF):
                    nc.scalar.activation(hb[:, s % 2, q, :], bank[2 + s % 2][:, q * P:(q + 1) * P], ACT.Gelu,
                                         bias=b1s[:, s, q:q + 1]).then_inc(hb_ready, 1)
            with act.Fori(0, ALLB // XS) as i:
                for s in range(XS):
                    step_act(i * XS + s, s)
            norm_act(act, 2)
            act.wait_ge(loaded3, 16 * 4)
            act.wait_ge(qk_scaled, 1)

            def part1(c, k):
                act.wait_ge(qk_mm, 2 * c + k + 1)
                if c >= CB:
                    act.wait_ge(parts_stored, 32 * CB)
                nc.scalar.activation(parts_of(k, c)[:, 0, :], bank[2 * k + c % 2], ACT.Identity,
                                     bias=bqk[:, k:k + 1]).then_inc(p1_done, 1)

            def part2(c, k):
                act.wait_ge(r1_done, 2 * c + k + 1)
                nc.scalar.copy(parts_of(k, c)[:, 1, :], ln_sq[:, k, :]).then_inc(p2_done, 1)
            for first in (0, CB):
                for n in range(2 * first, 2 * (first + CB)):
                    part1(n // 2, n % 2)
                    if n > 2 * first:
                        part2((n - 1) // 2, (n - 1) % 2)
                part2(first + CB - 1, 1)
            before = None
            for u, i in STEPS:
                seen = 0
                for kind, x in step_items(u, i):
                    if kind == "exp":
                        j, q0 = x
                        n = tiles_before(u, i) + seen
                        act.wait_ge(st_ready, n + 1)
                        if n >= WR:
                            act.wait_ge(pv_done, n - WR + 1)
                        nc.scalar.activation(PT[:, n % WR, q0:CH], bank[SB + n % SB][:, q0:CH], ACT.Exp).then_inc(exp_done, 1)
                        seen += 1
                        if seen == 3 and before:
                            ot_copy(act, *before)
                if u >= 0:
                    before = (u, i)
            ot_copy(act, *before)
            norm_act(act, 3)
            act.wait_ge(node_ready, 1)
            nc.scalar.activation(node, node, ACT.Sigmoid).then_inc(node_sig, 1)
            act.wait_ge(loaded3, 16 * (4 + 4))
            act.sem_inc(gelu_done, 4)
            act.sem_inc(yout_ready, 1)
            for s in range(2):
                act.sem_inc(yout_stored[s], 16)
            with act.Fori(0, NC // 2) as i:
                for s in range(2):
                    for k in range(HK):
                        m = s * HK + k
                        n = i * (2 * HK) + m
                        act.wait_ge(hid_mm, n + 1)
                        act.wait_ge(used, n + 1)
                        nc.scalar.activation(hid[:, m % HB, :], hidden_bank(m), ACT.Gelu,
                                             bias=fb1[:, k // KF, k % KF:k % KF + 1]).then_inc(gelu_done, 1)
                    act.wait_ge(yT_mm, i * 2 + (s + 2))
                    act.wait_ge(yout_stored[s], (i + 1) * 16)
                    nc.scalar.copy(yout[:, s], bank[5].rearrange("p (t d) -> p t d", t=TC)).then_inc(yout_ready, 1)

        @blk.gpsimd
        def _(pool):
            pool.wait_ge(col_max, 1)
            nc.gpsimd.partition_all_reduce(qcol[:, 2:4], qcol[:, 0:2], P, RMAX).then_inc(all_max, 1)
            pool.wait_ge(nmax_ready, 1)
            nc.gpsimd.partition_all_reduce(nall[:, :], nmax[:, :], P, RMAX).then_inc(nall_ready, 1)
            pool.wait_ge(cleared, 16 * BK)
            pool.wait_ge(routed, 1)
            pool.wait_ge(xtm_copied, NC)
            for k in range(BK):
                for t in range(NT):
                    pool.indirect_dma_start(out=xbuf[k].ap(), out_offset=bass.IndirectOffsetOnAxis(ap=put_at[:, k, t:t + 1], axis=0),
                                            in_=xtm[:, t, :], in_offset=None).then_inc(put[k], 16)
            for k in range(BK):
                for s in range(XS):
                    pool.wait_ge(yb_stored[s], 16 * ((k + 1) * NBLK // XS + 1))
                for t in range(NT):
                    pool.indirect_dma_start(out=ygt[:, t, k, :], out_offset=None, in_=ybuf[k].ap(),
                                            in_offset=bass.IndirectOffsetOnAxis(ap=get_at[:, k, t:t + 1], axis=0)).then_inc(got0 if k == 0 else got1[t // (NT // GG)], 16)
            pool.wait_ge(combT_ready, NC)
            nc.gpsimd.memset(V1[:, :, :, D1 + 1:], 0.0).then_inc(v1_cleared, 1)
            pool.wait_ge(v1_cleared, 1)
            nc.gpsimd.memset(V1[:, :, :, D1:D1 + 1], 1.0).then_inc(v1_cleared, 1)
            pool.wait_ge(v1_cleared, 2)
            for n in range(2 * NC):
                c, k = n // 2, n % 2
                pool.wait_ge(p2_done, n + 1)
                if n > 0:
                    pool.wait_ge(p3_done, n)
                nc.gpsimd.tensor_tensor(parts_of(k, c)[:, 2, :], ln_sq[:, k, :], parts_of(k, c)[:, 1, :], ALU.subtract).then_inc(p3_done, 1)
            pool.wait_ge(p3_done, 2 * NC)
            nc.gpsimd.memset(KS[KS_ROWS:KROWS, :, :], 1.0).then_inc(ones_set, 1)

        @blk.tensor
        def _(pe):
            for c in range(NC):
                pe.wait_ge(onehot_ready, c + 1)
                if c >= 2:
                    pe.wait_ge(e_copied, c - 1)
                nc.tensor.matmul(bank[c % 2][:, :], emb_e, onehot[:, c % 2, :],
                                 start=True, stop=True).then_inc(e_ready, 1)
                if c >= PL0:
                    norm_pe(pe, 0, c - PL0, c - PL0 + 1)
            norm_pe(pe, 0, NC - PL0)
            pe.wait_ge(xl_ready, NC)
            pe.wait_ge(loaded0, 16 * 5)
            for k in range(2):
                for g in range(PR):
                    last = nc.tensor.matmul(bank[k][:, g * P:(g + 1) * P], wqkv[:, k * 512 + g * P:k * 512 + (g + 1) * P], xl,
                                            start=True, stop=True)
            last.then_inc(lm_ready, 1)
            pe.wait_ge(lm_copied, 8)
            for w, t, o in ((wkT, QL, 2), (wqT, KL, 4)):
                for b in range(B):
                    for g in range(PR):
                        last = nc.tensor.matmul(bank[o + b][:, g * P:(g + 1) * P], w[:, g, :], t[:, b * PR + g, :],
                                                start=True, stop=True)
                    last.then_inc(fold_ready, 1)
            for b in range(B):
                for g in range(PR):
                    last = nc.tensor.matmul(bank[6 + b][:, g * P:(g + 1) * P], QL[:, b * PR + g, :], KL[:, b * PR + g, :],
                                            start=True, stop=True)
            last.then_inc(sim2_ready, 1)
            pe.wait_ge(a_ready, 1)
            for b in range(B):
                for g in range(PR):
                    last = nc.tensor.transpose(bank[b][:, g * P:(g + 1) * P], A[:, b * PR + g, :], ident[:, :])
                last.then_inc(at_ready, 1)

            def products(o, lhsT, rhs, waits):
                for k in range(2):
                    for s, v in waits:
                        pe.wait_ge(s, v + k)
                    for g in range(k * PR, (k + 1) * PR):
                        last = nc.tensor.matmul(bank[o + k][:, (g % PR) * P:(g % PR + 1) * P], lhsT[:, g, :], rhs[:, g, :],
                                                start=True, stop=True)
                    last.then_inc(pinv_mm, 1)
            pe.wait_ge(at_copied, 2)
            pe.wait_ge(m3_copied, 2)
            pe.wait_ge(m1_copied, 2)
            for it in range(ITERS):
                z, zt = Z[it % 2], ZT[it % 2]
                u = 6 * it
                products(0, AT, z, [(z_ready, 2 * it + 1)] + ([(u_ready, u - 1)] if it else []))
                products(2, z, AT, [(z_ready, 2 * it + 1)] + ([(zt_ready, 2 * it + 1)] if it else []))
                products(4, XZT, U, [(xzt_ready, 2 * it + 1), (u_ready, u + 1)])
                products(0, XZT, U, [(u_ready, u + 3)])
                products(4, zt, U, [(u_ready, u + 5), (zt_ready, 2 * it + 1)])
                products(2, U, zt, [(u_ready, u + 5)])
            for t in range(NT):
                if t >= 2:
                    pe.wait_ge(v_copied, t - 1)
                nc.tensor.matmul(bank[6 + t % 2][:, :], xnT[:, t * P:(t + 1) * P], wqkv[:, 1024:1536],
                                 start=True, stop=True).then_inc(v_ready, 1)
            pe.wait_ge(v_copied, NT)
            pe.wait_ge(z_ready, 2 * ITERS + 2)
            for i in range(BP + 2):
                if i < BP:
                    b = i // PR
                    for c in range(CB):
                        if i >= 1:
                            pe.wait_ge(exp3_ready, (i - 1) * CB + c + 1)
                        nc.tensor.matmul(bank[c][:, :], M3[:, i, :], xnT[:, b * T + c * CH:b * T + (c + 1) * CH],
                                         start=True, stop=True).then_inc(sim3_ready, 1)
                for q in range(4):
                    if 1 <= i <= BP:
                        m = 4 * (i - 1) + q
                        pe.wait_ge(exp3_ready, CB * (i - 1) + q + 1)
                        if m >= 2:
                            pe.wait_ge(p3t_copied_a if q % 2 == 0 else p3t_copied, m // 2)
                        for t in range(4 * q, 4 * q + 4):
                            last = nc.tensor.transpose(bank[4 + q % 2][:, (t % 4) * P:(t % 4 + 1) * P],
                                                       P3[:, (i - 1) % 2, t * P:(t + 1) * P], ident[:, :])
                        last.then_inc(p3t_ready, 1)
                    if i >= 2:
                        k = i - 2
                        b, g = k // PR, k % PR
                        if k >= 2 and q == 0:
                            pe.wait_ge(w_ready, k - 1)
                        pe.wait_ge(p3t_copied_a if q % 2 == 0 else p3t_copied, 2 * k + q // 2 + 1)
                        for t in range(4 * q, 4 * q + 4):
                            last = nc.tensor.matmul(bank[6 + k % 2][:, 0:P], P3T[:, k % 2, t, :], V[:, b * TB + t, g * P:(g + 1) * P],
                                                    start=(t == 0), stop=(t == TB - 1))
                        if q == 3:
                            last.then_inc(w3_ready, 1)
            pe.wait_ge(w_ready, BP)
            pe.wait_ge(zt_ready, 2 * ITERS + 2)
            for k in range(2):
                for g in range(PR):
                    last = nc.tensor.matmul(bank[6 + k][:, g * P:(g + 1) * P], ZT[ITERS % 2][:, k * PR + g, :], W[:, k * PR + g, :],
                                            start=True, stop=True)
                last.then_inc(g_mm, 1)

            def sim1(t):
                b = t // TB
                if t >= 2:
                    pe.wait_ge(sub1_ready, t - 1)
                nc.tensor.matmul(bank[t % 2][:, :], xnT[:, t * P:(t + 1) * P],
                                 M1[:, b * PR:(b + 1) * PR, :].rearrange("p g c -> p (g c)"),
                                 start=True, stop=True).then_inc(sim1_ready, 1)

            def turn1(t):
                pe.wait_ge(p1_ready, t + 1)
                if t >= 2:
                    pe.wait_ge(p1t_copied, t - 1)
                for g in range(PR):
                    last = nc.tensor.transpose(bank[2 + t % 2][:, g * P:(g + 1) * P],
                                               P1[:, t % 2, 2 * g:2 * g + 2, :].rearrange("p h m -> p (h m)"), ident[:, :])
                last.then_inc(p1t_ready, 1)

            def out1(c, g):
                pe.wait_ge(p1t_copied, TC * (c + 1))
                b, n = c // CB, c * PR + g
                if n >= 2:
                    pe.wait_ge(o_copied, n - 1)
                o = bank[4 + g % 2]
                nc.tensor.matmul(o[:, :], G[:, b * PR + g, :], P1T[:, c % 2, g, :], start=True, stop=False,
                                 skip_group_check=True)
                pieces = conv_pieces(c)
                for n, (t, c0, w, k0) in enumerate(pieces):
                    for j in range(2):
                        last = nc.tensor.matmul(o[64 * j:64 * j + 64, c0:c0 + w],
                                                V[:, b * TB + t, g * P + 64 * j:g * P + 64 * j + 64],
                                                band[:, 2 * g + j, k0:k0 + w], start=False,
                                                stop=(n == len(pieces) - 1), skip_group_check=True)
                last.then_inc(o_ready, 1)

            def project1(c):
                pe.wait_ge(o_copied, PR * (c + 1))
                if c >= 1:
                    pe.wait_ge(h_ready, NC + c)
                for g in range(PR):
                    last = nc.tensor.matmul(bank[7][:, :], wout[:, g, :], OT[:, g, :], start=(g == 0), stop=(g == PR - 1))
                last.then_inc(y_ready, 1)
            pe.wait_ge(g_copied, 2)
            pe.wait_ge(exp3_ready, BP * CB)
            for t in range(STEPS1):
                if t < NT:
                    sim1(t)
                if 2 <= t < NT + 2:
                    turn1(t - 2)
                c, g = divmod(t - OUT_LAG, PR)
                if c >= 1 and g == 0:
                    project1(c - 1)
                if 0 <= c < NC:
                    out1(c, g)
            for c in range(NC + 3):
                if c < NC + 2:
                    norm_pe(pe, 1, c, c + 1)
                if c == 3:
                    pe.wait_ge(loaded1, 16 * 8)
                    pe.wait_ge(h_ready, 2 * NC)
                if c >= 3:
                    pe.wait_ge(xn_ready, NC + c - 2)
                    for t in range(TC * (c - 3), TC * (c - 2)):
                        last = nc.tensor.matmul(bank[7][:, t * BK * E:(t + 1) * BK * E], xnT[:, t * P:(t + 1) * P], wr,
                                                start=True, stop=True)
            last.then_inc(logits_ready, 1)
            pe.wait_ge(loaded0, 16 * (5 + 2))

            def turn_tokens(q):
                if q >= 2:
                    pe.wait_ge(xtm_copied, q - 1)
                for t in range(4 * q, 4 * q + 4):
                    last = nc.tensor.transpose(bank[1 + q % 2][:, (t % 4) * P:(t % 4 + 1) * P], xnT[:, t * P:(t + 1) * P], ident[:, :])
                last.then_inc(xtm_mm, 1)
            for c in range(NC + 1):
                if c < NC:
                    for k in range(KF):
                        n = c * KF + k
                        if n >= 2:
                            pe.wait_ge(sh_gelu, n - 1)
                        nc.tensor.matmul(bank[3 + n % 2][:, :], ws1[:, k * P:(k + 1) * P], xnT[:, c * CH:(c + 1) * CH],
                                         start=True, stop=True).then_inc(sh_mm, 1)
                        if c < NC // 2 and k % 2 == 1:
                            turn_tokens(2 * c + k // 2)
                if c == 1:
                    pe.wait_ge(oneh_ready, 1)
                    nc.tensor.matmul(bank[6][:, :], tri, oneh, start=True, stop=True).then_inc(prefix_ready, 1)
                    nc.tensor.matmul(bank[7][:, :], ones, oneh, start=True, stop=True).then_inc(prefix_ready, 1)
                if c > 0:
                    pe.wait_ge(sh_gelu, c * KF)
                    if c >= 2:
                        pe.wait_ge(shy_added, c - 1)
                    for k in range(KF):
                        last = nc.tensor.matmul(bank[5][:, :], ws2[:, k, :], hs[:, (c - 1) % 2, k, :], start=(k == 0), stop=(k == KF - 1))
                    last.then_inc(shy_ready, 1)
            pe.wait_ge(shy_added, NC)
            pe.sem_inc(yb_mm, 2)
            pe.sem_inc(yb_ready, 2)
            for s in range(XS):
                pe.sem_inc(yb_stored[s], 16)
            pe.sem_inc(blocks_clear, 1)
            pe.wait_ge(loaded2, 16 * 5)

            def turn(n, s):
                pe.wait_ge(xb_loaded[s], whole(n, s) * 16)
                nc.tensor.transpose(bank[s % 2][:, 0:P], xb[:, s, :], ident[:, :]).then_inc(xbT_mm, 1)

            def hidden(n, s):
                pe.wait_ge(w1s_ready, n + 1)
                pe.wait_ge(xbT_copied, n + 1)
                for q in range(KF):
                    last = nc.tensor.matmul(bank[2 + s % 2][:, q * P:(q + 1) * P], w1s[:, s % 2, q * P:(q + 1) * P], xbT[:, s % 2, :],
                                            start=True, stop=True)
                last.then_inc(hb_mm, 1)

            def result(n, s):
                e = pe.value_load(experts[0:1, bass.ds(n, 1)], min_val=0, max_val=BK * E - 1)
                pe.wait_ge(yb_ready, n + 1)
                for q in range(KF):
                    pe.wait_ge(hb_ready, n * KF + (q + 1))
                    last = nc.tensor.matmul(bank[4 + s % 2][:, 0:P], hb[:, s % 2, q, :],
                                            w2[:, bass.ds(e, 1), q, :].rearrange("p e d -> p (e d)"),
                                            start=(q == 0), stop=(q == KF - 1))
                last.then_inc(yb_mm, 1)
            turn(0, 0)
            turn(1, 1)
            hidden(0, 0)

            def step_pe(n, s, left=2):
                if left >= 2:
                    pe.wait_ge(xbT_copied, n + 1)
                    turn(n + 2, (s + 2) % XS)
                if left >= 1:
                    hidden(n + 1, (s + 1) % XS)
                result(n, s)
            with pe.Fori(0, ALLB // XS - 1) as i:
                for s in range(XS):
                    step_pe(i * XS + s, s)
            for n in range(ALLB - XS, ALLB):
                step_pe(n, n % XS, ALLB - 1 - n)
            for c in range(NC):
                pe.wait_ge(comb_ready, TC * (c + 1))
                if c >= 2:
                    pe.wait_ge(h_ready, 2 * NC + c - 1)
                for t in range(TC):
                    last = nc.tensor.transpose(bank[6 + c % 2][:, t * P:(t + 1) * P], comb[:, TC * c + t, :], ident[:, :])
                last.then_inc(combT_ready, 1)
                if c >= PL:
                    norm_pe(pe, 2, c - PL, c - PL + 1)
            norm_pe(pe, 2, NC - PL)
            pe.wait_ge(qk_scaled, 1)
            pe.wait_ge(xn_ready, 3 * NC)
            for c in range(NC):
                for k in range(2):
                    if c >= 2:
                        pe.wait_ge(r1_done, 2 * (c - 2) + k + 1)
                    nc.tensor.matmul(bank[2 * k + c % 2], wqkvT[:, k, :], xnT[:, c * CH:(c + 1) * CH],
                                     start=True, stop=True).then_inc(qk_mm, 1)
                if c >= 2:
                    pe.wait_ge(v1_copied, c - 1)
                for t in range(TC):
                    last = nc.tensor.matmul(bank[4 + c % 2][:, t * P:(t + 1) * P], xnT[:, (TC * c + t) * P:(TC * c + t + 1) * P],
                                            wqkvT[:, 2, :], start=True, stop=True)
                last.then_inc(v1_mm, 1)
            pe.wait_ge(v1_cleared, 2)
            pe.wait_ge(v1_copied, NC)

            def maxima(u, i, k, x):
                qt, s, w = x
                n = pieces_before(u, i) + k
                if k == 0 and i == 0:
                    pe.wait_ge(stack_loaded[u % RING], 96 * (u // RING + 1))
                if n >= SB:
                    pe.wait_ge(s1_read, n - SB + 1)
                else:
                    pe.wait_ge(r1_done, 2 * NC)
                out = bank[n % SB]
                last = nc.tensor.matmul(out[:, 0:w], QS[0:KS_ROWS, u % RING, qt * P:(qt + 1) * P],
                                        KS[0:KS_ROWS, u % RING, CH * s:CH * s + w], start=True, stop=True)
                if CH * s + w == (qt + 1) * P:
                    last = nc.tensor.matmul(out[:, w - P:w], identb, mask_qk, start=False, stop=True, skip_group_check=True)
                last.then_inc(s1_ready, 1)

            def scores(u, i, k, x):
                j, q0 = x
                n = tiles_before(u, i) + k
                if k == 0 and i == 0:
                    pe.wait_ge(mrows[u % 2], 48 * (u // 2 + 1))
                    pe.wait_ge(ones_set, 1)
                if n >= SB:
                    pe.wait_ge(exp_done, n - SB + 1)
                out = bank[SB + n % SB]
                diag = j >= TC * i
                last = nc.tensor.matmul(out[:, q0:CH], KS[0:KROWS, u % RING, j * P:(j + 1) * P],
                                        QS[0:KROWS, u % RING, i * CH + q0:(i + 1) * CH], start=True, stop=True)
                if diag:
                    last = nc.tensor.matmul(out[:, q0:q0 + P], identb, mask_kq, start=False, stop=True, skip_group_check=True)
                last.then_inc(st_ready, 1)

            def weigh(n):
                u, i, k = where(n)
                j, q0 = exp_tiles(i)[k]
                pe.wait_ge(exp_done, n + 1)
                m = u * CB + i
                if k == 0 and m >= 2:
                    pe.wait_ge(otT_read, m - 1)
                if k == 0 and i == 1:
                    pe.wait_ge(mparts_ready, min(u + LEAD, UN))
                g = j % 4 if i else 0
                nc.tensor.matmul(bank[6 + m % 2][32 * g:32 * g + 32, q0:CH], V1[:, (u // H1) * TB + j, u % H1, :], PT[:, n % WR, q0:CH],
                                 start=(j < 4 if i else j == 0), stop=True, skip_group_check=True).then_inc(pv_done, 1)

            def left_over(u, i):
                if u >= 0:
                    m = u * CB + i
                    pe.wait_ge(ot_copied, m + 1)
                    rows = 32 if i == 0 else P
                    for t in range(TC):
                        last = nc.tensor.transpose(bank[6 + m % 2][:, t * P:t * P + rows], OTp[0:rows, m % 2, t * P:(t + 1) * P],
                                                   ident[0:rows, 0:rows])
                    last.then_inc(otT_ready, 1)
                if i == CB - 1 and u + LEAD < UN:
                    v = u + LEAD
                    pe.wait_ge(negm_ready, v + 1)
                    if u >= 0:
                        pe.wait_ge(otT_read, u * CB + i + 1)
                    if v >= 1:
                        pe.wait_ge(mparts_ready, v)
                    nc.tensor.transpose(bank[7][0:TB, 0:P], negm[:, v % 2, :], ident[:, :]).then_inc(mT_ready, 1)

            before = None
            for u, i in STEPS:
                items = step_items(u, i)
                seen = {"max": 0, "exp": 0}
                for n, (kind, x) in enumerate(items):
                    if kind == "max":
                        maxima(u + LEAD, i, seen[kind], x)
                    else:
                        scores(u, i, seen[kind], x)
                        m = tiles_before(u, i) + seen[kind]
                        if m >= SB:
                            weigh(m - SB)
                    seen[kind] += 1
                    if before and n + 1 == pause(items):
                        left_over(*before)
                before = (u, i)
            for n in range(tiles_before(UN, 0) - SB, tiles_before(UN, 0)):
                weigh(n)
            left_over(*before)
            pe.wait_ge(o_done, UN)
            for c in range(NC):
                if c >= 2:
                    pe.wait_ge(h_ready, 3 * NC + c - 1)
                for t in range(TC):
                    last = nc.tensor.transpose(bank[c % 2][:, t * P:(t + 1) * P],
                                               O[:, TC * c + t].rearrange("p h c -> p (h c)"), ident[:, :])
                last.then_inc(oT_ready, 1)
                if c >= PL:
                    norm_pe(pe, 3, c - PL, c - PL + 1)
            nodes = 0
            for c in range(NC - PL, NC + 3):
                if c < NC + 2:
                    norm_pe(pe, 3, c, c + 1)
                if c == NC - 1:
                    pe.wait_ge(loaded3, 16 * (4 + 4))
                if c >= NC - 1:
                    for t in range(nodes, TC * (c - 2)):
                        pe.wait_ge(xn_ready, 3 * NC + t // TC + 1)
                        last = nc.tensor.matmul(bank[0][:, t * 8:t * 8 + 7], xnT[:, t * P:(t + 1) * P], rwT, start=True, stop=True)
                    nodes = TC * (c - 2)
            last.then_inc(node_mm, 1)
            pe.wait_ge(leaf_ready, 1)
            for c in range(NC):
                if c >= 2:
                    pe.wait_ge(leafT_copied, c - 1)
                for t in range(TC):
                    last = nc.tensor.transpose(bank[1 + c % 2][0:E, t * P:(t + 1) * P], leaf3[:, TC * c + t, :], ident[:, :])
                last.then_inc(leafT_mm, 1)
            pe.wait_ge(leafT_copied, NC)
            pe.wait_ge(loaded5, 16 * 2)
            pe.sem_inc(used, HB)
            pe.sem_inc(yT_mm, 1)
            with pe.Fori(0, NC // 2) as i:
                for s in range(2):
                    xc = xnT[:, bass.ds((i * 2 + s) * CH, CH)]
                    for k in range(HK + LAG1):
                        m = s * HK + k
                        n = i * (2 * HK) + m
                        if k < HK:
                            pe.wait_ge(gelu_done, n + 1)
                            nc.tensor.matmul(hidden_bank(m), f1[:, k // KF, (k % KF) * P:(k % KF + 1) * P], xc,
                                             start=True, stop=True).then_inc(hid_mm, 1)
                        if k == 0:
                            nc.tensor.matmul(bank[3 + s], fb2, leafT[:, bass.ds((i * 2 + s) * CH, CH)], start=True, stop=False)
                        if k >= LAG1:
                            q = k - LAG1
                            pe.wait_ge(weighed, n + (1 - LAG1))
                            last = nc.tensor.matmul(bank[3 + s], f2[:, q // KF, q % KF, :], hid[:, (m - LAG1) % HB, :],
                                                    start=False, stop=(q == HK - 1))
                            last.then_inc(used, 1)
                    pe.wait_ge(yT_ready, i * 2 + s + 1)
                    pe.wait_ge(yout_ready, i * 2 + (s + 1))
                    for t in range(TC):
                        last = nc.tensor.transpose(bank[5][:, t * P:(t + 1) * P], yT[:, t * P:(t + 1) * P], ident[:, :])
                    last.then_inc(yT_mm, 1)


def host(ins):
    import numpy as np
    f = {}
    f["x"] = np.ascontiguousarray(ins["x"])
    f["emb"] = np.ascontiguousarray(ins["L0_tok_emb_weight"])
    f["conv2"] = np.ascontiguousarray(np.asarray(ins["L0_tok_conv_weight"])[:, 0, :])
    eye = np.eye(P, dtype=np.float32)
    f["c_ident"] = eye
    f["c_idk"] = np.ascontiguousarray(np.stack([7 * eye, 15 * eye, 13 * eye], axis=1))
    f["c_centre"] = eye - np.float32(1 / P)
    f["c_iota"] = np.arange(P, dtype=np.float32)[:, None].copy()
    f["b_out"] = np.asarray(ins["L0_attn_b_out"])[:, None].copy()
    w = np.asarray(ins["L0_attn_W_qkv"])
    f["wqkv"] = w
    f["wqT"] = np.ascontiguousarray(w[:, 0:512].T.reshape(PR, P, P).transpose(1, 0, 2))
    f["wkT"] = np.ascontiguousarray(w[:, 512:1024].T.reshape(PR, P, P).transpose(1, 0, 2))
    f["wout"] = np.ascontiguousarray(np.asarray(ins["L0_attn_W_out"]).reshape(PR, P, P).transpose(1, 0, 2))
    cw = np.asarray(ins["L0_attn_conv_w"])[:, 0, :, 0]
    band = np.zeros((P, H0, CW), np.float32)
    for p in range(P):
        band[p, :, p:p + K] = cw[:, ::-1]
    f["band"] = band

    def g(n):
        return np.asarray(ins[n])
    f["ws1"] = g("L0_ffn_Ws1")
    f["ws2"] = np.ascontiguousarray(g("L0_ffn_Ws2").reshape(KF, P, P).transpose(1, 0, 2))
    f["bs1"] = np.ascontiguousarray(g("L0_ffn_bs1").reshape(KF, P).T)
    f["bs2"] = g("L0_ffn_bs2")[:, None].copy()
    f["wr"] = np.concatenate([g("L0_ffn_Wr_sp"), g("L0_ffn_Wr_fq")], axis=1)
    f["brt"] = np.concatenate([g("L0_ffn_br_sp"), g("L0_ffn_br_fq")])
    f["w1"] = np.ascontiguousarray(np.concatenate([g("L0_ffn_W1_sp"), g("L0_ffn_W1_fq")]).transpose(1, 0, 2))
    w2 = np.concatenate([g("L0_ffn_W2_sp"), g("L0_ffn_W2_fq")])
    f["w2"] = np.ascontiguousarray(w2.reshape(BK * E, KF, P, P).transpose(2, 0, 1, 3))
    bb = np.concatenate([g("L0_ffn_b1_sp"), g("L0_ffn_b1_fq")])
    f["b1"] = np.ascontiguousarray(bb.reshape(BK * E, KF, P).transpose(2, 0, 1))
    f["b2"] = np.concatenate([g("L0_ffn_b2_sp"), g("L0_ffn_b2_fq")])
    f["f1"] = np.ascontiguousarray(g("L1_ffn_w1").transpose(1, 0, 2))
    f["f2"] = np.ascontiguousarray(g("L1_ffn_w2").reshape(E, KF, P, P).transpose(2, 0, 1, 3))
    f["fb1"] = np.ascontiguousarray(g("L1_ffn_b1").reshape(E, KF, P).transpose(2, 0, 1))
    f["fb2"] = g("L1_ffn_b2")
    f["rwT"] = np.ascontiguousarray(g("L1_ffn_rw").T)
    f["rb"] = g("L1_ffn_rb")
    wt = np.stack([g("L1_attn_W" + x).T for x in "qkv"], axis=1)
    f["wqkvT"] = np.ascontiguousarray(wt)
    f["bv"] = g("L1_attn_bv")
    f["bqk"] = np.stack([g("L1_attn_bq"), g("L1_attn_bk")], axis=1)
    f["c_masks"] = np.ascontiguousarray(np.stack([np.triu(np.full((P, P), NEG, np.float32), 1),
                                                  np.tril(np.full((P, P), NEG, np.float32), -1)], axis=1))
    f["c_ones"] = np.ones((P, P), np.float32)
    f["c_tri"] = np.triu(np.ones((P, P), np.float32), 1)
    cr = np.zeros((P, C_ROUTE), np.float32)
    cr[:, C_IOTA8:C_IOTA8 + E] = np.arange(E)
    cr[:, C_J128:C_J128 + CAP // P] = P * np.arange(CAP // P)
    cr[:, C_LT:C_LT + E * E] = np.tril(np.ones((E, E)), -1).ravel()
    cr[:, C_TRASH:C_TRASH + NT] = SLOTS + np.arange(P)[:, None] + P * np.arange(NT)[None]
    cr[:, C_IOTAB:C_IOTAB + NBLK] = np.arange(NBLK)
    f["c_route"] = cr
    return f


def kernel(**inputs):
    import concourse.bacc as bacc
    from concourse.bass_utils import run_bass_kernel_spmd

    nc = bacc.Bacc("TRN2", target_bir_lowering=False, num_devices=1)
    arrays, aps = {}, {}
    for name, value in host(inputs).items():
        arrays["in_" + name] = value
        aps[name] = nc.dram_tensor("in_" + name, value.shape, mybir.dt.from_np(value.dtype), kind="ExternalInput").ap()
    aps["out"] = nc.dram_tensor("out_h", (N, P), F32, kind="ExternalOutput").ap()
    tower(nc, aps)
    result = run_bass_kernel_spmd(nc, [arrays], core_ids=[0])
    return result.results[0]["out_h"].reshape(B, T, P)
```
